# Optimizing a Trainium2 kernel written in Bass

```python
import numpy as np
import jax
import jax.numpy as jnp

def _softmax(x, axis=-1):
    return jax.nn.softmax(x, axis=axis)

def _gelu(x):
    return jax.nn.gelu(x, approximate=True)

def _silu(x):
    return jax.nn.silu(x)

def _sigmoid(x):
    return jax.nn.sigmoid(x)

def _layernorm(x, axis=-1, eps=1e-05):
    m = jnp.mean(x, axis=axis, keepdims=True)
    v = jnp.var(x, axis=axis, keepdims=True)
    return (x - m) / jnp.sqrt(v + eps)

def _scatter_add(tgt, idx, src, axis=0):
    return tgt.at[idx].add(src)

def _segment_sum(src, seg, n):
    return jax.ops.segment_sum(src, seg, n)
kernel_name = 'mk_gnn_resnorm_d4_gnn_r32_e07581'

def setup_inputs(seed: int=0):
    np.random.seed(seed)
    _w = jnp.asarray

    def _rec_inputs():
        import jax
        import jax.numpy as jnp
        _gk = jax.random.key(seed)
        x = -0.0002117 + 1 * jax.random.normal(jax.random.fold_in(_gk, 1), (3125, 256), jnp.float32)
        src = jax.random.randint(jax.random.fold_in(_gk, 2), (50000,), 0, 3125, jnp.int32)
        dst = jnp.minimum((3125 * jax.random.uniform(jax.random.fold_in(_gk, 3), (50000,)) ** 2.0).astype(jnp.int32), 99999)
        _o = jnp.argsort(dst, stable=True)
        src = src[_o]
        dst = dst[_o]
        return (x, src, dst)
    x, src, dst = _rec_inputs()

    def _L0_gnn_setup():
        import jax, jax.numpy as jnp
        import numpy as np
        N_NODES = 3125
        N_EDGES = 50000
        IN_DIM = 256
        HID_DIM = 256
        key = jax.random.key(seed)
        k1, k2, k3, k4 = jax.random.split(key, 4)
        h = jax.random.normal(k1, (N_NODES, IN_DIM), dtype=jnp.float32)
        weight = jax.random.normal(k2, (IN_DIM, HID_DIM), dtype=jnp.float32) * (1.0 / np.sqrt(IN_DIM))
        bias = jnp.zeros((HID_DIM,), dtype=jnp.float32)
        src = jax.random.randint(k3, (N_EDGES,), 0, N_NODES, dtype=jnp.int32)
        dst = jax.random.randint(k4, (N_EDGES,), 0, N_NODES, dtype=jnp.int32)
        return {'h': h, 'weight': weight, 'bias': bias, 'src': src, 'dst': dst}
    _L0_gnn_all = _L0_gnn_setup()
    _L0_gnn_in = {k: v for k, v in _L0_gnn_all.items() if k in ('weight', 'bias')}
    del _L0_gnn_all

    def _L1_gnn_setup():
        import jax, jax.numpy as jnp
        import numpy as np
        N_NODES = 3125
        N_EDGES = 50000
        IN_DIM = 256
        HID0 = 128
        HID1 = 64

        def _glorot(key, shape):
            fan_in, fan_out = (shape[0], shape[1])
            lim = (6.0 / (fan_in + fan_out)) ** 0.5
            return jax.random.uniform(key, shape, jnp.float32, -lim, lim)

        def gcn_conv(x, edge_index, W, b):
            n = x.shape[0]
            loop = jnp.arange(n, dtype=edge_index.dtype)
            row = jnp.concatenate([edge_index[0], loop])
            col = jnp.concatenate([edge_index[1], loop])
            deg = jax.ops.segment_sum(jnp.ones_like(col, jnp.float32), col, num_segments=n)
            dis = jnp.where(deg > 0, jax.lax.rsqrt(jnp.maximum(deg, 1e-12)), 0.0)
            norm = dis[row] * dis[col]
            h = x @ W
            msg = h[row] * norm[:, None]
            out = jax.ops.segment_sum(msg, col, num_segments=n)
            return out + b
        key = jax.random.key(seed)
        ks = jax.random.split(key, 8)
        x = jax.random.normal(ks[0], (N_NODES, IN_DIM), jnp.float32)
        edge_index = jax.random.randint(ks[1], (2, N_EDGES), 0, N_NODES, jnp.int32)
        return {'x': x, 'edge_index': edge_index, 'W_conv': _glorot(ks[2], (IN_DIM, HID0)), 'b_conv': jnp.zeros((HID0,), jnp.float32), 'W_lin': _glorot(ks[3], (HID0, HID1)), 'b_lin': jnp.zeros((HID1,), jnp.float32), 'W_dec1': _glorot(ks[4], (HID1, HID0)), 'b_dec1': jnp.zeros((HID0,), jnp.float32), 'W_dec2': _glorot(ks[5], (HID0, IN_DIM)), 'b_dec2': jnp.zeros((IN_DIM,), jnp.float32)}
    _L1_gnn_all = _L1_gnn_setup()
    _L1_gnn_in = {k: v for k, v in _L1_gnn_all.items() if k in ('W_conv', 'b_conv', 'W_lin', 'b_lin', 'W_dec1', 'b_dec1', 'W_dec2', 'b_dec2')}
    del _L1_gnn_all

    def _L2_gnn_setup():
        import jax, jax.numpy as jnp
        import numpy as np
        N_NODES = 3125
        F_DIM = 256
        NNZ = 50000

        def _prelu(x, a):
            return jnp.where(x >= 0, x, a * x)

        def _hconv(x, W, b, src, dst, n):
            xt = x @ W
            ones = jnp.ones(src.shape, xt.dtype)
            D = jax.ops.segment_sum(ones, src, num_segments=n)
            B = jax.ops.segment_sum(ones, dst, num_segments=n)
            Dinv = jnp.where(D > 0, 1.0 / D, 0.0)
            Binv = jnp.where(B > 0, 1.0 / B, 0.0)
            m = jax.ops.segment_sum(xt[src], dst, num_segments=n) * Binv[:, None]
            out = jax.ops.segment_sum(m[dst], src, num_segments=n) * Dinv[:, None]
            return out + b
        key = jax.random.key(seed)
        k0, k1, k2, k3 = jax.random.split(key, 4)
        x = jax.random.normal(k0, (N_NODES, F_DIM), dtype=jnp.float32)
        edge_index = jax.random.randint(k1, (2, NNZ), 0, N_NODES, dtype=jnp.int32)
        scale = (2.0 / F_DIM) ** 0.5
        W1 = jax.random.normal(k2, (F_DIM, F_DIM), dtype=jnp.float32) * scale
        W2 = jax.random.normal(k3, (F_DIM, F_DIM), dtype=jnp.float32) * scale
        b1 = jnp.zeros((F_DIM,), jnp.float32)
        b2 = jnp.zeros((F_DIM,), jnp.float32)
        a = jnp.full((1,), 0.25, jnp.float32)
        return {'x': x, 'edge_index': edge_index, 'W1': W1, 'b1': b1, 'W2': W2, 'b2': b2, 'a': a}
    _L2_gnn_all = _L2_gnn_setup()
    _L2_gnn_in = {k: v for k, v in _L2_gnn_all.items() if k in ('W1', 'b1', 'W2', 'b2', 'a')}
    del _L2_gnn_all

    def _L3_gnn_setup():
        import jax, jax.numpy as jnp
        import numpy as np
        N_NODES = 512
        N_EDGES = 8192
        D_IN = 256
        D = 256
        H = 512
        E = 64
        TOP_K = 2
        CAP = 1024
        BN_EPS = 1e-05

        def _moe_ff(x, Wg, bg, w1, b1, w2, b2):
            N = x.shape[0]
            logits = x @ Wg + bg
            vals, idx = jax.lax.top_k(logits, TOP_K)
            gates = jax.nn.softmax(vals, axis=-1)
            e_flat = idx.reshape(-1)
            g_flat = gates.reshape(-1)
            tok = jnp.arange(N * TOP_K) // TOP_K
            order = jnp.argsort(e_flat)
            e_s, tok_s, g_s = (e_flat[order], tok[order], g_flat[order])
            counts = jnp.bincount(e_flat, length=E)
            offs = jnp.concatenate([jnp.zeros((1,), counts.dtype), jnp.cumsum(counts)[:-1]])
            rank = jnp.arange(N * TOP_K) - offs[e_s]
            valid = rank < CAP
            slot = jnp.where(valid, e_s * CAP + rank, E * CAP)
            buf = jnp.zeros((E * CAP + 1, D), x.dtype).at[slot].set(x[tok_s])
            h = buf[:E * CAP].reshape(E, CAP, D)
            h1 = jax.nn.gelu(jnp.einsum('ecd,edh->ech', h, w1) + b1[:, None, :], approximate=False)
            h2 = jnp.einsum('ech,ehd->ecd', h1, w2) + b2[:, None, :]
            out_buf = h2.reshape(E * CAP, D)
            y_s = jnp.where(valid[:, None], out_buf[jnp.minimum(slot, E * CAP - 1)], 0.0)
            return jnp.zeros((N, D), x.dtype).at[tok_s].add(g_s[:, None] * y_s)

        def _forward(feats, W_gc, b_gc, W_res, b_res, Wg, bg, w1, b1, w2, b2, gamma, beta, src, dst):
            n = feats.shape[0]
            ones = jnp.ones((src.shape[0],), feats.dtype)
            deg_out = jnp.clip(jax.ops.segment_sum(ones, src, num_segments=n), 1.0)
            deg_in = jnp.clip(jax.ops.segment_sum(ones, dst, num_segments=n), 1.0)
            h = feats * jax.lax.rsqrt(deg_out)[:, None]
            m = jax.ops.segment_sum(h[src], dst, num_segments=n) * jax.lax.rsqrt(deg_in)[:, None]
            gc = m @ W_gc + b_gc
            x = gc + (feats @ W_res + b_res)
            core = _moe_ff(x, Wg, bg, w1, b1, w2, b2)
            y = x + core
            mean = jnp.mean(y, axis=0)
            var = jnp.mean((y - mean) ** 2, axis=0)
            return (y - mean) * jax.lax.rsqrt(var + BN_EPS) * gamma + beta
        key = jax.random.key(seed)
        ks = jax.random.split(key, 16)
        s = lambda d: 1.0 / np.sqrt(d)
        inp = {'feats': jax.random.normal(ks[0], (N_NODES, D_IN), jnp.float32), 'W_gc': jax.random.normal(ks[1], (D_IN, D), jnp.float32) * s(D_IN), 'b_gc': jnp.zeros((D,), jnp.float32), 'W_res': jax.random.normal(ks[2], (D_IN, D), jnp.float32) * s(D_IN), 'b_res': jnp.zeros((D,), jnp.float32), 'Wg': jax.random.normal(ks[3], (D, E), jnp.float32) * s(D), 'bg': jnp.zeros((E,), jnp.float32), 'w1': jax.random.normal(ks[4], (E, D, H), jnp.float32) * s(D), 'b1': jnp.zeros((E, H), jnp.float32), 'w2': jax.random.normal(ks[5], (E, H, D), jnp.float32) * s(H), 'b2': jnp.zeros((E, D), jnp.float32), 'gamma': jnp.ones((D,), jnp.float32), 'beta': jnp.zeros((D,), jnp.float32), 'src': jax.random.randint(ks[6], (N_EDGES,), 0, N_NODES), 'dst': jax.random.randint(ks[7], (N_EDGES,), 0, N_NODES)}
        return inp
    _L3_gnn_all = _L3_gnn_setup()
    _L3_gnn_in = {k: v for k, v in _L3_gnn_all.items() if k in ('W_gc', 'b_gc', 'W_res', 'b_res', 'Wg', 'bg', 'w1', 'b1', 'w2', 'b2', 'gamma', 'beta')}
    del _L3_gnn_all
    return {'x': x, 'src': src, 'dst': dst, 'L0_gnn_weight': _L0_gnn_in['weight'], 'L0_gnn_bias': _L0_gnn_in['bias'], 'L1_gnn_W_conv': _L1_gnn_in['W_conv'], 'L1_gnn_b_conv': _L1_gnn_in['b_conv'], 'L1_gnn_W_lin': _L1_gnn_in['W_lin'], 'L1_gnn_b_lin': _L1_gnn_in['b_lin'], 'L1_gnn_W_dec1': _L1_gnn_in['W_dec1'], 'L1_gnn_b_dec1': _L1_gnn_in['b_dec1'], 'L1_gnn_W_dec2': _L1_gnn_in['W_dec2'], 'L1_gnn_b_dec2': _L1_gnn_in['b_dec2'], 'L2_gnn_W1': _L2_gnn_in['W1'], 'L2_gnn_b1': _L2_gnn_in['b1'], 'L2_gnn_W2': _L2_gnn_in['W2'], 'L2_gnn_b2': _L2_gnn_in['b2'], 'L2_gnn_a': _L2_gnn_in['a'], 'L3_gnn_W_gc': _L3_gnn_in['W_gc'], 'L3_gnn_b_gc': _L3_gnn_in['b_gc'], 'L3_gnn_W_res': _L3_gnn_in['W_res'], 'L3_gnn_b_res': _L3_gnn_in['b_res'], 'L3_gnn_Wg': _L3_gnn_in['Wg'], 'L3_gnn_bg': _L3_gnn_in['bg'], 'L3_gnn_w1': _L3_gnn_in['w1'], 'L3_gnn_b1': _L3_gnn_in['b1'], 'L3_gnn_w2': _L3_gnn_in['w2'], 'L3_gnn_b2': _L3_gnn_in['b2'], 'L3_gnn_gamma': _L3_gnn_in['gamma'], 'L3_gnn_beta': _L3_gnn_in['beta']}

def reference(x, src, dst, L0_gnn_weight, L0_gnn_bias, L1_gnn_W_conv, L1_gnn_b_conv, L1_gnn_W_lin, L1_gnn_b_lin, L1_gnn_W_dec1, L1_gnn_b_dec1, L1_gnn_W_dec2, L1_gnn_b_dec2, L2_gnn_W1, L2_gnn_b1, L2_gnn_W2, L2_gnn_b2, L2_gnn_a, L3_gnn_W_gc, L3_gnn_b_gc, L3_gnn_W_res, L3_gnn_b_res, L3_gnn_Wg, L3_gnn_bg, L3_gnn_w1, L3_gnn_b1, L3_gnn_w2, L3_gnn_b2, L3_gnn_gamma, L3_gnn_beta):
    import jax
    import jax.numpy as jnp

    def _L0_gnn_ref(h, weight, bias, src, dst):
        import jax, jax.numpy as jnp
        import numpy as np
        N_NODES = 3125
        N_EDGES = 50000
        IN_DIM = 256
        HID_DIM = 256
        n = h.shape[0]
        ones = jnp.ones_like(src, dtype=h.dtype)
        out_deg = jax.ops.segment_sum(ones, src, num_segments=n)
        in_deg = jax.ops.segment_sum(ones, dst, num_segments=n)
        norm_src = jax.lax.rsqrt(jnp.clip(out_deg, 1.0))
        norm_dst = jax.lax.rsqrt(jnp.clip(in_deg, 1.0))
        h_src = h * norm_src[:, None]
        msg = h_src[src]
        agg = jax.ops.segment_sum(msg, dst, num_segments=n)
        agg = agg * norm_dst[:, None]
        out = agg @ weight + bias
        return jax.nn.elu(out)

    def _L1_gnn_ref(x, edge_index, W_conv, b_conv, W_lin, b_lin, W_dec1, b_dec1, W_dec2, b_dec2):
        import jax, jax.numpy as jnp
        import numpy as np
        N_NODES = 3125
        N_EDGES = 50000
        IN_DIM = 256
        HID0 = 128
        HID1 = 64

        def _glorot(key, shape):
            fan_in, fan_out = (shape[0], shape[1])
            lim = (6.0 / (fan_in + fan_out)) ** 0.5
            return jax.random.uniform(key, shape, jnp.float32, -lim, lim)

        def gcn_conv(x, edge_index, W, b):
            n = x.shape[0]
            loop = jnp.arange(n, dtype=edge_index.dtype)
            row = jnp.concatenate([edge_index[0], loop])
            col = jnp.concatenate([edge_index[1], loop])
            deg = jax.ops.segment_sum(jnp.ones_like(col, jnp.float32), col, num_segments=n)
            dis = jnp.where(deg > 0, jax.lax.rsqrt(jnp.maximum(deg, 1e-12)), 0.0)
            norm = dis[row] * dis[col]
            h = x @ W
            msg = h[row] * norm[:, None]
            out = jax.ops.segment_sum(msg, col, num_segments=n)
            return out + b
        h = gcn_conv(x, edge_index, W_conv, b_conv)
        h = jax.nn.relu(h)
        z = h @ W_lin + b_lin
        d = jax.nn.relu(z @ W_dec1 + b_dec1)
        out = d @ W_dec2 + b_dec2
        return out

    def _L2_gnn_ref(x, edge_index, W1, b1, W2, b2, a):
        import jax, jax.numpy as jnp
        import numpy as np
        N_NODES = 3125
        F_DIM = 256
        NNZ = 50000

        def _prelu(x, a):
            return jnp.where(x >= 0, x, a * x)

        def _hconv(x, W, b, src, dst, n):
            xt = x @ W
            ones = jnp.ones(src.shape, xt.dtype)
            D = jax.ops.segment_sum(ones, src, num_segments=n)
            B = jax.ops.segment_sum(ones, dst, num_segments=n)
            Dinv = jnp.where(D > 0, 1.0 / D, 0.0)
            Binv = jnp.where(B > 0, 1.0 / B, 0.0)
            m = jax.ops.segment_sum(xt[src], dst, num_segments=n) * Binv[:, None]
            out = jax.ops.segment_sum(m[dst], src, num_segments=n) * Dinv[:, None]
            return out + b
        src, dst = (edge_index[0], edge_index[1])
        n = x.shape[0]
        h = _prelu(_hconv(x, W1, b1, src, dst, n), a)
        h = _hconv(h, W2, b2, src, dst, n) + x
        return _prelu(h, a)

    def _L3_gnn_ref(feats, W_gc, b_gc, W_res, b_res, Wg, bg, w1, b1, w2, b2, gamma, beta, src, dst):
        import jax, jax.numpy as jnp
        import numpy as np
        N_NODES = 512
        N_EDGES = 8192
        D_IN = 256
        D = 256
        H = 512
        E = 64
        TOP_K = 2
        CAP = 1024
        BN_EPS = 1e-05

        def _moe_ff(x, Wg, bg, w1, b1, w2, b2):
            N = x.shape[0]
            logits = x @ Wg + bg
            vals, idx = jax.lax.top_k(logits, TOP_K)
            gates = jax.nn.softmax(vals, axis=-1)
            e_flat = idx.reshape(-1)
            g_flat = gates.reshape(-1)
            tok = jnp.arange(N * TOP_K) // TOP_K
            order = jnp.argsort(e_flat)
            e_s, tok_s, g_s = (e_flat[order], tok[order], g_flat[order])
            counts = jnp.bincount(e_flat, length=E)
            offs = jnp.concatenate([jnp.zeros((1,), counts.dtype), jnp.cumsum(counts)[:-1]])
            rank = jnp.arange(N * TOP_K) - offs[e_s]
            valid = rank < CAP
            slot = jnp.where(valid, e_s * CAP + rank, E * CAP)
            buf = jnp.zeros((E * CAP + 1, D), x.dtype).at[slot].set(x[tok_s])
            h = buf[:E * CAP].reshape(E, CAP, D)
            h1 = jax.nn.gelu(jnp.einsum('ecd,edh->ech', h, w1) + b1[:, None, :], approximate=False)
            h2 = jnp.einsum('ech,ehd->ecd', h1, w2) + b2[:, None, :]
            out_buf = h2.reshape(E * CAP, D)
            y_s = jnp.where(valid[:, None], out_buf[jnp.minimum(slot, E * CAP - 1)], 0.0)
            return jnp.zeros((N, D), x.dtype).at[tok_s].add(g_s[:, None] * y_s)

        def _forward(feats, W_gc, b_gc, W_res, b_res, Wg, bg, w1, b1, w2, b2, gamma, beta, src, dst):
            n = feats.shape[0]
            ones = jnp.ones((src.shape[0],), feats.dtype)
            deg_out = jnp.clip(jax.ops.segment_sum(ones, src, num_segments=n), 1.0)
            deg_in = jnp.clip(jax.ops.segment_sum(ones, dst, num_segments=n), 1.0)
            h = feats * jax.lax.rsqrt(deg_out)[:, None]
            m = jax.ops.segment_sum(h[src], dst, num_segments=n) * jax.lax.rsqrt(deg_in)[:, None]
            gc = m @ W_gc + b_gc
            x = gc + (feats @ W_res + b_res)
            core = _moe_ff(x, Wg, bg, w1, b1, w2, b2)
            y = x + core
            mean = jnp.mean(y, axis=0)
            var = jnp.mean((y - mean) ** 2, axis=0)
            return (y - mean) * jax.lax.rsqrt(var + BN_EPS) * gamma + beta
        return _forward(feats, W_gc, b_gc, W_res, b_res, Wg, bg, w1, b1, w2, b2, gamma, beta, src, dst)
    edge_index = jnp.stack([src, dst])
    x = _layernorm(x + _L0_gnn_ref(x, L0_gnn_weight, L0_gnn_bias, src, dst), axis=-1)
    x = _layernorm(x + _L1_gnn_ref(x, edge_index, L1_gnn_W_conv, L1_gnn_b_conv, L1_gnn_W_lin, L1_gnn_b_lin, L1_gnn_W_dec1, L1_gnn_b_dec1, L1_gnn_W_dec2, L1_gnn_b_dec2), axis=-1)
    x = _layernorm(x + _L2_gnn_ref(x, edge_index, L2_gnn_W1, L2_gnn_b1, L2_gnn_W2, L2_gnn_b2, L2_gnn_a), axis=-1)
    x = _layernorm(x + _L3_gnn_ref(x, L3_gnn_W_gc, L3_gnn_b_gc, L3_gnn_W_res, L3_gnn_b_res, L3_gnn_Wg, L3_gnn_bg, L3_gnn_w1, L3_gnn_b1, L3_gnn_w2, L3_gnn_b2, L3_gnn_gamma, L3_gnn_beta, src, dst), axis=-1)
    return x

_drawn_inputs = setup_inputs


def setup_inputs(seed=0):
    import zlib

    import numpy as np

    out = dict(_drawn_inputs(seed))
    spreads = {'L0_gnn_bias': (0.0, 0.1),
     'L1_gnn_b_conv': (0.0, 0.1),
     'L1_gnn_b_lin': (0.0, 0.1),
     'L1_gnn_b_dec1': (0.0, 0.1),
     'L1_gnn_b_dec2': (0.0, 0.1),
     'L2_gnn_b1': (0.0, 0.1),
     'L2_gnn_b2': (0.0, 0.1),
     'L3_gnn_b_gc': (0.0, 0.1),
     'L3_gnn_b_res': (0.0, 0.1),
     'L3_gnn_bg': (0.0, 0.1),
     'L3_gnn_b1': (0.0, 0.1),
     'L3_gnn_b2': (0.0, 0.1),
     'L3_gnn_gamma': (1.0, 0.2),
     'L3_gnn_beta': (0.0, 0.1)}
    factors = {}
    for name, (base, spread) in spreads.items():
        noise = np.random.default_rng([zlib.crc32(name.encode()), seed]).standard_normal(out[name].shape)
        drawn = base * np.exp(spread * noise) if base else spread * noise
        out[name] = jnp.asarray(drawn.astype(out[name].dtype))
    for name, factor in factors.items():
        out[name] = (out[name] * factor).astype(out[name].dtype)
    return out
```

```python
from contextlib import ExitStack

import concourse.bass as bass
from concourse import mybir

ALU = mybir.AluOpType
ACT = mybir.ActivationFunctionType
AX = mybir.AxisListType
F32 = mybir.dt.float32
BF16 = mybir.dt.bfloat16
F16 = mybir.dt.float16
I32 = mybir.dt.int32
U32 = mybir.dt.uint32

P = 128
TOP = 2
CAP = 1024
EPS = 1e-05
FAR = 8191


class Steps:

    def __init__(self, eng, sem, per_tile=0):
        self.eng, self.sem, self.per_tile, self.base, self.n = eng, sem, per_tile, 0, 0

    def tile(self, i):
        assert self.n in (0, self.per_tile), (self.n, self.per_tile)
        self.base, self.n = i * self.per_tile, 0

    def done(self, ins):
        self.n += 1
        ins.then_inc(self.sem, 1)
        self.eng.wait_ge(self.sem, self.base + self.n)


def gnn_program(nc, A, out):
    x, src, dst = A["x"], A["src"], A["dst"]
    N, F = x.shape
    E = src.shape[0]
    T = (N + P - 1) // P
    NP = T * P
    LAST = N - (T - 1) * P
    EC = (E + P - 1) // P
    EG = (EC + P - 1) // P
    HC = A["L1_gnn_W_conv"].shape[1]
    HL = A["L1_gnn_W_lin"].shape[1]
    NE, _, H = A["L3_gnn_w1"].shape
    HT = H // P
    KF = F // P
    PARTS = 3
    BANK = 512
    NB = (NP + BANK - 1) // BANK
    TPB = BANK // P
    MID = NP // 2
    MAXCH = TOP * N // P + NE
    MAXCH += MAXCH % 2
    NCH = MAXCH + 2
    ZROWS = max(k for k in range(1, 21) if NCH % k == 0)
    TRASH = NCH * P
    assert T % 2 == 1 and MAXCH < P and F == 256 and HC == P

    a_fwd = nc.dram_tensor("counts_src_on_rows", (T, P, T * P), BF16, kind="Internal").ap()
    a_rev = nc.dram_tensor("counts_dst_on_rows", (T, P, T * P), BF16, kind="Internal").ap()
    xbuf = nc.dram_tensor("expert_rows_in", (TRASH + TOP * NP, F), F32, kind="Internal").ap()
    ybuf = nc.dram_tensor("expert_rows_out", (TRASH, F), F32, kind="Internal").ap()

    with ExitStack() as ctx:
        def sb(name, shape, dt=F32):
            return ctx.enter_context(nc.sbuf_tensor(name, shape, dt))

        sems = {}

        def S(name):
            if name not in sems:
                sems[name] = ctx.enter_context(nc.semaphore(name))
            return sems[name]

        X = sb("X", [P, T, F])
        X4 = sb("X4", [P, T, F])
        xsa = sb("xsa", [P, T * PARTS * F], BF16)
        xsb = sb("xsb", [P, T * PARTS * F], BF16)
        XSa = xsa[:, :].rearrange("p (t s f) -> p t s f", t=T, s=PARTS)
        XSb = xsb[:, :].rearrange("p (t s f) -> p t s f", t=T, s=PARTS)
        blk = [sb(f"blk{n}", [P, T * P], BF16) for n in range(2)]
        identF = sb("identF", [P, P])
        identB = sb("identB", [P, P], BF16)
        zrow = sb("zrow", [P, BANK], BF16)
        ones = sb("ones", [P, P])
        onesB = sb("onesB", [P, 1], BF16)
        wl0 = sb("wl0", [P, KF, F])
        wcv = sb("wcv", [P, KF, HC])
        wln = sb("wln", [P, HL])
        wd1 = sb("wd1", [HL, HC])
        wd2 = sb("wd2", [P, F])
        wh1 = sb("wh1", [P, KF, F])
        wh2 = sb("wh2", [P, KF, F])
        wgc = sb("wgc", [P, KF, F])
        wrs = sb("wrs", [P, KF, F])
        wgt = sb("wgt", [P, KF, NE])
        bc = {k: sb("bc_" + k, [P, F]) for k in ("l0", "dec2", "h1", "h2", "gc", "res", "gam", "bet")}
        bgb = sb("bgb", [P, NE])
        col = {k: sb("col_" + k, [P, 1]) for k in ("conv", "lin", "dec1", "a")}
        b1T = sb("b1T", [P, HT, NE])
        outdeg = sb("outdeg", [P, T])
        indeg = sb("indeg", [P, T])
        nsrc = sb("nsrc", [P, T])
        ndst = sb("ndst", [P, T])
        dis = sb("dis", [P, T])
        dinv = sb("dinv", [P, T])
        binv = sb("binv", [P, T])
        mhalf = sb("mhalf", [P, T])
        tab = sb("tab", [1, 3, 32], I32)
        G = sb("G", [P, F])
        G2 = sb("G2", [P, F])
        V = sb("V", [P, F])
        R1 = sb("R1", [P, F])
        U = sb("U", [P, F])
        Xn = sb("Xn", [P, F])
        tT = sb("tT", [P, KF, P])
        tT2 = sb("tT2", [P, KF, P])
        st6 = sb("st6", [P, 6])
        mv = sb("mv", [P, 2])
        ve = sb("ve", [P, 1])
        rstd = sb("rstd", [P, 1])
        max8 = sb("max8", [P, 8])
        idx8 = sb("idx8", [P, 8], U32)

        def view(buf, at, n, dt):
            w = 2 if dt in (F32, I32, U32) else 1
            v = buf[:, at:at + n * w]
            return (v if dt == BF16 else v.bitcast(dt)), at + n * w

        at = 0
        iota_s, at = view(xsb, at, NP, F16)
        iota_p, at = view(xsb, at, P, F16)
        src_rows_i, at = view(xsb, at, EG * P, I32)
        dst_rows_i, at = view(xsb, at, EG * P, I32)
        src_rows, at = view(xsb, at, EG * P, F32)
        dst_rows, at = view(xsb, at, EG * P, F32)
        chunk_lo, at = view(xsb, at, EG * 32, F32)
        chunk_hi, at = view(xsb, at, EG * 32, F32)
        chunk_id, at = view(xsb, at, EG * P, F32)
        in_band, at = view(xsb, at, EG * P, F32)
        scr1, at = view(xsb, at, EG * P, F32)
        bandcol, at = view(xsb, at, 8, F32)
        bandrow, at = view(xsb, at, 4 * 32, F32)
        assert at <= T * PARTS * F
        at = 0
        one_s = [None, None]
        one_s[0], at = view(xsa, at, NP, BF16)
        one_s[1], at = view(xsa, at, NP, BF16)
        both_s = xsa[:, 0:2 * NP].rearrange("p (b s) -> p b s", b=2)
        band_rows, at = view(xsa, at, NP, BF16)
        band_cols, at = view(xsa, at, NP, BF16)
        dcol, at = view(xsa, at, EG * P, F32)
        scol, at = view(xsa, at, EG * P, F32)
        both_d, at = view(xsa, at, 2 * P, BF16)
        both_d = both_d.rearrange("p (b s) -> p b s", b=2)
        assert at <= T * PARTS * F

        b1rows = sb("b1rows", [NE, H])
        tri = sb("tri", [P, P])
        vmask = sb("vmask", [P, P])
        iota_e = sb("iota_e", [P, NE])
        valid = sb("valid", [P, T])
        trash = sb("trash", [P, TOP, T])
        pcol = sb("pcol", [P, 1])
        etab = sb("etab", [1, P], I32)
        npair = sb("npair", [1, 1], I32)
        gate = sb("gate", [P, TOP, T])
        slot_to = sb("slot_to", [P, TOP, T], U32)
        slot_from = sb("slot_from", [P, TOP, T], U32)

        def cut(buf, at, shape, dt=F32):
            n = 1
            for s_ in shape:
                n *= s_
            v, at = view(buf, at, n, dt)
            if len(shape) == 2:
                v = v.rearrange("p (a b) -> p a b", a=shape[0])
            return v, at

        at = 0
        top_val, at = cut(xsb, at, (T, TOP))
        top_idx, at = cut(xsb, at, (T, TOP), U32)
        idxf, at = cut(xsb, at, (T, TOP))
        gap, at = cut(xsb, at, (T,))
        OH1, at = cut(xsb, at, (T, NE))
        OH2, at = cut(xsb, at, (T, NE))
        M, at = cut(xsb, at, (T, NE))
        CS, at = cut(xsb, at, (T, NE))
        rk, at = cut(xsb, at, (TOP, T))
        slot, at = cut(xsb, at, (TOP, T))
        keep, at = cut(xsb, at, (TOP, T))
        ecnt, at = cut(xsb, at, (NE,))
        eint, at = cut(xsb, at, (NE,), I32)
        eincl, at = cut(xsb, at, (NE,))
        ebase, at = cut(xsb, at, (NE,))
        ecol, at = cut(xsb, at, (2,))
        assert at <= T * PARTS * F
        SQ, at = cut(xsb, 0, (T, F))
        at = 0
        RNK, at = cut(xsa, at, (T, NE))
        w1s, w2s, xin, xTs, hTs, yout, b2s, ring = ([] for _ in range(8))
        for bufs, shape in ((w1s, (KF, H)), (w2s, (HT, F)), (xin, (F,)), (xTs, (F,)), (hTs, (HT, P)), (yout, (F,)),
                            (b2s, (F,))):
            for _ in range(2):
                v, at = cut(xsa, at, shape)
                bufs.append(v)
        assert at <= T * PARTS * F
        for n in range(4):
            v, _ = cut(xsa, 2 * n * TOP * F, (TOP, F))
            ring.append(v)

        psum = ctx.enter_context(nc.psum_tensor("psum", [P, 8, BANK], F32))
        agg = [psum[:, 0, 0:F], psum[:, 1, 0:F]]
        pT, pD, pT2, pD2, pE, pF = (psum[:, n, 0:F] for n in range(2, 8))

        block = ctx.enter_context(nc.Block())
        PHASES = ["load", "table", "counts", "split", "l0", "l1", "h1a", "h1b", "h2a", "h2b", "l3", "route", "experts",
                  "combine"]

        def phase_end(e, name):
            e.drain().then_inc(S("phases_ended"), 1)
            e.wait_ge(S("phases_ended"), 5 * (PHASES.index(name) + 1))

        SIGNALS = {
            "scaled": ["split", "l0", "h2b"], "part0": ["split", "l0", "l1", "h1a", "h1b", "h2a", "h2b"],
            "summed": ["l0", "l1", "h1a", "h1b", "h2a", "h2b", "l3"],
            "g_turned": ["l0", "l1", "h1b", "l3"], "pre": ["l0", "l1", "l3"], "x_turned": ["l0", "l1", "l3"],
            "proj": ["l0", "l1", "h1b"], "lin": ["l1"], "dec": ["l1"], "zT": ["l1"], "dT": ["l1"],
            "normed": ["l0", "l1", "h2b"], "negative": ["l0"], "exped": ["l0"], "active": ["h1b"],
            "own_copied": ["l3"], "x4_made": ["l3"], "x4_turned": ["l3"], "x4T": ["l3"], "logits": ["l3"],
            "x4_kept": ["l3"], "top": ["l3"]}
        SIGNALS["rest"] = SIGNALS["part1"] = SIGNALS["part2"] = SIGNALS["part0"]
        SIGNALS["sum_read"] = SIGNALS["summed"]
        SIGNALS["gT"], SIGNALS["xT"] = SIGNALS["g_turned"], SIGNALS["x_turned"]
        SIGNALS["moments"] = SIGNALS["eps"] = SIGNALS["rstd"] = SIGNALS["x_kept"] = SIGNALS["normed"]

        def past(ph, name):
            return T * SIGNALS[name].index(ph)

        def past_blocks(ph, par):
            return (T // 2 + (1 - par)) * SIGNALS["summed"].index(ph)

        def carry_wait(e):
            e.sem_inc(S("waits_carried"), 1)

        def tiles(e, body):
            with e.Fori(0, T // 2) as j:
                body(2 * j, 0)
                body(2 * j + 1, 1)
            body(T - 1, 0)

        def at_tile(buf, i):
            return buf[:, bass.ds(i, 1)]

        def sync_moe(e):
            phase_end(e, "route")

            def load_rows(c, par):
                e.dma_start(xin[par], xbuf[bass.ds(c * P, P), :]).then_inc(S(f"rows_in{par}"), 16)

            def load_w1(c, ex, par):
                e.dma_start(w1s[par], A["L3_gnn_w1"][bass.ds(ex, 1), :, :].rearrange("a (k p) h -> p (a k) h", p=P))\
                    .then_inc(S(f"w1_in{par}"), 16)

            def load_w2(c, ex, par):
                e.dma_start(w2s[par], A["L3_gnn_w2"][bass.ds(ex, 1), :, :].rearrange("a (k p) f -> p (a k) f", p=P))\
                    .then_inc(S(f"w2_in{par}"), 16)
                e.dma_start(b2s[par], A["L3_gnn_b2"][bass.ds(ex, 1), :].to_broadcast([P, F]))\
                    .then_inc(S(f"b2_in{par}"), 16)

            def expert_of(c):
                return e.value_load(etab[0:1, bass.ds(c, 1)], min_val=0, max_val=NE - 1)

            for c in range(2):
                ex = expert_of(c)
                load_rows(c, c)
                load_w1(c, ex, c)
                load_w2(c, ex, c)
            pairs = e.value_load(npair[0:1, 0:1], min_val=1, max_val=MAXCH // 2)
            with e.Fori(0, pairs) as j:
                for par in range(2):
                    c = 2 * j + par
                    ex = expert_of(c + 2)
                    e.wait_ge(S("chunk_turned"), c + 1)
                    load_rows(c + 2, par)
                    e.wait_ge(S("hidden_summed"), c + 1)
                    load_w1(c + 2, ex, par)
                    e.wait_ge(S("chunk_made"), c + 3)
                    load_w2(c + 2, ex, par)
            for par in range(2):
                for name in ("rows_in", "w1_in", "w2_in", "b2_in"):
                    e.wait_ge(S(f"{name}{par}"), 16 * pairs + 16)
            carry_wait(e)
            phase_end(e, "experts")
            phase_end(e, "combine")
            with e.Fori(0, T - 1) as t:
                e.wait_ge(S("out_made"), t + 1)
                e.dma_start(out[bass.ds(t * P, P), :], X4[:, bass.ds(t, 1), :].rearrange("p a f -> p (a f)"))\
                    .then_inc(S("out_stored"), 16)
            e.wait_ge(S("out_made"), T)
            e.dma_start(out[(T - 1) * P:N, :], X4[0:LAST, T - 1, :]).then_inc(S("out_stored"), 16)
            e.wait_ge(S("out_stored"), 16 * T)

        def pe_moe(e):
            for h in range(HT):
                mm = e.transpose(psum[:, 5, h * NE:(h + 1) * NE], b1rows[:, h * P:(h + 1) * P], identF[0:NE, 0:NE])
            mm.then_inc(S("b1_turned"), 1)
            e.wait_ge(S("running_counts"), 1)
            for t in range(T):
                o = psum[:, t // 8, (t % 8) * NE:(t % 8 + 1) * NE]
                mm = e.matmul(o, tri[:, :], M[:, t, :], start=True, stop=(t == 0))
                if t:
                    mm = e.matmul(o, ones[:, :], CS[:, t - 1, :], start=False, stop=True)
            e.matmul(psum[:, 4, 0:NE], ones[:, :], CS[:, T - 1, :], start=True, stop=True).then_inc(S("ranked"), 1)
            e.wait_ge(S("chunk_experts"), 1)
            e.transpose(psum[0:1, 6, 0:P], ecol[:, 0:1], identF[:, :]).then_inc(S("chunk_experts_up"), 1)
            phase_end(e, "route")

            def turn(c, j, par):
                e.wait_ge(S(f"rows_in{par}"), 16 * j + 16)
                for k in range(KF):
                    mm = e.transpose(psum[:, par, k * P:(k + 1) * P], xin[par][:, k * P:(k + 1) * P], identF[:, :])
                mm.then_inc(S("chunk_turned"), 1)

            def hidden(c, j, par):
                e.wait_ge(S("chunk_copied"), c + 1)
                e.wait_ge(S(f"w1_in{par}"), 16 * j + 16)
                for h in range(HT):
                    for k in range(KF):
                        mm = e.matmul(psum[:, 2 + par, h * P:(h + 1) * P], w1s[par][:, k, h * P:(h + 1) * P],
                                      xTs[par][:, k * P:(k + 1) * P], start=(k == 0), stop=(k == KF - 1))
                mm.then_inc(S("hidden_summed"), 1)

            def rows_out(c, j, par):
                e.wait_ge(S("gelu_made"), c + 1)
                e.wait_ge(S(f"w2_in{par}"), 16 * j + 16)
                e.wait_ge(S("chunk_made"), c + 1)
                for h in range(HT):
                    mm = e.matmul(psum[:, 4 + par, 0:F], hTs[par][:, h, :], w2s[par][:, h, :],
                                  start=(h == 0), stop=(h == HT - 1))
                mm.then_inc(S("chunk_summed"), 1)

            pairs = e.value_load(npair[0:1, 0:1], min_val=1, max_val=MAXCH // 2)
            turn(0, 0, 0)
            turn(1, 0, 1)
            hidden(0, 0, 0)
            with e.Fori(0, pairs) as j:
                for par in range(2):
                    c = 2 * j + par
                    e.wait_ge(S("chunk_copied"), c + 1)
                    turn(c + 2, j + 1, par)
                    e.wait_ge(S("gelu_made"), c)
                    hidden(c + 1, j + par, 1 - par)
                    rows_out(c, j, par)
            phase_end(e, "experts")
            for n in range(2):
                e.matmul(psum[:, n, 0:F], zrow[:, 0:P], zrow[:, 0:F], start=True, stop=True)
            for n, (name, buf) in enumerate((("combined", X4), ("squared", SQ))):
                with e.Fori(0, T - 1) as t:
                    e.wait_ge(S(name), t + 1)
                    r = buf[:, bass.ds(t, 1), :].rearrange("p a f -> p (a f)")
                    e.matmul(psum[:, n, 0:F], ones[:, :], r, start=False, stop=True, skip_group_check=True)
                e.wait_ge(S(name), T)
                e.matmul(psum[:, n, 0:F], vmask[:, :], buf[:, T - 1, :], start=False, stop=True,
                         skip_group_check=True).then_inc(S("bn_summed"), 1)
            phase_end(e, "combine")

        def act_moe(e):
            e.wait_ge(S("top_gap"), 1)
            e.activation(gate[:, 1, :], gap, ACT.Exp).then_inc(S("top_exp"), 1)
            e.wait_ge(S("b1_turned"), 1)
            e.activation(b1T[:, :, :].rearrange("p h x -> p (h x)"), psum[:, 5, 0:HT * NE], ACT.Copy)\
                .then_inc(S("b1_ready"), 1)
            e.wait_ge(S("b1_ready"), 1)
            phase_end(e, "route")

            def gelu(c, par):
                ex = e.value_load(etab[0:1, bass.ds(c, 1)], min_val=0, max_val=NE - 1)
                e.wait_ge(S("hidden_summed"), c + 1)
                for h in range(HT):
                    mm = e.activation(hTs[par][:, h, :], psum[:, 2 + par, h * P:(h + 1) * P], ACT.Gelu,
                                      bias=b1T[:, h, bass.ds(ex, 1)])
                mm.then_inc(S("gelu_made"), 1)

            pairs = e.value_load(npair[0:1, 0:1], min_val=1, max_val=MAXCH // 2)
            gelu(0, 0)
            with e.Fori(0, pairs) as j:
                for par in range(2):
                    c = 2 * j + par
                    e.wait_ge(S("chunk_summed"), c)
                    gelu(c + 1, 1 - par)
            phase_end(e, "experts")

            def square(t, par):
                e.wait_ge(S("centred"), t + 1)
                e.activation(SQ[:, bass.ds(t, 1), :].rearrange("p a f -> p (a f)"),
                             X4[:, bass.ds(t, 1), :].rearrange("p a f -> p (a f)"), ACT.Square)\
                    .then_inc(S("squared"), 1)
            tiles(e, square)
            phase_end(e, "combine")

        def dve_moe(e):
            phase_end(e, "l3")
            st = Steps(e, S("dve_route"))
            e.tensor_tensor(gap, top_val[:, :, 1], top_val[:, :, 0], ALU.subtract).then_inc(S("top_gap"), 1)
            st.done(e.tensor_copy(idxf, top_idx[:, :, 0:TOP]))
            one_hot = (OH1, OH2)
            ex_ids = iota_e[:, :].unsqueeze(1).to_broadcast([P, T, NE])
            alive = valid[:, :].unsqueeze(2).to_broadcast([P, T, NE])
            for k in range(TOP):
                st.done(e.tensor_tensor(one_hot[k], ex_ids, idxf[:, :, k:k + 1].to_broadcast([P, T, NE]),
                                        ALU.is_equal))
                st.done(e.tensor_tensor(one_hot[k], one_hot[k], alive, ALU.mult))
            st.done(e.tensor_tensor(M, OH1, OH2, ALU.add))
            st.done(e.tensor_copy(CS[:, 0, :], M[:, 0, :]))
            for t in range(1, T):
                st.done(e.tensor_tensor(CS[:, t, :], CS[:, t - 1, :], M[:, t, :], ALU.add))
            e.sem_inc(S("running_counts"), 1)
            e.wait_ge(S("ranked"), 1)
            for q in range(4):
                w = min(BANK, T * NE - q * BANK)
                st.done(e.tensor_copy(RNK.rearrange("p t x -> p (t x)")[:, q * BANK:q * BANK + w],
                                      psum[:, q, 0:w]))
            st.done(e.tensor_scalar(ecnt, psum[:, 4, 0:NE], float(CAP), float(P - 1), ALU.min, ALU.add))
            st.done(e.tensor_copy(eint, ecnt))
            st.done(e.tensor_scalar(eint, eint, 7, None, ALU.arith_shift_right))
            st.done(e.tensor_copy(ecnt, eint))
            st.done(e.tensor_tensor_scan(eincl, ones[:, 0:NE], ecnt, 0.0, ALU.mult, ALU.add))
            st.done(e.tensor_tensor(ebase, eincl, ecnt, ALU.subtract))
            st.done(e.tensor_scalar(ecnt, eincl, pcol[:, 0:1], None, ALU.is_le))
            st.done(e.tensor_reduce(ecol[:, 1:2], ecnt, AX.X, ALU.add))
            e.tensor_scalar(ecol[:, 0:1], ecol[:, 1:2], float(NE - 1), None, ALU.min)\
                .then_inc(S("chunk_experts"), 1)
            st.done(e.tensor_scalar(eint[0:1, 0:1], eincl[0:1, NE - 1:NE], 1.0, None, ALU.add))
            st.done(e.tensor_scalar(npair[0:1, 0:1], eint[0:1, 0:1], 1, None, ALU.arith_shift_right))
            st.done(e.tensor_scalar(ebase, ebase, float(P), None, ALU.mult))
            first_row = ebase.unsqueeze(1).to_broadcast([P, T, NE])
            for k in range(TOP):
                st.done(e.tensor_tensor(M, one_hot[k], RNK, ALU.mult))
                st.done(e.tensor_reduce(rk[:, k, :], M, AX.X, ALU.add))
                st.done(e.tensor_tensor(M, one_hot[k], first_row, ALU.mult))
                st.done(e.tensor_reduce(slot[:, k, :], M, AX.X, ALU.add))
                st.done(e.tensor_tensor(slot[:, k, :], slot[:, k, :], rk[:, k, :], ALU.add))
                st.done(e.scalar_tensor_tensor(keep[:, k, :], rk[:, k, :], float(CAP), valid[:, :],
                                               ALU.is_lt, ALU.mult))
                st.done(e.tensor_tensor(slot[:, k, :], slot[:, k, :], keep[:, k, :], ALU.mult))
                st.done(e.tensor_copy(slot_from[:, k, :], slot[:, k, :]))
                st.done(e.tensor_scalar(rk[:, k, :], keep[:, k, :], -1.0, 1.0, ALU.mult, ALU.add))
                st.done(e.tensor_tensor(rk[:, k, :], rk[:, k, :], trash[:, k, :], ALU.mult))
                st.done(e.tensor_tensor(slot[:, k, :], slot[:, k, :], rk[:, k, :], ALU.add))
                st.done(e.tensor_copy(slot_to[:, k, :], slot[:, k, :]))
            e.sem_inc(S("slots_ready"), 1)
            e.wait_ge(S("top_exp"), 1)
            st.done(e.tensor_scalar(gap, gate[:, 1, :], 1.0, None, ALU.add))
            st.done(e.reciprocal(gate[:, 0, :], gap))
            st.done(e.tensor_tensor(gate[:, 1, :], gate[:, 1, :], gate[:, 0, :], ALU.mult))
            for k in range(TOP):
                st.done(e.tensor_tensor(gate[:, k, :], gate[:, k, :], keep[:, k, :], ALU.mult))
            e.wait_ge(S("chunk_experts_up"), 1)
            st.done(e.tensor_copy(etab[0:1, :], psum[0:1, 6, 0:P]))
            phase_end(e, "route")

            def copy_turned(c, par):
                e.wait_ge(S("chunk_turned"), c + 1)
                e.tensor_copy(xTs[par], psum[:, par, 0:F]).then_inc(S("chunk_copied"), 1)

            e.sem_inc(S("chunk_made"), 2)
            copy_turned(0, 0)
            copy_turned(1, 1)
            pairs = e.value_load(npair[0:1, 0:1], min_val=1, max_val=MAXCH // 2)
            with e.Fori(0, pairs) as j:
                for par in range(2):
                    c = 2 * j + par
                    e.wait_ge(S("hidden_summed"), c + 1)
                    copy_turned(c + 2, par)
                    e.wait_ge(S("chunk_summed"), c + 1)
                    e.wait_ge(S(f"b2_in{par}"), 16 * j + 16)
                    e.wait_ge(S(f"rows_stored{par}"), 16 * j)
                    e.tensor_tensor(yout[par], psum[:, 4 + par, 0:F], b2s[par], ALU.add)\
                        .then_inc(S("chunk_made"), 1)
            phase_end(e, "experts")
            st = Steps(e, S("dve_bn"))
            for t in range(T):
                r = ring[t % 4]
                e.wait_ge(S(f"gathered{t % 4}"), 32 * (t // 4) + 32)
                st.done(e.scalar_tensor_tensor(X4[:, t, :], r[:, 0, :], gate[:, 0, t:t + 1], X4[:, t, :],
                                               ALU.mult, ALU.add))
                e.scalar_tensor_tensor(X4[:, t, :], r[:, 1, :], gate[:, 1, t:t + 1], X4[:, t, :],
                                       ALU.mult, ALU.add).then_inc(S("combined"), 1)
            e.wait_ge(S("combined"), T)
            e.wait_ge(S("bn_summed"), 1)
            st.done(e.tensor_scalar(G[:, :], psum[:, 0, 0:F], 1.0 / N, None, ALU.mult))
            for t in range(T):
                e.tensor_tensor(X4[:, t, :], X4[:, t, :], G[:, :], ALU.subtract).then_inc(S("centred"), 1)
            e.wait_ge(S("centred"), T)
            e.wait_ge(S("bn_summed"), 2)
            e.tensor_scalar(V[:, :], psum[:, 1, 0:F], 1.0 / N, EPS, ALU.mult, ALU.add).then_inc(S("bn_var"), 1)
            e.wait_ge(S("bn_rstd"), 1)
            st.done(e.tensor_tensor(U[:, :], V[:, :], bc["gam"][:, :], ALU.mult))
            phase_end(e, "combine")
            stf = Steps(e, S("dve_out"), 6)

            def last(t, par):
                stf.tile(t)
                xt = X[:, bass.ds(t, 1), :].rearrange("p a f -> p (a f)")
                yt = X4[:, bass.ds(t, 1), :].rearrange("p a f -> p (a f)")
                stf.done(e.tensor_tensor(yt, yt, U[:, :], ALU.mult))
                stf.done(e.tensor_tensor(yt, yt, bc["bet"][:, :], ALU.add))
                stf.done(e.tensor_tensor(yt, yt, xt, ALU.add))
                carry_wait(e)
                stf.done(e.bn_stats(st6[:, :], yt))
                carry_wait(e)
                stf.done(e.bn_aggr(mv[:, :], st6[:, :]))
                e.sem_inc(S("out_moments"), 1)
                e.wait_ge(S("out_rstd"), t + 1)
                stf.done(e.tensor_scalar(yt, yt, mv[:, 0:1], rstd[:, 0:1], ALU.subtract, ALU.mult))
                e.sem_inc(S("out_made"), 1)
            tiles(e, last)

        def pool_moe(e):
            phase_end(e, "l3")
            e.wait_ge(S("slots_ready"), 1)
            for t in range(T):
                for k in range(TOP):
                    e.indirect_dma_start(out=xbuf, out_offset=bass.IndirectOffsetOnAxis(ap=slot_to[:, k, t:t + 1], axis=0),
                                         in_=X4[:, t, :], in_offset=None).then_inc(S("rows_scattered"), 16)
            e.wait_ge(S("rows_scattered"), 16 * TOP * T)
            phase_end(e, "route")
            pairs = e.value_load(npair[0:1, 0:1], min_val=1, max_val=MAXCH // 2)
            with e.Fori(0, pairs) as j:
                for par in range(2):
                    c = 2 * j + par
                    e.wait_ge(S("chunk_made"), c + 3)
                    e.dma_start(ybuf[bass.ds(c * P, P), :], yout[par]).then_inc(S(f"rows_stored{par}"), 16)
            for par in range(2):
                e.wait_ge(S(f"rows_stored{par}"), 16 * pairs)
            carry_wait(e)
            phase_end(e, "experts")
            for t in range(T):
                if t >= 4:
                    e.wait_ge(S("combined"), t - 3)
                for k in range(TOP):
                    e.indirect_dma_start(out=ring[t % 4][:, k, :], out_offset=None, in_=ybuf,
                                         in_offset=bass.IndirectOffsetOnAxis(ap=slot_from[:, k, t:t + 1], axis=0))\
                        .then_inc(S(f"gathered{t % 4}"), 16)
            e.wait_ge(S("bn_var"), 1)
            for f in range(0, F, T):
                w = min(T, F - f)
                mm = e.tensor_tensor(V[:, f:f + w], V[:, f:f + w], mhalf[:, 0:w], ALU.pow)
            mm.then_inc(S("bn_rstd"), 1)
            phase_end(e, "combine")

            def norm(t, par):
                e.wait_ge(S("out_moments"), t + 1)
                carry_wait(e)
                e.tensor_scalar(ve[:, :], mv[:, 1:2], EPS, None, ALU.add).then_inc(S("out_eps"), 1)
                e.wait_ge(S("out_eps"), t + 1)
                e.tensor_tensor(rstd[:, :], ve[:, :], mhalf[:, 0:1], ALU.pow).then_inc(S("out_rstd"), 1)
            tiles(e, norm)

        @block.sync
        def _(e):
            ld = S("inputs_loaded")
            n = [0]

            def load(o, i):
                e.dma_start(o, i).then_inc(ld, 16)
                n[0] += 16

            full = EC - 1
            e.wait_ge(S("pads_set"), 3)
            for rows, a in ((src_rows_i, src), (dst_rows_i, dst)):
                r = rows.rearrange("c (g e) -> c g e", g=EG)
                load(r[:, 0:EG - 1, :], a[0:(EG - 1) * P * P].rearrange("(g c e) -> c g e", g=EG - 1, c=P))
                k = full - (EG - 1) * P
                load(r[0:k, EG - 1, :], a[(EG - 1) * P * P:full * P].rearrange("(c e) -> c e", e=P))
                load(r[k:k + 1, EG - 1, 0:E - full * P], a[full * P:E].rearrange("(c e) -> c e", c=1))
            e.wait_ge(ld, n[0])
            e.sem_inc(S("edges_loaded"), 1)
            load(X[:, 0:T - 1, :], x[0:(T - 1) * P, :].rearrange("(t p) f -> p t f", p=P))
            load(X[0:LAST, T - 1, :], x[(T - 1) * P:N, :])
            for w, k in ((wl0, "L0_gnn_weight"), (wcv, "L1_gnn_W_conv"), (wh1, "L2_gnn_W1"), (wh2, "L2_gnn_W2"),
                         (wgc, "L3_gnn_W_gc"), (wrs, "L3_gnn_W_res"), (wgt, "L3_gnn_Wg")):
                load(w[:, :, :], A[k].rearrange("(k p) f -> p k f", p=P))
            for w, k in ((wln, "L1_gnn_W_lin"), (wd1, "L1_gnn_W_dec1"), (wd2, "L1_gnn_W_dec2")):
                load(w[:, :], A[k])
            for w, k in (("l0", "L0_gnn_bias"), ("dec2", "L1_gnn_b_dec2"), ("h1", "L2_gnn_b1"), ("h2", "L2_gnn_b2"),
                         ("gc", "L3_gnn_b_gc"), ("res", "L3_gnn_b_res"), ("gam", "L3_gnn_gamma"),
                         ("bet", "L3_gnn_beta")):
                load(bc[w][:, :], A[k].rearrange("(a f) -> a f", a=1).to_broadcast([P, F]))
            load(b1rows[:, :], A["L3_gnn_b1"])
            load(bgb[:, :], A["L3_gnn_bg"].rearrange("(a f) -> a f", a=1).to_broadcast([P, NE]))
            load(col["conv"][:, :], A["L1_gnn_b_conv"].rearrange("(p a) -> p a", a=1))
            load(col["lin"][0:HL, :], A["L1_gnn_b_lin"].rearrange("(p a) -> p a", a=1))
            load(col["dec1"][:, :], A["L1_gnn_b_dec1"].rearrange("(p a) -> p a", a=1))
            load(col["a"][:, :], A["L2_gnn_a"].rearrange("(p a) -> p a", a=1).to_broadcast([P, 1]))
            e.wait_ge(ld, n[0])
            phase_end(e, "load")
            phase_end(e, "table")
            e.wait_ge(S("zeros_set"), 1)
            zeros = X4[:, :, :].rearrange("p t f -> p (t f)")[:, 0:ZROWS * F].rearrange("p (k f) -> p k f", f=F)
            for buf in (xbuf, ybuf):
                with e.Fori(0, NCH // ZROWS) as g:
                    e.dma_start(buf[bass.ds(g * ZROWS * P, ZROWS * P), :].rearrange("(p k) f -> p k f", p=P),
                                zeros).then_inc(S("rows_zeroed"), 16)
            e.wait_ge(S("rows_zeroed"), 2 * 16 * (NCH // ZROWS))

            with e.Fori(0, T) as b:
                e.wait_ge(S("band_copied"), NB * (b + 1))
                e.dma_start(a_rev[:, :, bass.ds(b * P, P)].rearrange("s p c -> p s c"),
                            band_rows.rearrange("p (s c) -> p s c", c=P)).then_inc(S("band_rows_stored"), 16)
                e.wait_ge(S("band_turned"), NB * (b + 1))
                e.dma_start(a_fwd[bass.ds(b, 1), :, :].rearrange("a p c -> p (a c)"), band_cols)\
                    .then_inc(S("band_cols_stored"), 16)
            e.wait_ge(S("band_rows_stored"), 16 * T)
            e.wait_ge(S("band_cols_stored"), 16 * T)
            phase_end(e, "counts")
            phase_end(e, "split")

            def blocks(ph, mat):
                def load_block(i, par):
                    e.dma_start(blk[par][:, :], mat[bass.ds(i, 1), :, :].rearrange("a p c -> p (a c)"))\
                        .then_inc(S(f"block_in{par}"), 16)

                load_block(0, 0)
                load_block(1, 1)
                with e.Fori(1, T // 2) as j:
                    for par in range(2):
                        e.wait_ge(S("tile_summed"), past(ph, "summed") + 2 * j + par - 1)
                        load_block(2 * j + par, par)
                e.wait_ge(S("tile_summed"), past(ph, "summed") + T - 2)
                load_block(T - 1, 0)
                phase_end(e, ph)

            blocks("l0", a_fwd)
            blocks("l1", a_fwd)
            blocks("h1a", a_fwd)
            blocks("h1b", a_rev)
            blocks("h2a", a_fwd)
            blocks("h2b", a_rev)
            blocks("l3", a_fwd)
            sync_moe(e)

        @block.tensor
        def _(e):
            phase_end(e, "load")
            e.wait_ge(S("rows_float"), 2)
            e.wait_ge(S("ident_set"), 2)
            for g in range(EG):
                e.transpose(psum[:, 0, g * P:(g + 1) * P], src_rows[:, g * P:(g + 1) * P], identF[:, :])
                mm = e.transpose(psum[:, 1, g * P:(g + 1) * P], dst_rows[:, g * P:(g + 1) * P], identF[:, :])
            mm.then_inc(S("edges_turned"), 1)
            e.wait_ge(S("chunk_ends"), 2)
            for g in range(EG):
                e.matmul(psum[0:32, 2, g * P:(g + 1) * P], chunk_lo[:, g * 32:(g + 1) * 32], identF[:, :],
                         start=True, stop=True)
                mm = e.matmul(psum[0:32, 3, g * P:(g + 1) * P], chunk_hi[:, g * 32:(g + 1) * 32], identF[:, :],
                              start=True, stop=True)
            mm.then_inc(S("chunk_rows"), 1)
            e.wait_ge(S("band_cols_ready"), 2)
            for k in range(2):
                mm = e.transpose(psum[0:1, 4, k * 32:(k + 1) * 32], bandcol[0:32, k:k + 1], identF[0:32, 0:32])
            mm.then_inc(S("band_rows_up"), 1)
            phase_end(e, "table")

            psb = psum[:, :, :].rearrange("p b c -> p (b c)").bitcast(BF16).rearrange("p (b c) -> p b c", b=8)
            with e.Fori(0, T) as b:
                before = e.value_load(tab[0:1, 1, bass.ds(b, 1)], min_val=0, max_val=T * EC)
                upto = e.value_load(tab[0:1, 2, bass.ds(b, 1)], min_val=1, max_val=T * EC)
                e.wait_ge(S("band_turned"), NB * b)
                e.wait_ge(S("degrees_read"), b)
                for q in range(NB):
                    w = min(BANK, NP - q * BANK)
                    e.matmul(psum[:, q, 0:w], zrow[:, 0:P], zrow[:, 0:w], start=True, stop=True)
                e.matmul(psum[:, 7, 0:1], zrow[:, 0:P], zrow[:, 0:1], start=True, stop=True)
                with e.Fori(before, upto) as k:
                    e.wait_ge(S("onehots_ready"), 2 * k + 2)
                    lhs = both_d[:, bass.ds(k % 2, 1), :].rearrange("p a c -> p (a c)")
                    e.matmul(psum[:, 7, 0:1], lhs, onesB[:, :], start=False, stop=True, skip_group_check=True)
                    for q in range(NB):
                        w = min(BANK, NP - q * BANK)
                        mm = e.matmul(psum[:, q, 0:w], lhs,
                                      both_s[:, bass.ds(k % 2, 1), q * BANK:q * BANK + w].rearrange("p a c -> p (a c)"),
                                      start=False, stop=True, skip_group_check=True)
                    mm.then_inc(S("onehots_used"), 1)
                e.matmul(psum[:, 7, 1:2], zrow[:, 0:P], zrow[:, 0:1], start=True, stop=True)\
                    .then_inc(S("band_summed"), 1)
                for q in range(NB):
                    e.wait_ge(S("band_copied"), NB * b + q + 1)
                    for t in range(q * TPB, min(T, (q + 1) * TPB)):
                        o = (t - q * TPB) * P
                        e.matmul(psum[:, 7, 32 + t:33 + t], band_rows[:, t * P:(t + 1) * P], onesB[:, :],
                                 start=True, stop=True)
                        mm = e.transpose(psb[:, q, o:o + P], band_rows[:, t * P:(t + 1) * P], identB[:, :])
                    mm.then_inc(S("band_transposed"), 1)
            phase_end(e, "counts")
            phase_end(e, "split")

            def aggregate(ph, XS, Fw, own, steps):
                def add(i, par, side):
                    e.wait_ge(S(f"block_in{par}"), 16 * past_blocks(ph, par) + 8 * (i - par) + 16)
                    if isinstance(i, int) and i < 2:
                        pass
                    else:
                        e.wait_ge(S("tile_sum_read"), past(ph, "sum_read") + i - 1)
                    o = agg[par][:, 0:Fw]
                    for k in range(T):
                        for s in range(PARTS):
                            mm = e.matmul(o, blk[par][:, k * P:(k + 1) * P], XS[:, k, s, 0:Fw],
                                          start=(k == 0 and s == 0), stop=(not own and k == T - 1 and s == PARTS - 1))
                        if k % 4 == 3 and k // 4 < len(side) and not (own and k == T - 1):
                            side[k // 4]()
                    if own:
                        for s in range(PARTS):
                            mm = e.matmul(o, identB[:, :],
                                          XS[:, bass.ds(i, 1), s, 0:Fw].rearrange("p a f -> p (a f)"),
                                          start=False, stop=(s == PARTS - 1))
                    mm.then_inc(S("tile_summed"), 1)

                add(0, 0, [])
                with e.Fori(0, T // 2) as j:
                    add(2 * j + 1, 1, [lambda s=s: s(2 * j) for s in steps])
                    add(2 * j + 2, 0, [lambda s=s: s(2 * j + 1) for s in steps])
                for s in steps:
                    s(T - 1)
                phase_end(e, ph)

            def turn(ph, need, sig, o, a, nt):
                def step(i):
                    e.wait_ge(S("tile_" + need), past(ph, need) + i + 1)
                    for k in range(nt):
                        mm = e.transpose(o[:, k * P:(k + 1) * P], a[:, k * P:(k + 1) * P], identF[:, :])
                    mm.then_inc(S("tile_" + sig), 1)
                return step

            def dense(ph, need, sig, o, pairs):
                def step(i):
                    for nd in need:
                        e.wait_ge(S("tile_" + nd), past(ph, nd) + i + 1)
                    for n_, (l, r) in enumerate(pairs):
                        mm = e.matmul(o, l, r, start=(n_ == 0), stop=(n_ == len(pairs) - 1))
                    mm.then_inc(S("tile_" + sig), 1)
                return step

            def two(t, w):
                return [(t[:, k, :], w[:, k, :]) for k in range(KF)]

            aggregate("l0", XSa, F, False, [
                turn("l0", "sum_read", "g_turned", pT, G, KF),
                dense("l0", ["gT"], "pre", pD, two(tT, wl0)),
                turn("l0", "normed", "x_turned", pT2, Xn, KF),
                dense("l0", ["xT"], "proj", pD2[:, 0:HC], two(tT2, wcv))])
            aggregate("l1", XSb, HC, True, [
                turn("l1", "sum_read", "g_turned", pT, G, 1),
                dense("l1", ["gT"], "lin", pD[0:HL, 0:P], [(wln[:, :], tT[:, 0, :])]),
                dense("l1", ["zT"], "dec", pE[:, 0:P], [(wd1[:, :], G2[0:HL, 0:P])]),
                dense("l1", ["dT"], "pre", pF, [(tT[:, 1, :], wd2[:, :])]),
                turn("l1", "normed", "x_turned", pT2, Xn, KF),
                dense("l1", ["xT"], "proj", pD2, two(tT2, wh1))])
            aggregate("h1a", XSa, F, False, [])
            aggregate("h1b", XSb, F, False, [
                turn("h1b", "active", "g_turned", pT, G, KF),
                dense("h1b", ["gT"], "proj", pD2, two(tT, wh2))])
            aggregate("h2a", XSa, F, False, [])
            aggregate("h2b", XSb, F, False, [])
            aggregate("l3", XSa, F, False, [
                turn("l3", "own_copied", "x_turned", pT2, Xn, KF),
                turn("l3", "sum_read", "g_turned", pT, G, KF),
                dense("l3", ["xT", "gT"], "pre", pD, two(tT, wgc) + two(tT2, wrs)),
                turn("l3", "x4_made", "x4_turned", pT, V, KF),
                dense("l3", ["x4T"], "logits", pD2[:, 0:NE], two(tT, wgt))])
            pe_moe(e)

        @block.scalar
        def _(e):
            phase_end(e, "load")
            phase_end(e, "table")
            psb = psum[:, :, :].rearrange("p b c -> p (b c)").bitcast(BF16).rearrange("p (b c) -> p b c", b=8)
            with e.Fori(0, T) as b:
                e.wait_ge(S("band_summed"), b + 1)
                e.wait_ge(S("band_rows_stored"), 16 * b)
                for q in range(NB):
                    w = min(BANK, NP - q * BANK)
                    e.activation(band_rows[:, q * BANK:q * BANK + w], psum[:, q, 0:w], ACT.Copy)\
                        .then_inc(S("band_copied"), 1)
                e.wait_ge(S("band_cols_stored"), 16 * b)
                for q in range(NB):
                    w = min(BANK, NP - q * BANK)
                    e.wait_ge(S("band_transposed"), NB * b + q + 1)
                    e.activation(band_cols[:, q * BANK:q * BANK + w], psb[:, q, 0:w], ACT.Copy)\
                        .then_inc(S("band_turned"), 1)
            phase_end(e, "counts")

            def split_a(ph, need, a, XS, w):
                def do(i, v=a):
                    e.wait_ge(S("tile_" + need), past(ph, need) + i + 1)
                    e.activation(XS[:, bass.ds(i, 1), 0, 0:w].rearrange("p a f -> p (a f)"), v, ACT.Copy)\
                        .then_inc(S("tile_part0"), 1)
                    e.wait_ge(S("tile_rest"), past(ph, "rest") + i + 1)
                    e.activation(XS[:, bass.ds(i, 1), 1, 0:w].rearrange("p a f -> p (a f)"), R1[:, 0:w], ACT.Copy)\
                        .then_inc(S("tile_part1"), 1)
                return do

            def copy(ph, need, sig, o, a, func=ACT.Copy, **kw):
                def do(i):
                    e.wait_ge(S("tile_" + need), past(ph, need) + i + 1)
                    e.activation(o, a, func, **kw).then_inc(S("tile_" + sig), 1)
                return do

            def run(ph, todo):
                def body(i, par):
                    for d in todo:
                        d(i)
                tiles(e, body)
                phase_end(e, ph)

            def flat(t):
                return t[:, :, :].rearrange("p k c -> p (k c)")

            run("split", [split_a("split", "scaled", G[:, :], XSa, F)])
            run("l0", [copy("l0", "g_turned", "gT", flat(tT), pT),
                       copy("l0", "negative", "exped", G2[:, :], U[:, :], ACT.Exp),
                       copy("l0", "x_turned", "xT", flat(tT2), pT2),
                       split_a("l0", "scaled", G[:, 0:HC], XSb, HC)])
            run("l1", [copy("l1", "g_turned", "gT", tT[:, 0, :], pT[:, 0:P], ACT.Relu, bias=col["conv"][:, :]),
                       copy("l1", "lin", "zT", G2[0:HL, 0:P], pD[0:HL, 0:P], ACT.Identity, bias=col["lin"][0:HL, :]),
                       copy("l1", "dec", "dT", tT[:, 1, :], pE[:, 0:P], ACT.Relu, bias=col["dec1"][:, :]),
                       copy("l1", "x_turned", "xT", flat(tT2), pT2),
                       split_a("l1", "proj", pD2, XSa, F)])
            run("h1a", [split_a("h1a", "sum_read", G[:, :], XSb, F)])
            run("h1b", [copy("h1b", "g_turned", "gT", flat(tT), pT),
                        split_a("h1b", "proj", pD2, XSa, F)])
            run("h2a", [split_a("h2a", "sum_read", G[:, :], XSb, F)])
            run("h2b", [split_a("h2b", "scaled", G2[:, :], XSa, F)])
            run("l3", [copy("l3", "x_turned", "xT", flat(tT2), pT2),
                       copy("l3", "g_turned", "gT", flat(tT), pT),
                       copy("l3", "x4_turned", "x4T", flat(tT), pT)])
            act_moe(e)

        @block.vector
        def _(e):
            st = Steps(e, S("dve_setup"))
            st.done(e.memset(src_rows_i, FAR))
            st.done(e.memset(dst_rows_i, FAR))
            e.memset(zrow[:, :], 0.0)
            e.memset(mhalf[:, :], -0.5)
            e.memset(ones[:, :], 1.0)
            e.memset(onesB[:, :], 1.0)
            e.memset(outdeg[:, :], 0.0)
            e.memset(X4[:, :, :], 0.0).then_inc(S("zeros_set"), 1)
            st.done(e.memset(X[:, T - 1, :], 0.0))
            e.sem_inc(S("pads_set"), 3)
            e.wait_ge(S("edges_loaded"), 1)
            e.tensor_copy(src_rows, src_rows_i).then_inc(S("rows_float"), 1)
            e.tensor_copy(dst_rows, dst_rows_i).then_inc(S("rows_float"), 1)
            e.wait_ge(S("rows_float"), 2)
            phase_end(e, "load")
            ends = scr1[:, 0:2 * EG]
            d3 = dst_rows.rearrange("c (g e) -> c g e", g=EG)
            st.done(e.tensor_reduce(ends[:, 0:EG], d3, AX.X, ALU.min))
            st.done(e.tensor_reduce(ends[:, EG:2 * EG], d3, AX.X, ALU.max))
            e.tensor_copy(chunk_lo.rearrange("p (g b) -> p g b", g=EG),
                          ends[:, 0:EG].unsqueeze(2).to_broadcast([P, EG, 32])).then_inc(S("chunk_ends"), 1)
            e.tensor_copy(chunk_hi.rearrange("p (g b) -> p g b", g=EG),
                          ends[:, EG:2 * EG].unsqueeze(2).to_broadcast([P, EG, 32])).then_inc(S("chunk_ends"), 1)
            e.wait_ge(S("edges_turned"), 1)
            st.done(e.tensor_scalar(scol, psum[:, 0, 0:EG * P], float(-MID), None, ALU.add))
            st.done(e.tensor_scalar(dcol, psum[:, 1, 0:EG * P], float(P), None, ALU.add))
            e.wait_ge(S("chunk_rows"), 1)
            e.wait_ge(S("iotas_set"), 4)
            e.wait_ge(S("chunk_ends"), 2)
            B = slice(0, 32)
            st.done(e.tensor_scalar(in_band[B, :], psum[B, 2, :], bandcol[B, 3:4], None, ALU.is_le))
            st.done(e.scalar_tensor_tensor(in_band[B, :], psum[B, 3, :], bandcol[B, 2:3], in_band[B, :],
                                           ALU.is_ge, ALU.mult))
            BIG = float(EG * P)
            st.done(e.scalar_tensor_tensor(scr1[B, :], chunk_id[B, :], 1.0, in_band[B, :], ALU.add, ALU.mult))
            st.done(e.tensor_reduce(bandcol[B, 5:6], scr1[B, :], AX.X, ALU.max))
            st.done(e.scalar_tensor_tensor(scr1[B, :], chunk_id[B, :], -BIG, in_band[B, :], ALU.add, ALU.mult))
            st.done(e.tensor_reduce(bandcol[B, 4:5], scr1[B, :], AX.X, ALU.min))
            e.tensor_scalar(bandcol[B, 0:1], bandcol[B, 4:5], BIG, float(EC - 1), ALU.add, ALU.min)\
                .then_inc(S("band_cols_ready"), 1)
            e.wait_ge(S("band_cols_ready"), 1)
            st.done(e.tensor_scalar(bandcol[B, 6:7], bandcol[B, 0:1], 1.0, None, ALU.add))
            e.tensor_tensor(bandcol[B, 1:2], bandcol[B, 5:6], bandcol[B, 6:7], ALU.max)\
                .then_inc(S("band_cols_ready"), 1)
            e.wait_ge(S("band_rows_up"), 1)
            br = bandrow[0:1, :]
            st.done(e.tensor_copy(br[:, 0:64], psum[0:1, 4, 0:64]))
            st.done(e.tensor_tensor(scr1[0:1, 0:32], br[:, 32:64], br[:, 0:32], ALU.subtract))
            st.done(e.memset(br[:, 96:128], 1.0))
            st.done(e.tensor_tensor_scan(br[:, 64:96], br[:, 96:128], scr1[0:1, 0:32], 0.0, ALU.mult, ALU.add))
            st.done(e.tensor_tensor(br[:, 32:64], br[:, 64:96], scr1[0:1, 0:32], ALU.subtract))
            st.done(e.tensor_copy(tab[:, :, :].rearrange("a k b -> a (k b)"), br[:, 0:96]))
            phase_end(e, "table")

            with e.Fori(0, T) as b:
                first = e.value_load(tab[0:1, 0, bass.ds(b, 1)], min_val=0, max_val=EC - 1)
                before = e.value_load(tab[0:1, 1, bass.ds(b, 1)], min_val=0, max_val=T * EC)
                upto = e.value_load(tab[0:1, 2, bass.ds(b, 1)], min_val=1, max_val=T * EC)
                e.tensor_scalar(dcol, dcol, float(-P), None, ALU.add).then_inc(S("band_shifted"), 1)
                e.wait_ge(S("band_shifted"), b + 1)
                carry_wait(e)
                with e.Fori(before, upto) as k:
                    c = nc.s_assert_within(first + k - before, 0, EC - 1,
                                           skip_runtime_bounds_check_because="k runs from before to upto")
                    e.wait_ge(S("onehots_used"), k + 1)
                    e.tensor_scalar(both_d[:, bass.ds(k % 2, 1), :].rearrange("p a c -> p (a c)"), iota_p,
                                    dcol[:, bass.ds(c, 1)], None, ALU.is_equal).then_inc(S("onehots_ready"), 1)
                    e.tensor_scalar(both_s[:, bass.ds(k % 2, 1), :].rearrange("p a c -> p (a c)"), iota_s,
                                    scol[:, bass.ds(c, 1)], None, ALU.is_equal).then_inc(S("onehots_ready"), 1)
                e.wait_ge(S("band_transposed"), NB * (b + 1))
                e.tensor_copy(indeg[:, bass.ds(b, 1)], psum[:, 7, 0:1])
                e.tensor_tensor(outdeg[:, :], outdeg[:, :], psum[:, 7, 32:32 + T], ALU.add)\
                    .then_inc(S("degrees_read"), 1)
                e.wait_ge(S("degrees_read"), b + 1)
            st.done(e.tensor_scalar(nsrc[:, :], outdeg[:, :], 1.0, None, ALU.max))
            st.done(e.tensor_scalar(ndst[:, :], indeg[:, :], 1.0, None, ALU.max))
            st.done(e.tensor_scalar(dis[:, :], indeg[:, :], 1.0, None, ALU.add))
            st.done(e.reciprocal(dinv[:, :], nsrc[:, :]))
            st.done(e.reciprocal(binv[:, :], ndst[:, :]))
            st.done(e.scalar_tensor_tensor(dinv[:, :], outdeg[:, :], 0.5, dinv[:, :], ALU.is_ge, ALU.mult))
            st.done(e.scalar_tensor_tensor(binv[:, :], indeg[:, :], 0.5, binv[:, :], ALU.is_ge, ALU.mult))
            e.sem_inc(S("inverses_made"), 1)
            e.wait_ge(S("norms_ready"), 3)
            phase_end(e, "counts")

            def row(buf, i):
                return buf[:, bass.ds(i, 1), :].rearrange("p a f -> p (a f)")

            def tcol(buf, i):
                return buf[:, bass.ds(i, 1)]

            def split_v(ph, a, XS, w, i):
                e.wait_ge(S("tile_part0"), past(ph, "part0") + i + 1)
                e.tensor_tensor(R1[:, 0:w], a, XS[:, bass.ds(i, 1), 0, 0:w].rearrange("p a f -> p (a f)"),
                                ALU.subtract).then_inc(S("tile_rest"), 1)
                e.wait_ge(S("tile_part1"), past(ph, "part1") + i + 1)
                e.tensor_tensor(XS[:, bass.ds(i, 1), 2, 0:w].rearrange("p a f -> p (a f)"), R1[:, 0:w],
                                XS[:, bass.ds(i, 1), 1, 0:w].rearrange("p a f -> p (a f)"), ALU.subtract)\
                    .then_inc(S("tile_part2"), 1)

            def read_sum(ph, i, par, w, scale, o=None):
                e.wait_ge(S("tile_summed"), past(ph, "summed") + i + 1)
                e.tensor_scalar((G if o is None else o)[:, 0:w], agg[par][:, 0:w], tcol(scale, i), None, ALU.mult)\
                    .then_inc(S("tile_sum_read"), 1)
                e.wait_ge(S("tile_sum_read"), past(ph, "sum_read") + i + 1)

            def layernorm(ph, st, i, a, o):
                st.done(e.bn_stats(st6[:, :], a))
                carry_wait(e)
                e.bn_aggr(mv[:, :], st6[:, :]).then_inc(S("tile_moments"), 1)
                e.wait_ge(S("tile_moments"), past(ph, "moments") + i + 1)
                e.wait_ge(S("tile_rstd"), past(ph, "rstd") + i + 1)
                e.wait_ge(S("tile_x_kept"), past(ph, "x_kept") + i)
                e.tensor_scalar(o, a, mv[:, 0:1], rstd[:, 0:1], ALU.subtract, ALU.mult)\
                    .then_inc(S("tile_normed"), 1)
                e.wait_ge(S("tile_normed"), past(ph, "normed") + i + 1)

            def prelu(st, o, a, tmp):
                st.done(e.tensor_scalar(tmp, a, 0.0, col["a"][:, 0:1], ALU.min, ALU.mult))
                return e.scalar_tensor_tensor(o, a, 0.0, tmp, ALU.max, ALU.add)

            def split_body(i, par):
                e.tensor_scalar(G[:, :], row(X, i), tcol(nsrc, i), None, ALU.mult)\
                    .then_inc(S("tile_scaled"), 1)
                e.wait_ge(S("tile_scaled"), past("split", "scaled") + i + 1)
                split_v("split", G[:, :], XSa, F, i)
            tiles(e, split_body)
            phase_end(e, "split")

            st0 = Steps(e, S("steps_l0"), 4)

            def l0(i, par):
                st0.tile(i)
                read_sum("l0", i, par, F, ndst)
                e.wait_ge(S("tile_pre"), past("l0", "pre") + i + 1)
                st0.done(e.tensor_tensor(V[:, :], pD, bc["l0"][:, :], ALU.add))
                e.tensor_scalar(U[:, :], V[:, :], 0.0, None, ALU.min).then_inc(S("tile_negative"), 1)
                st0.done(e.scalar_tensor_tensor(R1[:, :], V[:, :], 0.0, row(X, i), ALU.max, ALU.add))
                e.wait_ge(S("tile_exped"), past("l0", "exped") + i + 1)
                st0.done(e.scalar_tensor_tensor(V[:, :], G2[:, :], -1.0, R1[:, :], ALU.add, ALU.add))
                layernorm("l0", st0, i, V[:, :], Xn[:, :])
                e.wait_ge(S("tile_proj"), past("l0", "proj") + i + 1)
                e.tensor_scalar(G[:, 0:HC], pD2[:, 0:HC], tcol(dis, i), None, ALU.mult)\
                    .then_inc(S("tile_scaled"), 1)
                e.wait_ge(S("tile_scaled"), past("l0", "scaled") + i + 1)
                split_v("l0", G[:, 0:HC], XSb, HC, i)
            tiles(e, l0)
            phase_end(e, "l0")

            st1 = Steps(e, S("steps_l1"), 3)

            def l1(i, par):
                st1.tile(i)
                read_sum("l1", i, par, HC, dis)
                e.wait_ge(S("tile_pre"), past("l1", "pre") + i + 1)
                st1.done(e.tensor_tensor(V[:, :], pF, bc["dec2"][:, :], ALU.add))
                st1.done(e.tensor_tensor(V[:, :], V[:, :], row(X, i), ALU.add))
                layernorm("l1", st1, i, V[:, :], Xn[:, :])
                split_v("l1", pD2, XSa, F, i)
            tiles(e, l1)
            phase_end(e, "l1")

            def hyperedge(ph):
                def body(i, par):
                    read_sum(ph, i, par, F, binv)
                    split_v(ph, G[:, :], XSb, F, i)
                tiles(e, body)
                phase_end(e, ph)

            hyperedge("h1a")
            st2 = Steps(e, S("steps_h1b"), 2)

            def h1b(i, par):
                st2.tile(i)
                read_sum("h1b", i, par, F, dinv, V)
                st2.done(e.tensor_tensor(V[:, :], V[:, :], bc["h1"][:, :], ALU.add))
                prelu(st2, G[:, :], V[:, :], U[:, :]).then_inc(S("tile_active"), 1)
                split_v("h1b", pD2, XSa, F, i)
            tiles(e, h1b)
            phase_end(e, "h1b")
            hyperedge("h2a")
            st3 = Steps(e, S("steps_h2b"), 6)

            def h2b(i, par):
                st3.tile(i)
                read_sum("h2b", i, par, F, dinv)
                st3.done(e.tensor_tensor(V[:, :], G[:, :], bc["h2"][:, :], ALU.add))
                st3.done(e.tensor_tensor(V[:, :], V[:, :], row(X, i), ALU.add))
                st3.done(prelu(st3, V[:, :], V[:, :], U[:, :]))
                st3.done(e.tensor_tensor(V[:, :], V[:, :], row(X, i), ALU.add))
                layernorm("h2b", st3, i, V[:, :], Xn[:, :])
                e.tensor_scalar(G2[:, :], Xn[:, :], tcol(nsrc, i), None, ALU.mult).then_inc(S("tile_scaled"), 1)
                e.wait_ge(S("tile_scaled"), past("h2b", "scaled") + i + 1)
                split_v("h2b", G2[:, :], XSa, F, i)
            tiles(e, h2b)
            phase_end(e, "h2b")

            st.done(e.tensor_tensor(bc["gc"][:, :], bc["gc"][:, :], bc["res"][:, :], ALU.add))
            st4 = Steps(e, S("steps_l3"), 3)

            def l3(i, par):
                st4.tile(i)
                read_sum("l3", i, par, F, ndst)
                e.wait_ge(S("tile_pre"), past("l3", "pre") + i + 1)
                e.wait_ge(S("tile_x4_kept"), past("l3", "x4_kept") + i)
                e.tensor_tensor(V[:, :], pD, bc["gc"][:, :], ALU.add).then_inc(S("tile_x4_made"), 1)
                e.wait_ge(S("tile_logits"), past("l3", "logits") + i + 1)
                st4.done(e.tensor_tensor(U[:, 0:NE], pD2[:, 0:NE], bgb[:, :], ALU.add))
                carry_wait(e)
                st4.done(e.max(max8[:, :], U[:, 0:NE]))
                carry_wait(e)
                st4.done(e.max_index(idx8[:, :], max8[:, :], U[:, 0:NE]))
                e.tensor_copy(row(top_val, i), max8[:, 0:TOP])
                e.tensor_copy(row(top_idx, i), idx8[:, 0:TOP]).then_inc(S("tile_top"), 1)
                e.wait_ge(S("tile_top"), past("l3", "top") + i + 1)
            tiles(e, l3)
            dve_moe(e)

        @block.gpsimd
        def _(e):
            e.memset(identF[:, :], 0.0).then_inc(S("pool_cleared"), 1)
            e.memset(identB[:, :], 0.0).then_inc(S("pool_cleared"), 1)
            e.wait_ge(S("pool_cleared"), 2)
            for m in (identF, identB):
                e.affine_select(out=m[:, :], in_=m[:, :], compare_op=ALU.not_equal, fill=1.0, base=0,
                                pattern=[[-1, P]], channel_multiplier=1).then_inc(S("ident_set"), 1)
            e.iota(iota_s, [[1, NP]], base=-MID, channel_multiplier=0, allow_small_or_imprecise_dtypes=True)\
                .then_inc(S("iotas_set"), 1)
            e.iota(iota_p, [[1, P]], base=0, channel_multiplier=0, allow_small_or_imprecise_dtypes=True)\
                .then_inc(S("iotas_set"), 1)
            e.iota(chunk_id, [[1, EG * P]], base=0, channel_multiplier=0, allow_small_or_imprecise_dtypes=True)\
                .then_inc(S("iotas_set"), 1)
            e.iota(bandcol[:, 2:4], [[P - 1, 2]], base=0, channel_multiplier=P,
                   allow_small_or_imprecise_dtypes=True).then_inc(S("iotas_set"), 1)
            for m in (tri, vmask):
                e.memset(m[:, :], 1.0).then_inc(S("masks_set"), 1)
            e.memset(valid[:, :], 1.0).then_inc(S("masks_set"), 1)
            e.wait_ge(S("masks_set"), 3)
            e.affine_select(out=tri[:, :], in_=tri[:, :], compare_op=ALU.is_gt, fill=0.0, base=0,
                            pattern=[[1, P]], channel_multiplier=-1).then_inc(S("masks_set"), 1)
            e.affine_select(out=vmask[:, :], in_=vmask[:, :], compare_op=ALU.is_ge, fill=0.0, base=LAST - 1,
                            pattern=[[0, P]], channel_multiplier=-1).then_inc(S("masks_set"), 1)
            e.affine_select(out=valid[:, :], in_=valid[:, :], compare_op=ALU.is_ge, fill=0.0, base=N - 1,
                            pattern=[[-P, T]], channel_multiplier=-1).then_inc(S("masks_set"), 1)
            e.iota(iota_e[:, :], [[1, NE]], base=0, channel_multiplier=0, allow_small_or_imprecise_dtypes=True)\
                .then_inc(S("masks_set"), 1)
            e.iota(trash[:, :, :], [[NP, TOP], [P, T]], base=TRASH, channel_multiplier=1,
                   allow_small_or_imprecise_dtypes=True).then_inc(S("masks_set"), 1)
            e.iota(pcol[:, :], [[0, 1]], base=0, channel_multiplier=1, allow_small_or_imprecise_dtypes=True)\
                .then_inc(S("masks_set"), 1)
            e.wait_ge(S("iotas_set"), 4)
            e.wait_ge(S("masks_set"), 9)
            phase_end(e, "load")
            phase_end(e, "table")
            e.sem_inc(S("onehots_used"), 2)
            e.wait_ge(S("inverses_made"), 1)
            for n in (nsrc, ndst, dis):
                e.tensor_tensor(n[:, :], n[:, :], mhalf[:, :], ALU.pow).then_inc(S("norms_ready"), 1)
            e.wait_ge(S("norms_ready"), 3)
            phase_end(e, "counts")
            phase_end(e, "split")

            def norm_tile(ph, body_copy=True):
                def body(i, par):
                    e.wait_ge(S("tile_moments"), past(ph, "moments") + i + 1)
                    carry_wait(e)
                    e.tensor_scalar(ve[:, :], mv[:, 1:2], EPS, None, ALU.add).then_inc(S("tile_eps"), 1)
                    e.wait_ge(S("tile_eps"), past(ph, "eps") + i + 1)
                    e.tensor_tensor(rstd[:, :], ve[:, :], mhalf[:, 0:1], ALU.pow).then_inc(S("tile_rstd"), 1)
                    e.wait_ge(S("tile_normed"), past(ph, "normed") + i + 1)
                    e.tensor_copy(X[:, bass.ds(i, 1), :].rearrange("p a f -> p (a f)"), Xn[:, :])\
                        .then_inc(S("tile_x_kept"), 1)
                tiles(e, body)
                e.wait_ge(S("tile_x_kept"), past(ph, "x_kept") + T)
                phase_end(e, ph)

            norm_tile("l0")
            norm_tile("l1")
            phase_end(e, "h1a")
            phase_end(e, "h1b")
            phase_end(e, "h2a")
            norm_tile("h2b")

            def l3(i, par):
                e.wait_ge(S("tile_x_turned"), past("l3", "x_turned") + i)
                e.tensor_copy(Xn[:, :], X[:, bass.ds(i, 1), :].rearrange("p a f -> p (a f)"))\
                    .then_inc(S("tile_own_copied"), 1)
                e.wait_ge(S("tile_x4_made"), past("l3", "x4_made") + i + 1)
                e.tensor_copy(X4[:, bass.ds(i, 1), :].rearrange("p a f -> p (a f)"), V[:, :])\
                    .then_inc(S("tile_x4_kept"), 1)
            tiles(e, l3)
            e.wait_ge(S("tile_x4_kept"), past("l3", "x4_kept") + T)
            pool_moe(e)


_INS = ["x", "src", "dst", "L0_gnn_weight", "L0_gnn_bias", "L1_gnn_W_conv", "L1_gnn_b_conv", "L1_gnn_W_lin",
        "L1_gnn_b_lin", "L1_gnn_W_dec1", "L1_gnn_b_dec1", "L1_gnn_W_dec2", "L1_gnn_b_dec2", "L2_gnn_W1", "L2_gnn_b1",
        "L2_gnn_W2", "L2_gnn_b2", "L2_gnn_a", "L3_gnn_W_gc", "L3_gnn_b_gc", "L3_gnn_W_res", "L3_gnn_b_res",
        "L3_gnn_Wg", "L3_gnn_bg", "L3_gnn_w1", "L3_gnn_b1", "L3_gnn_w2", "L3_gnn_b2", "L3_gnn_gamma", "L3_gnn_beta"]


def kernel(**inputs):
    import numpy as _np
    import concourse.bacc as _bacc
    from concourse import mybir as _mybir
    from concourse.bass_utils import run_bass_kernel_spmd as _run

    nc = _bacc.Bacc("TRN2", target_bir_lowering=False, num_devices=1)
    arrays, args = {}, {}
    for name in _INS:
        a = _np.ascontiguousarray(inputs[name])
        arrays[f"in_{name}"] = a
        args[name] = nc.dram_tensor(f"in_{name}", a.shape, _mybir.dt.from_np(a.dtype), kind="ExternalInput").ap()
    out = nc.dram_tensor("out", arrays["in_x"].shape, F32, kind="ExternalOutput").ap()
    gnn_program(nc, args, out)
    return _run(nc, [arrays], core_ids=[0]).results[0]["out"]
```

```python
from contextlib import ExitStack

import concourse.bass as bass
from concourse import mybir

ALU = mybir.AluOpType
ACT = mybir.ActivationFunctionType
AX = mybir.AxisListType
F32 = mybir.dt.float32
BF16 = mybir.dt.bfloat16
F16 = mybir.dt.float16
I32 = mybir.dt.int32
U32 = mybir.dt.uint32

P = 128
TOP = 2
CAP = 1024
EPS = 1e-05
FAR = 8191
RING = 4


class Steps:

    def __init__(self, eng, sem, per_tile=0):
        self.eng, self.sem, self.per_tile, self.base, self.n = eng, sem, per_tile, 0, 0

    def tile(self, i):
        assert self.n in (0, self.per_tile), (self.n, self.per_tile)
        self.base, self.n = i * self.per_tile, 0

    def done(self, ins):
        self.n += 1
        ins.then_inc(self.sem, 1)
        self.eng.wait_ge(self.sem, self.base + self.n)


def gnn_program(nc, A, out):
    x, src, dst = A["x"], A["src"], A["dst"]
    N, F = x.shape
    E = src.shape[0]
    T = (N + P - 1) // P
    NP = T * P
    LAST = N - (T - 1) * P
    EC = (E + P - 1) // P
    EG = (EC + P - 1) // P
    HC = A["L1_gnn_W_conv"].shape[1]
    HL = A["L1_gnn_W_lin"].shape[1]
    NE, _, H = A["L3_gnn_w1"].shape
    HT = H // P
    KF = F // P
    PARTS = 3
    BANK = 512
    NB = (NP + BANK - 1) // BANK
    TPB = BANK // P
    MID = NP // 2
    MAXCH = TOP * N // P + NE
    MAXCH = -(-MAXCH // RING) * RING
    ZROWS = 20
    NCH = -(-(MAXCH + RING) // ZROWS) * ZROWS
    TRASH = NCH * P
    assert T % 2 == 1 and NCH <= P and F == 256 and HC == P

    a_fwd = nc.dram_tensor("counts_src_on_rows", (T, P, T * P), BF16, kind="Internal").ap()
    a_rev = nc.dram_tensor("counts_dst_on_rows", (T, P, T * P), BF16, kind="Internal").ap()
    xbuf = nc.dram_tensor("expert_rows_in", (TRASH + TOP * NP, F), F32, kind="Internal").ap()
    ybuf = nc.dram_tensor("expert_rows_out", (TRASH, F), F32, kind="Internal").ap()

    with ExitStack() as ctx:
        def sb(name, shape, dt=F32):
            return ctx.enter_context(nc.sbuf_tensor(name, shape, dt))

        sems = {}

        def S(name):
            if name not in sems:
                sems[name] = ctx.enter_context(nc.semaphore(name))
            return sems[name]

        X = sb("X", [P, T, F])
        X4 = sb("X4", [P, T, F])
        xsa = sb("xsa", [P, T * PARTS * F], BF16)
        xsb = sb("xsb", [P, T * PARTS * F], BF16)
        XSa = xsa[:, :].rearrange("p (t s f) -> p t s f", t=T, s=PARTS)
        XSb = xsb[:, :].rearrange("p (t s f) -> p t s f", t=T, s=PARTS)
        blk = [sb(f"blk{n}", [P, T * P], BF16) for n in range(2)]
        identF = sb("identF", [P, P])
        identB = sb("identB", [P, P], BF16)
        zrow = sb("zrow", [P, BANK], BF16)
        ones = sb("ones", [P, P])
        onesB = sb("onesB", [P, 1], BF16)
        wl0 = sb("wl0", [P, KF, F])
        wcv = sb("wcv", [P, KF, HC])
        wln = sb("wln", [P, HL])
        wd1 = sb("wd1", [HL, HC])
        wd2 = sb("wd2", [P, F])
        wh1 = sb("wh1", [P, KF, F])
        wh2 = sb("wh2", [P, KF, F])
        wgc = sb("wgc", [P, KF, F])
        wrs = sb("wrs", [P, KF, F])
        wgt = sb("wgt", [P, KF, NE])
        bc = {k: sb("bc_" + k, [P, F]) for k in ("l0", "dec2", "h1", "h2", "gc", "res", "gam", "bet")}
        bgb = sb("bgb", [P, NE])
        col = {k: sb("col_" + k, [P, 1]) for k in ("conv", "lin", "dec1", "a")}
        b1T = sb("b1T", [P, HT, NE])
        outdeg = sb("outdeg", [P, T])
        indeg = sb("indeg", [P, T])
        nsrc = sb("nsrc", [P, T])
        ndst = sb("ndst", [P, T])
        dis = sb("dis", [P, T])
        dinv = sb("dinv", [P, T])
        binv = sb("binv", [P, T])
        mhalf = sb("mhalf", [P, T])
        tab = sb("tab", [1, 3, 32], I32)
        G = sb("G", [P, F])
        G2 = sb("G2", [P, F])
        V = sb("V", [P, F])
        R1 = sb("R1", [P, F])
        U = sb("U", [P, F])
        Xn = [sb(f"Xn{n}", [P, F])[:, :] for n in range(2)]
        V2 = sb("V2", [P, F])
        R2 = sb("R2", [P, F])
        tT = sb("tT", [P, KF, P])
        tT2 = sb("tT2", [P, KF, P])
        tT3 = sb("tT3", [P, KF, P])
        st6 = sb("st6", [P, 6])
        mv = sb("mv", [P, 2])
        ve = sb("ve", [P, 1])
        rstd = sb("rstd", [P, 1])
        max8 = sb("max8", [P, 8])
        idx8 = sb("idx8", [P, 8], U32)

        def view(buf, at, n, dt):
            w = 2 if dt in (F32, I32, U32) else 1
            v = buf[:, at:at + n * w]
            return (v if dt == BF16 else v.bitcast(dt)), at + n * w

        at = 0
        iota_s, at = view(xsb, at, NP, F16)
        iota_p, at = view(xsb, at, P, F16)
        src_rows_i, at = view(xsb, at, EG * P, I32)
        dst_rows_i, at = view(xsb, at, EG * P, I32)
        src_rows, at = view(xsb, at, EG * P, F32)
        dst_rows, at = view(xsb, at, EG * P, F32)
        chunk_lo, at = view(xsb, at, EG * 32, F32)
        chunk_hi, at = view(xsb, at, EG * 32, F32)
        chunk_id, at = view(xsb, at, EG * P, F32)
        in_band, at = view(xsb, at, EG * P, F32)
        scr1, at = view(xsb, at, EG * P, F32)
        bandcol, at = view(xsb, at, 8, F32)
        bandrow, at = view(xsb, at, 4 * 32, F32)
        assert at <= T * PARTS * F
        at = 0
        one_s = [None, None]
        one_s[0], at = view(xsa, at, NP, BF16)
        one_s[1], at = view(xsa, at, NP, BF16)
        both_s = xsa[:, 0:2 * NP].rearrange("p (b s) -> p b s", b=2)
        band_rows, at = view(xsa, at, NP, BF16)
        band_cols, at = view(xsa, at, NP, BF16)
        dcol, at = view(xsa, at, EG * P, F32)
        scol, at = view(xsa, at, EG * P, F32)
        both_d, at = view(xsa, at, 2 * P, BF16)
        both_d = both_d.rearrange("p (b s) -> p b s", b=2)
        assert at <= T * PARTS * F

        b1rows = sb("b1rows", [NE, H])
        tri = sb("tri", [P, P])
        vmask = sb("vmask", [P, P])
        iota_e = sb("iota_e", [P, NE])
        valid = sb("valid", [P, T])
        trash = sb("trash", [P, TOP, T])
        pcol = sb("pcol", [P, 1])
        etab = sb("etab", [1, P], I32)
        nturn = sb("nturn", [1, 1], I32)
        gate = sb("gate", [P, TOP, T])
        slot_to = sb("slot_to", [P, TOP, T], U32)
        slot_from = sb("slot_from", [P, TOP, T], U32)

        def cut(buf, at, shape, dt=F32):
            n = 1
            for s_ in shape:
                n *= s_
            v, at = view(buf, at, n, dt)
            if len(shape) == 2:
                v = v.rearrange("p (a b) -> p a b", a=shape[0])
            return v, at

        at = 0
        top_val, at = cut(xsb, at, (T, TOP))
        top_idx, at = cut(xsb, at, (T, TOP), U32)
        idxf, at = cut(xsb, at, (T, TOP))
        gap, at = cut(xsb, at, (T,))
        OH1, at = cut(xsb, at, (T, NE))
        OH2, at = cut(xsb, at, (T, NE))
        M, at = cut(xsb, at, (T, NE))
        CS, at = cut(xsb, at, (T, NE))
        rk, at = cut(xsb, at, (TOP, T))
        slot, at = cut(xsb, at, (TOP, T))
        keep, at = cut(xsb, at, (TOP, T))
        ecnt, at = cut(xsb, at, (NE,))
        eint, at = cut(xsb, at, (NE,), I32)
        eincl, at = cut(xsb, at, (NE,))
        ebase, at = cut(xsb, at, (NE,))
        ecol, at = cut(xsb, at, (2,))
        assert at <= T * PARTS * F
        SQ, at = cut(xsb, 0, (T, F))
        at = 0
        RNK, at = cut(xsa, at, (T, NE))
        assert at <= T * PARTS * F
        w1s, w2s, xin, xTs, hTs, yout, b2s, ring = ([] for _ in range(8))
        for base, lot in ((xsa, ((w1s, (KF, H), RING), (w2s, (HT, F), RING))),
                          (xsb, ((xin, (F,), RING), (yout, (F,), RING), (b2s, (F,), RING), (xTs, (F,), 2),
                                 (hTs, (HT, P), 2)))):
            at = 0
            for bufs, shape, n in lot:
                for _ in range(n):
                    v, at = cut(base, at, shape)
                    bufs.append(v)
            assert at <= T * PARTS * F
        for n in range(4):
            v, _ = cut(xsa, 2 * n * TOP * F, (TOP, F))
            ring.append(v)

        psum = ctx.enter_context(nc.psum_tensor("psum", [P, 8, BANK], F32))
        agg = [psum[:, 0, 0:F], psum[:, 1, 0:F]]
        pT, pT2 = psum[:, 2, 0:F], psum[:, 3, 0:F]
        pD, pD2 = [psum[:, 4, 0:F], psum[:, 5, 0:F]], [psum[:, 6, 0:F], psum[:, 7, 0:F]]
        plin, pdec, px4 = psum[0:HL, 5, 0:P], psum[:, 5, P:2 * P], psum[:, 5, 0:F]

        block = ctx.enter_context(nc.Block())
        PHASES = ["load", "table", "counts", "split", "l0", "l1", "h1a", "h1b", "h2a", "h2b", "l3", "route", "experts",
                  "combine"]

        def phase_end(e, name):
            e.drain().then_inc(S("phases_ended"), 1)
            e.wait_ge(S("phases_ended"), 5 * (PHASES.index(name) + 1))

        SIGNALS = {
            "scaled": ["split", "l0", "h2b"], "part0": ["split", "l0", "l1", "h1a", "h1b", "h2a", "h2b"],
            "summed": ["l0", "l1", "h1a", "h1b", "h2a", "h2b", "l3"],
            "g_turned": ["l0", "l1", "h1b", "l3"], "pre": ["l0", "l1", "l3"], "x_turned": ["l0", "l1", "l3"],
            "proj": ["l0", "l1", "h1b"], "lin": ["l1"], "dec": ["l1"], "zT": ["l1"], "dT": ["l1"],
            "normed": ["l0", "l1", "h2b"], "negative": ["l0"], "exped": ["l0"], "active": ["h1b"],
            "own_copied": ["l3"], "x4_made": ["l3"], "x4_turned": ["l3"], "x4T": ["l3"], "logits": ["l3"],
            "x4_kept": ["l3"], "top": ["l3"]}
        SIGNALS["rest"] = SIGNALS["part1"] = SIGNALS["part2"] = SIGNALS["part0"]
        SIGNALS["sum_read"] = SIGNALS["summed"]
        SIGNALS["gT"], SIGNALS["xT"] = SIGNALS["g_turned"], SIGNALS["x_turned"]
        SIGNALS["moments"] = SIGNALS["eps"] = SIGNALS["rstd"] = SIGNALS["x_kept"] = SIGNALS["normed"]

        def past(ph, name):
            return T * SIGNALS[name].index(ph)

        def past_blocks(ph, par):
            return (T // 2 + (1 - par)) * SIGNALS["summed"].index(ph)

        def carry_wait(e):
            e.sem_inc(S("waits_carried"), 1)

        def tiles(e, body):
            pipeline(e, [(0, body)])

        def pipeline(e, stages, whole=None):
            depth = max(lag for lag, _ in stages)

            def turn(it, par, known):
                todo = [(lambda f=f, lag=lag: f(it(lag), (par + lag) % 2)) for lag, f in stages
                        if not known or 0 <= it(lag) < T]
                if whole is None:
                    for f in todo:
                        f()
                else:
                    whole(it, par, todo, known)

            pairs = (T - depth) // 2
            for n in range(depth):
                turn(lambda lag, n=n: n - lag, n % 2, True)
            with e.Fori(0, pairs) as j:
                for u in range(2):
                    turn(lambda lag, u=u: 2 * j + (depth + u - lag), (depth + u) % 2, False)
            for n in range(depth + 2 * pairs, T + depth):
                turn(lambda lag, n=n: n - lag, n % 2, True)

        def at_tile(buf, i):
            return buf[:, bass.ds(i, 1)]

        def sync_moe(e):
            phase_end(e, "route")

            def expert_of(c):
                return e.value_load(etab[0:1, bass.ds(c, 1)], min_val=0, max_val=NE - 1)

            def load_rows(c, n):
                e.dma_start(xin[n], xbuf[bass.ds(c * P, P), :]).then_inc(S(f"rows_in{n}"), 16)

            def load_w1(ex, n):
                e.dma_start(w1s[n], A["L3_gnn_w1"][bass.ds(ex, 1), :, :].rearrange("a (k p) h -> p (a k) h", p=P))\
                    .then_inc(S(f"w1_in{n}"), 16)

            def load_w2(ex, n):
                e.dma_start(w2s[n], A["L3_gnn_w2"][bass.ds(ex, 1), :, :].rearrange("a (k p) f -> p (a k) f", p=P))\
                    .then_inc(S(f"w2_in{n}"), 16)
                e.dma_start(b2s[n], A["L3_gnn_b2"][bass.ds(ex, 1), :].to_broadcast([P, F]))\
                    .then_inc(S(f"b2_in{n}"), 16)

            for c in range(RING):
                ex = expert_of(c)
                load_rows(c, c)
                load_w1(ex, c)
                load_w2(ex, c)
            turns = e.value_load(nturn[0:1, 0:1], min_val=1, max_val=MAXCH // RING)
            with e.Fori(0, turns) as j:
                for n in range(RING):
                    c = RING * j + n
                    ex = expert_of(c + RING)
                    e.wait_ge(S("chunk_turned"), c + 1)
                    load_rows(c + RING, n)
                    e.wait_ge(S("hidden_summed"), c + 1)
                    load_w1(ex, n)
                    e.wait_ge(S("chunk_made"), c + 3)
                    load_w2(ex, n)
            for n in range(RING):
                for name in ("rows_in", "w1_in", "w2_in", "b2_in"):
                    e.wait_ge(S(f"{name}{n}"), 16 * turns + 16)
            carry_wait(e)
            phase_end(e, "experts")
            phase_end(e, "combine")
            with e.Fori(0, T - 1) as t:
                e.wait_ge(S("out_made"), t + 1)
                e.dma_start(out[bass.ds(t * P, P), :], X4[:, bass.ds(t, 1), :].rearrange("p a f -> p (a f)"))\
                    .then_inc(S("out_stored"), 16)
            e.wait_ge(S("out_made"), T)
            e.dma_start(out[(T - 1) * P:N, :], X4[0:LAST, T - 1, :]).then_inc(S("out_stored"), 16)
            e.wait_ge(S("out_stored"), 16 * T)

        def pe_moe(e):
            for h in range(HT):
                mm = e.transpose(psum[:, 5, h * NE:(h + 1) * NE], b1rows[:, h * P:(h + 1) * P], identF[0:NE, 0:NE])
            mm.then_inc(S("b1_turned"), 1)
            e.wait_ge(S("running_counts"), 1)
            for t in range(T):
                o = psum[:, t // 8, (t % 8) * NE:(t % 8 + 1) * NE]
                mm = e.matmul(o, tri[:, :], M[:, t, :], start=True, stop=(t == 0))
                if t:
                    mm = e.matmul(o, ones[:, :], CS[:, t - 1, :], start=False, stop=True)
            e.matmul(psum[:, 4, 0:NE], ones[:, :], CS[:, T - 1, :], start=True, stop=True).then_inc(S("ranked"), 1)
            e.wait_ge(S("chunk_experts"), 1)
            e.transpose(psum[0:1, 6, 0:P], ecol[:, 0:1], identF[:, :]).then_inc(S("chunk_experts_up"), 1)
            phase_end(e, "route")

            def turn(c, j, n, par):
                e.wait_ge(S(f"rows_in{n}"), 16 * j + 16)
                for k in range(KF):
                    mm = e.transpose(psum[:, par, k * P:(k + 1) * P], xin[n][:, k * P:(k + 1) * P], identF[:, :])
                mm.then_inc(S("chunk_turned"), 1)

            def hidden(c, j, n, par):
                e.wait_ge(S("chunk_copied"), c + 1)
                e.wait_ge(S(f"w1_in{n}"), 16 * j + 16)
                for h in range(HT):
                    for k in range(KF):
                        mm = e.matmul(psum[:, 2 + par, h * P:(h + 1) * P], w1s[n][:, k, h * P:(h + 1) * P],
                                      xTs[par][:, k * P:(k + 1) * P], start=(k == 0), stop=(k == KF - 1))
                mm.then_inc(S("hidden_summed"), 1)

            def rows_out(c, j, n, par):
                e.wait_ge(S("gelu_made"), c + 1)
                e.wait_ge(S(f"w2_in{n}"), 16 * j + 16)
                e.wait_ge(S("chunk_made"), c + 1)
                for h in range(HT):
                    mm = e.matmul(psum[:, 4 + par, 0:F], hTs[par][:, h, :], w2s[n][:, h, :],
                                  start=(h == 0), stop=(h == HT - 1))
                mm.then_inc(S("chunk_summed"), 1)

            turns = e.value_load(nturn[0:1, 0:1], min_val=1, max_val=MAXCH // RING)
            turn(0, 0, 0, 0)
            turn(1, 0, 1, 1)
            hidden(0, 0, 0, 0)
            with e.Fori(0, turns) as j:
                for n in range(RING):
                    c = RING * j + n
                    par = n % 2
                    e.wait_ge(S("chunk_copied"), c + 1)
                    turn(c + 2, j + (n + 2) // RING, (n + 2) % RING, par)
                    e.wait_ge(S("gelu_made"), c)
                    hidden(c + 1, j + (n + 1) // RING, (n + 1) % RING, 1 - par)
                    rows_out(c, j, n, par)
            phase_end(e, "experts")
            for n in range(2):
                e.matmul(psum[:, n, 0:F], zrow[:, 0:P], zrow[:, 0:F], start=True, stop=True)
            for n, (name, buf) in enumerate((("combined", X4), ("squared", SQ))):
                with e.Fori(0, T - 1) as t:
                    e.wait_ge(S(name), t + 1)
                    r = buf[:, bass.ds(t, 1), :].rearrange("p a f -> p (a f)")
                    e.matmul(psum[:, n, 0:F], ones[:, :], r, start=False, stop=True, skip_group_check=True)
                e.wait_ge(S(name), T)
                e.matmul(psum[:, n, 0:F], vmask[:, :], buf[:, T - 1, :], start=False, stop=True,
                         skip_group_check=True).then_inc(S("bn_summed"), 1)
            phase_end(e, "combine")

        def act_moe(e):
            e.wait_ge(S("top_gap"), 1)
            e.activation(gate[:, 1, :], gap, ACT.Exp).then_inc(S("top_exp"), 1)
            e.wait_ge(S("b1_turned"), 1)
            e.activation(b1T[:, :, :].rearrange("p h x -> p (h x)"), psum[:, 5, 0:HT * NE], ACT.Copy)\
                .then_inc(S("b1_ready"), 1)
            e.wait_ge(S("b1_ready"), 1)
            phase_end(e, "route")

            def gelu(c, par):
                ex = e.value_load(etab[0:1, bass.ds(c, 1)], min_val=0, max_val=NE - 1)
                e.wait_ge(S("hidden_summed"), c + 1)
                for h in range(HT):
                    mm = e.activation(hTs[par][:, h, :], psum[:, 2 + par, h * P:(h + 1) * P], ACT.Gelu,
                                      bias=b1T[:, h, bass.ds(ex, 1)])
                mm.then_inc(S("gelu_made"), 1)

            turns = e.value_load(nturn[0:1, 0:1], min_val=1, max_val=MAXCH // RING)
            gelu(0, 0)
            with e.Fori(0, turns) as j:
                for n in range(RING):
                    c, par = RING * j + n, n % 2
                    e.wait_ge(S("chunk_summed"), c)
                    gelu(c + 1, 1 - par)
            phase_end(e, "experts")

            def square(t, par):
                e.wait_ge(S("centred"), t + 1)
                e.activation(SQ[:, bass.ds(t, 1), :].rearrange("p a f -> p (a f)"),
                             X4[:, bass.ds(t, 1), :].rearrange("p a f -> p (a f)"), ACT.Square)\
                    .then_inc(S("squared"), 1)
            tiles(e, square)
            phase_end(e, "combine")

        def dve_moe(e):
            phase_end(e, "l3")
            st = Steps(e, S("dve_route"))
            e.tensor_tensor(gap, top_val[:, :, 1], top_val[:, :, 0], ALU.subtract).then_inc(S("top_gap"), 1)
            st.done(e.tensor_copy(idxf, top_idx[:, :, 0:TOP]))
            one_hot = (OH1, OH2)
            ex_ids = iota_e[:, :].unsqueeze(1).to_broadcast([P, T, NE])
            alive = valid[:, :].unsqueeze(2).to_broadcast([P, T, NE])
            for k in range(TOP):
                st.done(e.tensor_tensor(one_hot[k], ex_ids, idxf[:, :, k:k + 1].to_broadcast([P, T, NE]),
                                        ALU.is_equal))
                st.done(e.tensor_tensor(one_hot[k], one_hot[k], alive, ALU.mult))
            st.done(e.tensor_tensor(M, OH1, OH2, ALU.add))
            st.done(e.tensor_copy(CS[:, 0, :], M[:, 0, :]))
            for t in range(1, T):
                st.done(e.tensor_tensor(CS[:, t, :], CS[:, t - 1, :], M[:, t, :], ALU.add))
            e.sem_inc(S("running_counts"), 1)
            e.wait_ge(S("ranked"), 1)
            for q in range(4):
                w = min(BANK, T * NE - q * BANK)
                st.done(e.tensor_copy(RNK.rearrange("p t x -> p (t x)")[:, q * BANK:q * BANK + w],
                                      psum[:, q, 0:w]))
            st.done(e.tensor_scalar(ecnt, psum[:, 4, 0:NE], float(CAP), float(P - 1), ALU.min, ALU.add))
            st.done(e.tensor_copy(eint, ecnt))
            st.done(e.tensor_scalar(eint, eint, 7, None, ALU.arith_shift_right))
            st.done(e.tensor_copy(ecnt, eint))
            st.done(e.tensor_tensor_scan(eincl, ones[:, 0:NE], ecnt, 0.0, ALU.mult, ALU.add))
            st.done(e.tensor_tensor(ebase, eincl, ecnt, ALU.subtract))
            st.done(e.tensor_scalar(ecnt, eincl, pcol[:, 0:1], None, ALU.is_le))
            st.done(e.tensor_reduce(ecol[:, 1:2], ecnt, AX.X, ALU.add))
            e.tensor_scalar(ecol[:, 0:1], ecol[:, 1:2], float(NE - 1), None, ALU.min)\
                .then_inc(S("chunk_experts"), 1)
            st.done(e.tensor_scalar(eint[0:1, 0:1], eincl[0:1, NE - 1:NE], float(RING - 1), None, ALU.add))
            st.done(e.tensor_scalar(nturn[0:1, 0:1], eint[0:1, 0:1], RING.bit_length() - 1, None,
                                    ALU.arith_shift_right))
            st.done(e.tensor_scalar(ebase, ebase, float(P), None, ALU.mult))
            first_row = ebase.unsqueeze(1).to_broadcast([P, T, NE])
            for k in range(TOP):
                st.done(e.tensor_tensor(M, one_hot[k], RNK, ALU.mult))
                st.done(e.tensor_reduce(rk[:, k, :], M, AX.X, ALU.add))
                st.done(e.tensor_tensor(M, one_hot[k], first_row, ALU.mult))
                st.done(e.tensor_reduce(slot[:, k, :], M, AX.X, ALU.add))
                st.done(e.tensor_tensor(slot[:, k, :], slot[:, k, :], rk[:, k, :], ALU.add))
                st.done(e.scalar_tensor_tensor(keep[:, k, :], rk[:, k, :], float(CAP), valid[:, :],
                                               ALU.is_lt, ALU.mult))
                st.done(e.tensor_tensor(slot[:, k, :], slot[:, k, :], keep[:, k, :], ALU.mult))
                st.done(e.tensor_copy(slot_from[:, k, :], slot[:, k, :]))
                st.done(e.tensor_scalar(rk[:, k, :], keep[:, k, :], -1.0, 1.0, ALU.mult, ALU.add))
                st.done(e.tensor_tensor(rk[:, k, :], rk[:, k, :], trash[:, k, :], ALU.mult))
                st.done(e.tensor_tensor(slot[:, k, :], slot[:, k, :], rk[:, k, :], ALU.add))
                st.done(e.tensor_copy(slot_to[:, k, :], slot[:, k, :]))
            e.sem_inc(S("slots_ready"), 1)
            e.wait_ge(S("top_exp"), 1)
            st.done(e.tensor_scalar(gap, gate[:, 1, :], 1.0, None, ALU.add))
            st.done(e.reciprocal(gate[:, 0, :], gap))
            st.done(e.tensor_tensor(gate[:, 1, :], gate[:, 1, :], gate[:, 0, :], ALU.mult))
            for k in range(TOP):
                st.done(e.tensor_tensor(gate[:, k, :], gate[:, k, :], keep[:, k, :], ALU.mult))
            e.wait_ge(S("chunk_experts_up"), 1)
            st.done(e.tensor_copy(etab[0:1, :], psum[0:1, 6, 0:P]))
            phase_end(e, "route")

            def copy_turned(c, par):
                e.wait_ge(S("chunk_turned"), c + 1)
                e.tensor_copy(xTs[par], psum[:, par, 0:F]).then_inc(S("chunk_copied"), 1)

            e.sem_inc(S("chunk_made"), 2)
            copy_turned(0, 0)
            copy_turned(1, 1)
            turns = e.value_load(nturn[0:1, 0:1], min_val=1, max_val=MAXCH // RING)
            with e.Fori(0, turns) as j:
                for n in range(RING):
                    c, par = RING * j + n, n % 2
                    e.wait_ge(S("hidden_summed"), c + 1)
                    copy_turned(c + 2, par)
                    e.wait_ge(S("chunk_summed"), c + 1)
                    e.wait_ge(S(f"b2_in{n}"), 16 * j + 16)
                    e.wait_ge(S(f"rows_stored{n}"), 16 * j)
                    e.tensor_tensor(yout[n], psum[:, 4 + par, 0:F], b2s[n], ALU.add)\
                        .then_inc(S("chunk_made"), 1)
            phase_end(e, "experts")
            st = Steps(e, S("dve_bn"))
            for t in range(T):
                r = ring[t % 4]
                e.wait_ge(S(f"gathered{t % 4}"), 32 * (t // 4) + 32)
                st.done(e.scalar_tensor_tensor(X4[:, t, :], r[:, 0, :], gate[:, 0, t:t + 1], X4[:, t, :],
                                               ALU.mult, ALU.add))
                e.scalar_tensor_tensor(X4[:, t, :], r[:, 1, :], gate[:, 1, t:t + 1], X4[:, t, :],
                                       ALU.mult, ALU.add).then_inc(S("combined"), 1)
            e.wait_ge(S("combined"), T)
            e.wait_ge(S("bn_summed"), 1)
            st.done(e.tensor_scalar(G[:, :], psum[:, 0, 0:F], 1.0 / N, None, ALU.mult))
            for t in range(T):
                e.tensor_tensor(X4[:, t, :], X4[:, t, :], G[:, :], ALU.subtract).then_inc(S("centred"), 1)
            e.wait_ge(S("centred"), T)
            e.wait_ge(S("bn_summed"), 2)
            e.tensor_scalar(V[:, :], psum[:, 1, 0:F], 1.0 / N, EPS, ALU.mult, ALU.add).then_inc(S("bn_var"), 1)
            e.wait_ge(S("bn_rstd"), 1)
            st.done(e.tensor_tensor(U[:, :], V[:, :], bc["gam"][:, :], ALU.mult))
            phase_end(e, "combine")
            stf = Steps(e, S("dve_out"), 6)

            def last(t, par):
                stf.tile(t)
                xt = X[:, bass.ds(t, 1), :].rearrange("p a f -> p (a f)")
                yt = X4[:, bass.ds(t, 1), :].rearrange("p a f -> p (a f)")
                stf.done(e.tensor_tensor(yt, yt, U[:, :], ALU.mult))
                stf.done(e.tensor_tensor(yt, yt, bc["bet"][:, :], ALU.add))
                stf.done(e.tensor_tensor(yt, yt, xt, ALU.add))
                carry_wait(e)
                stf.done(e.bn_stats(st6[:, :], yt))
                carry_wait(e)
                stf.done(e.bn_aggr(mv[:, :], st6[:, :]))
                e.sem_inc(S("out_moments"), 1)
                e.wait_ge(S("out_rstd"), t + 1)
                stf.done(e.tensor_scalar(yt, yt, mv[:, 0:1], rstd[:, 0:1], ALU.subtract, ALU.mult))
                e.sem_inc(S("out_made"), 1)
            tiles(e, last)

        def pool_moe(e):
            phase_end(e, "l3")
            e.wait_ge(S("slots_ready"), 1)
            for t in range(T):
                for k in range(TOP):
                    e.indirect_dma_start(out=xbuf, out_offset=bass.IndirectOffsetOnAxis(ap=slot_to[:, k, t:t + 1], axis=0),
                                         in_=X4[:, t, :], in_offset=None).then_inc(S("rows_scattered"), 16)
            e.wait_ge(S("rows_scattered"), 16 * TOP * T)
            phase_end(e, "route")
            turns = e.value_load(nturn[0:1, 0:1], min_val=1, max_val=MAXCH // RING)
            with e.Fori(0, turns) as j:
                for n in range(RING):
                    c, par = RING * j + n, n % 2
                    e.wait_ge(S("chunk_made"), c + 3)
                    e.dma_start(ybuf[bass.ds(c * P, P), :], yout[n]).then_inc(S(f"rows_stored{n}"), 16)
            for n in range(RING):
                e.wait_ge(S(f"rows_stored{n}"), 16 * turns)
            carry_wait(e)
            phase_end(e, "experts")
            for t in range(T):
                if t >= 4:
                    e.wait_ge(S("combined"), t - 3)
                for k in range(TOP):
                    e.indirect_dma_start(out=ring[t % 4][:, k, :], out_offset=None, in_=ybuf,
                                         in_offset=bass.IndirectOffsetOnAxis(ap=slot_from[:, k, t:t + 1], axis=0))\
                        .then_inc(S(f"gathered{t % 4}"), 16)
            e.wait_ge(S("bn_var"), 1)
            for f in range(0, F, T):
                w = min(T, F - f)
                mm = e.tensor_tensor(V[:, f:f + w], V[:, f:f + w], mhalf[:, 0:w], ALU.pow)
            mm.then_inc(S("bn_rstd"), 1)
            phase_end(e, "combine")

            def norm(t, par):
                e.wait_ge(S("out_moments"), t + 1)
                carry_wait(e)
                e.tensor_scalar(ve[:, :], mv[:, 1:2], EPS, None, ALU.add).then_inc(S("out_eps"), 1)
                e.wait_ge(S("out_eps"), t + 1)
                e.tensor_tensor(rstd[:, :], ve[:, :], mhalf[:, 0:1], ALU.pow).then_inc(S("out_rstd"), 1)
            tiles(e, norm)

        @block.sync
        def _(e):
            ld = S("inputs_loaded")
            n = [0]

            def load(o, i):
                e.dma_start(o, i).then_inc(ld, 16)
                n[0] += 16

            full = EC - 1
            e.wait_ge(S("pads_set"), 3)
            for rows, a in ((src_rows_i, src), (dst_rows_i, dst)):
                r = rows.rearrange("c (g e) -> c g e", g=EG)
                load(r[:, 0:EG - 1, :], a[0:(EG - 1) * P * P].rearrange("(g c e) -> c g e", g=EG - 1, c=P))
                k = full - (EG - 1) * P
                load(r[0:k, EG - 1, :], a[(EG - 1) * P * P:full * P].rearrange("(c e) -> c e", e=P))
                load(r[k:k + 1, EG - 1, 0:E - full * P], a[full * P:E].rearrange("(c e) -> c e", c=1))
            e.wait_ge(ld, n[0])
            e.sem_inc(S("edges_loaded"), 1)
            load(X[:, 0:T - 1, :], x[0:(T - 1) * P, :].rearrange("(t p) f -> p t f", p=P))
            load(X[0:LAST, T - 1, :], x[(T - 1) * P:N, :])
            for w, k in ((wl0, "L0_gnn_weight"), (wcv, "L1_gnn_W_conv"), (wh1, "L2_gnn_W1"), (wh2, "L2_gnn_W2"),
                         (wgc, "L3_gnn_W_gc"), (wrs, "L3_gnn_W_res"), (wgt, "L3_gnn_Wg")):
                load(w[:, :, :], A[k].rearrange("(k p) f -> p k f", p=P))
            for w, k in ((wln, "L1_gnn_W_lin"), (wd1, "L1_gnn_W_dec1"), (wd2, "L1_gnn_W_dec2")):
                load(w[:, :], A[k])
            for w, k in (("l0", "L0_gnn_bias"), ("dec2", "L1_gnn_b_dec2"), ("h1", "L2_gnn_b1"), ("h2", "L2_gnn_b2"),
                         ("gc", "L3_gnn_b_gc"), ("res", "L3_gnn_b_res"), ("gam", "L3_gnn_gamma"),
                         ("bet", "L3_gnn_beta")):
                load(bc[w][:, :], A[k].rearrange("(a f) -> a f", a=1).to_broadcast([P, F]))
            load(b1rows[:, :], A["L3_gnn_b1"])
            load(bgb[:, :], A["L3_gnn_bg"].rearrange("(a f) -> a f", a=1).to_broadcast([P, NE]))
            load(col["conv"][:, :], A["L1_gnn_b_conv"].rearrange("(p a) -> p a", a=1))
            load(col["lin"][0:HL, :], A["L1_gnn_b_lin"].rearrange("(p a) -> p a", a=1))
            load(col["dec1"][:, :], A["L1_gnn_b_dec1"].rearrange("(p a) -> p a", a=1))
            load(col["a"][:, :], A["L2_gnn_a"].rearrange("(p a) -> p a", a=1).to_broadcast([P, 1]))
            e.wait_ge(ld, n[0])
            phase_end(e, "load")
            phase_end(e, "table")
            e.wait_ge(S("zeros_set"), 1)
            zeros = X4[:, :, :].rearrange("p t f -> p (t f)")[:, 0:ZROWS * F].rearrange("p (k f) -> p k f", f=F)
            for buf in (xbuf, ybuf):
                with e.Fori(0, NCH // ZROWS) as g:
                    e.dma_start(buf[bass.ds(g * ZROWS * P, ZROWS * P), :].rearrange("(p k) f -> p k f", p=P),
                                zeros).then_inc(S("rows_zeroed"), 16)
            e.wait_ge(S("rows_zeroed"), 2 * 16 * (NCH // ZROWS))

            with e.Fori(0, T) as b:
                e.wait_ge(S("band_copied"), NB * (b + 1))
                e.dma_start(a_rev[:, :, bass.ds(b * P, P)].rearrange("s p c -> p s c"),
                            band_rows.rearrange("p (s c) -> p s c", c=P)).then_inc(S("band_rows_stored"), 16)
                e.wait_ge(S("band_turned"), NB * (b + 1))
                e.dma_start(a_fwd[bass.ds(b, 1), :, :].rearrange("a p c -> p (a c)"), band_cols)\
                    .then_inc(S("band_cols_stored"), 16)
            e.wait_ge(S("band_rows_stored"), 16 * T)
            e.wait_ge(S("band_cols_stored"), 16 * T)
            phase_end(e, "counts")
            phase_end(e, "split")

            def blocks(ph, mat):
                def load_block(i, par):
                    e.dma_start(blk[par][:, :], mat[bass.ds(i, 1), :, :].rearrange("a p c -> p (a c)"))\
                        .then_inc(S(f"block_in{par}"), 16)

                load_block(0, 0)
                load_block(1, 1)
                with e.Fori(1, T // 2) as j:
                    for par in range(2):
                        e.wait_ge(S("tile_summed"), past(ph, "summed") + 2 * j + par - 1)
                        load_block(2 * j + par, par)
                e.wait_ge(S("tile_summed"), past(ph, "summed") + T - 2)
                load_block(T - 1, 0)
                phase_end(e, ph)

            blocks("l0", a_fwd)
            blocks("l1", a_fwd)
            blocks("h1a", a_fwd)
            blocks("h1b", a_rev)
            blocks("h2a", a_fwd)
            blocks("h2b", a_rev)
            blocks("l3", a_fwd)
            sync_moe(e)

        @block.tensor
        def _(e):
            phase_end(e, "load")
            e.wait_ge(S("rows_float"), 2)
            e.wait_ge(S("ident_set"), 2)
            for g in range(EG):
                e.transpose(psum[:, 0, g * P:(g + 1) * P], src_rows[:, g * P:(g + 1) * P], identF[:, :])
                mm = e.transpose(psum[:, 1, g * P:(g + 1) * P], dst_rows[:, g * P:(g + 1) * P], identF[:, :])
            mm.then_inc(S("edges_turned"), 1)
            e.wait_ge(S("chunk_ends"), 2)
            for g in range(EG):
                e.matmul(psum[0:32, 2, g * P:(g + 1) * P], chunk_lo[:, g * 32:(g + 1) * 32], identF[:, :],
                         start=True, stop=True)
                mm = e.matmul(psum[0:32, 3, g * P:(g + 1) * P], chunk_hi[:, g * 32:(g + 1) * 32], identF[:, :],
                              start=True, stop=True)
            mm.then_inc(S("chunk_rows"), 1)
            e.wait_ge(S("band_cols_ready"), 2)
            for k in range(2):
                mm = e.transpose(psum[0:1, 4, k * 32:(k + 1) * 32], bandcol[0:32, k:k + 1], identF[0:32, 0:32])
            mm.then_inc(S("band_rows_up"), 1)
            phase_end(e, "table")

            psb = psum[:, :, :].rearrange("p b c -> p (b c)").bitcast(BF16).rearrange("p (b c) -> p b c", b=8)
            with e.Fori(0, T) as b:
                before = e.value_load(tab[0:1, 1, bass.ds(b, 1)], min_val=0, max_val=T * EC)
                upto = e.value_load(tab[0:1, 2, bass.ds(b, 1)], min_val=1, max_val=T * EC)
                e.wait_ge(S("band_turned"), NB * b)
                e.wait_ge(S("degrees_read"), b)
                for q in range(NB):
                    w = min(BANK, NP - q * BANK)
                    e.matmul(psum[:, q, 0:w], zrow[:, 0:P], zrow[:, 0:w], start=True, stop=True)
                e.matmul(psum[:, 7, 0:1], zrow[:, 0:P], zrow[:, 0:1], start=True, stop=True)
                with e.Fori(before, upto) as k:
                    e.wait_ge(S("onehots_ready"), 2 * k + 2)
                    lhs = both_d[:, bass.ds(k % 2, 1), :].rearrange("p a c -> p (a c)")
                    e.matmul(psum[:, 7, 0:1], lhs, onesB[:, :], start=False, stop=True, skip_group_check=True)
                    for q in range(NB):
                        w = min(BANK, NP - q * BANK)
                        mm = e.matmul(psum[:, q, 0:w], lhs,
                                      both_s[:, bass.ds(k % 2, 1), q * BANK:q * BANK + w].rearrange("p a c -> p (a c)"),
                                      start=False, stop=True, skip_group_check=True)
                    mm.then_inc(S("onehots_used"), 1)
                e.matmul(psum[:, 7, 1:2], zrow[:, 0:P], zrow[:, 0:1], start=True, stop=True)\
                    .then_inc(S("band_summed"), 1)
                for q in range(NB):
                    e.wait_ge(S("band_copied"), NB * b + q + 1)
                    for t in range(q * TPB, min(T, (q + 1) * TPB)):
                        o = (t - q * TPB) * P
                        e.matmul(psum[:, 7, 32 + t:33 + t], band_rows[:, t * P:(t + 1) * P], onesB[:, :],
                                 start=True, stop=True)
                        mm = e.transpose(psb[:, q, o:o + P], band_rows[:, t * P:(t + 1) * P], identB[:, :])
                    mm.then_inc(S("band_transposed"), 1)
            phase_end(e, "counts")
            phase_end(e, "split")

            def aggregate(ph, XS, Fw, own, steps):
                def add(i, par, side):
                    e.wait_ge(S(f"block_in{par}"), 16 * past_blocks(ph, par) + 8 * (i - par) + 16)
                    if isinstance(i, int) and i < 2:
                        pass
                    else:
                        e.wait_ge(S("tile_sum_read"), past(ph, "sum_read") + i - 1)
                    o = agg[par][:, 0:Fw]
                    gap = 4 if len(side) < 6 else 3
                    for k in range(T):
                        for s in range(PARTS):
                            mm = e.matmul(o, blk[par][:, k * P:(k + 1) * P], XS[:, k, s, 0:Fw],
                                          start=(k == 0 and s == 0), stop=(not own and k == T - 1 and s == PARTS - 1))
                        if k % gap == gap - 1 and k // gap < len(side) and k < T - 1:
                            side[k // gap]()
                    if own:
                        for s in range(PARTS):
                            mm = e.matmul(o, identB[:, :],
                                          XS[:, bass.ds(i, 1), s, 0:Fw].rearrange("p a f -> p (a f)"),
                                          start=False, stop=(s == PARTS - 1))
                    mm.then_inc(S("tile_summed"), 1)

                def whole(it, par, side, known):
                    if known and it(0) >= T:
                        for f in side:
                            f()
                    else:
                        add(it(0), par, side)

                pipeline(e, [(lag, f) for lag, f in steps] or [(0, lambda i, par: None)], whole)
                phase_end(e, ph)

            def turn(ph, need, sig, o, a, nt):
                def step(i, par):
                    e.wait_ge(S("tile_" + need), past(ph, need) + i + 1)
                    v = a[par] if isinstance(a, list) else a
                    for k in range(nt):
                        mm = e.transpose(o[:, k * P:(k + 1) * P], v[:, k * P:(k + 1) * P], identF[:, :])
                    mm.then_inc(S("tile_" + sig), 1)
                return step

            def dense(ph, need, sig, o, pairs):
                def step(i, par):
                    for nd in need:
                        e.wait_ge(S("tile_" + nd), past(ph, nd) + i + 1)
                    v = o[par] if isinstance(o, list) else o
                    if ph == "l1" and sig == "pre":
                        e.wait_ge(S("tile_moments"), past(ph, "moments") + i)
                    for n_, (l, r) in enumerate(pairs):
                        mm = e.matmul(v, l, r, start=(n_ == 0), stop=(n_ == len(pairs) - 1))
                    mm.then_inc(S("tile_" + sig), 1)
                return step

            def two(t, w):
                return [(t[:, k, :], w[:, k, :]) for k in range(KF)]

            aggregate("l0", XSa, F, False, [
                (1, turn("l0", "sum_read", "g_turned", pT, G, KF)),
                (3, turn("l0", "normed", "x_turned", pT2, Xn, KF)),
                (1, dense("l0", ["gT"], "pre", pD, two(tT, wl0))),
                (3, dense("l0", ["xT"], "proj", [o[:, 0:HC] for o in pD2], two(tT2, wcv)))])
            aggregate("l1", XSb, HC, True, [
                (2, dense("l1", ["zT"], "dec", pdec, [(wd1[:, :], G2[0:HL, 0:P])])),
                (1, turn("l1", "sum_read", "g_turned", pT, G, 1)),
                (4, turn("l1", "normed", "x_turned", pT2, Xn, KF)),
                (2, dense("l1", ["dT"], "pre", pD[0], [(tT[:, 1, :], wd2[:, :])])),
                (1, dense("l1", ["gT"], "lin", plin, [(wln[:, :], tT[:, 0, :])])),
                (4, dense("l1", ["xT"], "proj", pD2, two(tT2, wh1)))])
            aggregate("h1a", XSa, F, False, [])
            aggregate("h1b", XSb, F, False, [
                (1, turn("h1b", "active", "g_turned", pT, G, KF)),
                (1, dense("h1b", ["gT"], "proj", pD2, two(tT, wh2)))])
            aggregate("h2a", XSa, F, False, [])
            aggregate("h2b", XSb, F, False, [])
            aggregate("l3", XSa, F, False, [
                (1, turn("l3", "own_copied", "x_turned", pT2, Xn, KF)),
                (1, turn("l3", "sum_read", "g_turned", pT, G, KF)),
                (2, turn("l3", "x4_made", "x4_turned", px4, V, KF)),
                (1, dense("l3", ["xT", "gT"], "pre", pD[0], two(tT, wgc) + two(tT2, wrs))),
                (2, dense("l3", ["x4T"], "logits", [o[:, 0:NE] for o in pD2], two(tT3, wgt)))])
            pe_moe(e)

        @block.scalar
        def _(e):
            phase_end(e, "load")
            phase_end(e, "table")
            psb = psum[:, :, :].rearrange("p b c -> p (b c)").bitcast(BF16).rearrange("p (b c) -> p b c", b=8)
            with e.Fori(0, T) as b:
                e.wait_ge(S("band_summed"), b + 1)
                e.wait_ge(S("band_rows_stored"), 16 * b)
                for q in range(NB):
                    w = min(BANK, NP - q * BANK)
                    e.activation(band_rows[:, q * BANK:q * BANK + w], psum[:, q, 0:w], ACT.Copy)\
                        .then_inc(S("band_copied"), 1)
                e.wait_ge(S("band_cols_stored"), 16 * b)
                for q in range(NB):
                    w = min(BANK, NP - q * BANK)
                    e.wait_ge(S("band_transposed"), NB * b + q + 1)
                    e.activation(band_cols[:, q * BANK:q * BANK + w], psb[:, q, 0:w], ACT.Copy)\
                        .then_inc(S("band_turned"), 1)
            phase_end(e, "counts")

            def pick(v, par):
                return v[par] if isinstance(v, list) else v

            def split_a(ph, need, a, XS, w):
                def do(i, par):
                    e.wait_ge(S("tile_" + need), past(ph, need) + i + 1)
                    e.activation(XS[:, bass.ds(i, 1), 0, 0:w].rearrange("p a f -> p (a f)"), pick(a, par), ACT.Copy)\
                        .then_inc(S("tile_part0"), 1)
                    e.wait_ge(S("tile_rest"), past(ph, "rest") + i + 1)
                    e.activation(XS[:, bass.ds(i, 1), 1, 0:w].rearrange("p a f -> p (a f)"), R1[:, 0:w], ACT.Copy)\
                        .then_inc(S("tile_part1"), 1)
                return do

            def copy(ph, need, sig, o, a, func=ACT.Copy, **kw):
                def do(i, par):
                    e.wait_ge(S("tile_" + need), past(ph, need) + i + 1)
                    e.activation(o, pick(a, par), func, **kw).then_inc(S("tile_" + sig), 1)
                return do

            def run(ph, stages):
                pipeline(e, stages)
                phase_end(e, ph)

            def flat(t):
                return t[:, :, :].rearrange("p k c -> p (k c)")

            run("split", [(0, split_a("split", "scaled", G[:, :], XSa, F))])
            run("l0", [(1, copy("l0", "g_turned", "gT", flat(tT), pT)),
                       (3, copy("l0", "x_turned", "xT", flat(tT2), pT2)),
                       (2, copy("l0", "negative", "exped", G2[:, :], U[:, :], ACT.Exp)),
                       (4, split_a("l0", "scaled", V2[:, 0:HC], XSb, HC))])
            run("l1", [(2, copy("l1", "lin", "zT", G2[0:HL, 0:P], plin, ACT.Identity, bias=col["lin"][0:HL, :])),
                       (1, copy("l1", "g_turned", "gT", tT[:, 0, :], pT[:, 0:P], ACT.Relu, bias=col["conv"][:, :])),
                       (2, copy("l1", "dec", "dT", tT[:, 1, :], pdec, ACT.Relu, bias=col["dec1"][:, :])),
                       (4, copy("l1", "x_turned", "xT", flat(tT2), pT2)),
                       (5, split_a("l1", "proj", pD2, XSa, F))])
            run("h1a", [(1, split_a("h1a", "sum_read", G[:, :], XSb, F))])
            run("h1b", [(2, split_a("h1b", "proj", pD2, XSa, F)),
                        (1, copy("h1b", "g_turned", "gT", flat(tT), pT))])
            run("h2a", [(1, split_a("h2a", "sum_read", G[:, :], XSb, F))])
            run("h2b", [(1, split_a("h2b", "scaled", G2[:, :], XSa, F))])
            run("l3", [(1, copy("l3", "x_turned", "xT", flat(tT2), pT2)),
                       (1, copy("l3", "g_turned", "gT", flat(tT), pT)),
                       (2, copy("l3", "x4_turned", "x4T", flat(tT3), px4))])
            act_moe(e)

        @block.vector
        def _(e):
            st = Steps(e, S("dve_setup"))
            st.done(e.memset(src_rows_i, FAR))
            st.done(e.memset(dst_rows_i, FAR))
            e.memset(zrow[:, :], 0.0)
            e.memset(mhalf[:, :], -0.5)
            e.memset(ones[:, :], 1.0)
            e.memset(onesB[:, :], 1.0)
            e.memset(outdeg[:, :], 0.0)
            e.memset(X4[:, :, :], 0.0).then_inc(S("zeros_set"), 1)
            st.done(e.memset(X[:, T - 1, :], 0.0))
            e.sem_inc(S("pads_set"), 3)
            e.wait_ge(S("edges_loaded"), 1)
            e.tensor_copy(src_rows, src_rows_i).then_inc(S("rows_float"), 1)
            e.tensor_copy(dst_rows, dst_rows_i).then_inc(S("rows_float"), 1)
            e.wait_ge(S("rows_float"), 2)
            phase_end(e, "load")
            ends = scr1[:, 0:2 * EG]
            d3 = dst_rows.rearrange("c (g e) -> c g e", g=EG)
            st.done(e.tensor_reduce(ends[:, 0:EG], d3, AX.X, ALU.min))
            st.done(e.tensor_reduce(ends[:, EG:2 * EG], d3, AX.X, ALU.max))
            e.tensor_copy(chunk_lo.rearrange("p (g b) -> p g b", g=EG),
                          ends[:, 0:EG].unsqueeze(2).to_broadcast([P, EG, 32])).then_inc(S("chunk_ends"), 1)
            e.tensor_copy(chunk_hi.rearrange("p (g b) -> p g b", g=EG),
                          ends[:, EG:2 * EG].unsqueeze(2).to_broadcast([P, EG, 32])).then_inc(S("chunk_ends"), 1)
            e.wait_ge(S("edges_turned"), 1)
            st.done(e.tensor_scalar(scol, psum[:, 0, 0:EG * P], float(-MID), None, ALU.add))
            st.done(e.tensor_scalar(dcol, psum[:, 1, 0:EG * P], float(P), None, ALU.add))
            e.wait_ge(S("chunk_rows"), 1)
            e.wait_ge(S("iotas_set"), 4)
            e.wait_ge(S("chunk_ends"), 2)
            B = slice(0, 32)
            st.done(e.tensor_scalar(in_band[B, :], psum[B, 2, :], bandcol[B, 3:4], None, ALU.is_le))
            st.done(e.scalar_tensor_tensor(in_band[B, :], psum[B, 3, :], bandcol[B, 2:3], in_band[B, :],
                                           ALU.is_ge, ALU.mult))
            BIG = float(EG * P)
            st.done(e.scalar_tensor_tensor(scr1[B, :], chunk_id[B, :], 1.0, in_band[B, :], ALU.add, ALU.mult))
            st.done(e.tensor_reduce(bandcol[B, 5:6], scr1[B, :], AX.X, ALU.max))
            st.done(e.scalar_tensor_tensor(scr1[B, :], chunk_id[B, :], -BIG, in_band[B, :], ALU.add, ALU.mult))
            st.done(e.tensor_reduce(bandcol[B, 4:5], scr1[B, :], AX.X, ALU.min))
            e.tensor_scalar(bandcol[B, 0:1], bandcol[B, 4:5], BIG, float(EC - 1), ALU.add, ALU.min)\
                .then_inc(S("band_cols_ready"), 1)
            e.wait_ge(S("band_cols_ready"), 1)
            st.done(e.tensor_scalar(bandcol[B, 6:7], bandcol[B, 0:1], 1.0, None, ALU.add))
            e.tensor_tensor(bandcol[B, 1:2], bandcol[B, 5:6], bandcol[B, 6:7], ALU.max)\
                .then_inc(S("band_cols_ready"), 1)
            e.wait_ge(S("band_rows_up"), 1)
            br = bandrow[0:1, :]
            st.done(e.tensor_copy(br[:, 0:64], psum[0:1, 4, 0:64]))
            st.done(e.tensor_tensor(scr1[0:1, 0:32], br[:, 32:64], br[:, 0:32], ALU.subtract))
            st.done(e.memset(br[:, 96:128], 1.0))
            st.done(e.tensor_tensor_scan(br[:, 64:96], br[:, 96:128], scr1[0:1, 0:32], 0.0, ALU.mult, ALU.add))
            st.done(e.tensor_tensor(br[:, 32:64], br[:, 64:96], scr1[0:1, 0:32], ALU.subtract))
            st.done(e.tensor_copy(tab[:, :, :].rearrange("a k b -> a (k b)"), br[:, 0:96]))
            phase_end(e, "table")

            with e.Fori(0, T) as b:
                first = e.value_load(tab[0:1, 0, bass.ds(b, 1)], min_val=0, max_val=EC - 1)
                before = e.value_load(tab[0:1, 1, bass.ds(b, 1)], min_val=0, max_val=T * EC)
                upto = e.value_load(tab[0:1, 2, bass.ds(b, 1)], min_val=1, max_val=T * EC)
                e.tensor_scalar(dcol, dcol, float(-P), None, ALU.add).then_inc(S("band_shifted"), 1)
                e.wait_ge(S("band_shifted"), b + 1)
                carry_wait(e)
                with e.Fori(before, upto) as k:
                    c = nc.s_assert_within(first + k - before, 0, EC - 1,
                                           skip_runtime_bounds_check_because="k runs from before to upto")
                    e.wait_ge(S("onehots_used"), k + 1)
                    e.tensor_scalar(both_d[:, bass.ds(k % 2, 1), :].rearrange("p a c -> p (a c)"), iota_p,
                                    dcol[:, bass.ds(c, 1)], None, ALU.is_equal).then_inc(S("onehots_ready"), 1)
                    e.tensor_scalar(both_s[:, bass.ds(k % 2, 1), :].rearrange("p a c -> p (a c)"), iota_s,
                                    scol[:, bass.ds(c, 1)], None, ALU.is_equal).then_inc(S("onehots_ready"), 1)
                e.wait_ge(S("band_transposed"), NB * (b + 1))
                e.tensor_copy(indeg[:, bass.ds(b, 1)], psum[:, 7, 0:1])
                e.tensor_tensor(outdeg[:, :], outdeg[:, :], psum[:, 7, 32:32 + T], ALU.add)\
                    .then_inc(S("degrees_read"), 1)
                e.wait_ge(S("degrees_read"), b + 1)
            st.done(e.tensor_scalar(nsrc[:, :], outdeg[:, :], 1.0, None, ALU.max))
            st.done(e.tensor_scalar(ndst[:, :], indeg[:, :], 1.0, None, ALU.max))
            st.done(e.tensor_scalar(dis[:, :], indeg[:, :], 1.0, None, ALU.add))
            st.done(e.reciprocal(dinv[:, :], nsrc[:, :]))
            st.done(e.reciprocal(binv[:, :], ndst[:, :]))
            st.done(e.scalar_tensor_tensor(dinv[:, :], outdeg[:, :], 0.5, dinv[:, :], ALU.is_ge, ALU.mult))
            st.done(e.scalar_tensor_tensor(binv[:, :], indeg[:, :], 0.5, binv[:, :], ALU.is_ge, ALU.mult))
            e.sem_inc(S("inverses_made"), 1)
            e.wait_ge(S("norms_ready"), 3)
            phase_end(e, "counts")

            def row(buf, i):
                return buf[:, bass.ds(i, 1), :].rearrange("p a f -> p (a f)")

            def tcol(buf, i):
                return buf[:, bass.ds(i, 1)]

            def split_v(ph, a, XS, w, i):
                e.wait_ge(S("tile_part2"), past(ph, "part2") + i)
                e.wait_ge(S("tile_part0"), past(ph, "part0") + i + 1)
                e.tensor_tensor(R1[:, 0:w], a, XS[:, bass.ds(i, 1), 0, 0:w].rearrange("p a f -> p (a f)"),
                                ALU.subtract).then_inc(S("tile_rest"), 1)
                e.wait_ge(S("tile_part1"), past(ph, "part1") + i + 1)
                e.tensor_tensor(XS[:, bass.ds(i, 1), 2, 0:w].rearrange("p a f -> p (a f)"), R1[:, 0:w],
                                XS[:, bass.ds(i, 1), 1, 0:w].rearrange("p a f -> p (a f)"), ALU.subtract)\
                    .then_inc(S("tile_part2"), 1)

            def read_sum(ph, i, par, w, scale, o=None):
                e.wait_ge(S("tile_summed"), past(ph, "summed") + i + 1)
                e.tensor_scalar((G if o is None else o)[:, 0:w], agg[par][:, 0:w], tcol(scale, i), None, ALU.mult)\
                    .then_inc(S("tile_sum_read"), 1)
                e.wait_ge(S("tile_sum_read"), past(ph, "sum_read") + i + 1)

            def layernorm(ph, st, i, a, o):
                st.done(e.bn_stats(st6[:, :], a))
                carry_wait(e)
                e.bn_aggr(mv[:, :], st6[:, :]).then_inc(S("tile_moments"), 1)
                e.wait_ge(S("tile_moments"), past(ph, "moments") + i + 1)
                e.wait_ge(S("tile_rstd"), past(ph, "rstd") + i + 1)
                e.wait_ge(S("tile_x_kept"), past(ph, "x_kept") + i)
                e.tensor_scalar(o, a, mv[:, 0:1], rstd[:, 0:1], ALU.subtract, ALU.mult)\
                    .then_inc(S("tile_normed"), 1)
                e.wait_ge(S("tile_normed"), past(ph, "normed") + i + 1)

            def prelu(st, o, a, tmp):
                st.done(e.tensor_scalar(tmp, a, 0.0, col["a"][:, 0:1], ALU.min, ALU.mult))
                return e.scalar_tensor_tensor(o, a, 0.0, tmp, ALU.max, ALU.add)

            def split_body(i, par):
                e.tensor_scalar(G[:, :], row(X, i), tcol(nsrc, i), None, ALU.mult)\
                    .then_inc(S("tile_scaled"), 1)
                e.wait_ge(S("tile_scaled"), past("split", "scaled") + i + 1)
                split_v("split", G[:, :], XSa, F, i)
            tiles(e, split_body)
            phase_end(e, "split")

            def run(ph, stages):
                pipeline(e, stages)
                phase_end(e, ph)

            st0 = Steps(e, S("steps_l0"), 4)

            def l0_sum(i, par):
                read_sum("l0", i, par, F, ndst)

            def l0_norm(i, par):
                st0.tile(i)
                e.wait_ge(S("tile_pre"), past("l0", "pre") + i + 1)
                st0.done(e.tensor_tensor(V[:, :], pD[par], bc["l0"][:, :], ALU.add))
                e.tensor_scalar(U[:, :], V[:, :], 0.0, None, ALU.min).then_inc(S("tile_negative"), 1)
                st0.done(e.scalar_tensor_tensor(R2[:, :], V[:, :], 0.0, row(X, i), ALU.max, ALU.add))
                e.wait_ge(S("tile_exped"), past("l0", "exped") + i + 1)
                st0.done(e.scalar_tensor_tensor(V[:, :], G2[:, :], -1.0, R2[:, :], ALU.add, ALU.add))
                layernorm("l0", st0, i, V[:, :], Xn[par])

            def l0_split(i, par):
                e.wait_ge(S("tile_proj"), past("l0", "proj") + i + 1)
                e.tensor_scalar(V2[:, 0:HC], pD2[par][:, 0:HC], tcol(dis, i), None, ALU.mult)\
                    .then_inc(S("tile_scaled"), 1)
                e.wait_ge(S("tile_scaled"), past("l0", "scaled") + i + 1)
                split_v("l0", V2[:, 0:HC], XSb, HC, i)
            run("l0", [(1, l0_sum), (2, l0_norm), (4, l0_split)])

            st1 = Steps(e, S("steps_l1"), 3)

            def l1_sum(i, par):
                read_sum("l1", i, par, HC, dis)

            def l1_norm(i, par):
                st1.tile(i)
                e.wait_ge(S("tile_pre"), past("l1", "pre") + i + 1)
                st1.done(e.tensor_tensor(V[:, :], pD[0], bc["dec2"][:, :], ALU.add))
                st1.done(e.tensor_tensor(V[:, :], V[:, :], row(X, i), ALU.add))
                layernorm("l1", st1, i, V[:, :], Xn[par])

            def l1_split(i, par):
                split_v("l1", pD2[par], XSa, F, i)
            run("l1", [(1, l1_sum), (3, l1_norm), (5, l1_split)])

            def hyperedge(ph):
                def body(i, par):
                    read_sum(ph, i, par, F, binv)
                    split_v(ph, G[:, :], XSb, F, i)
                run(ph, [(1, body)])

            hyperedge("h1a")
            st2 = Steps(e, S("steps_h1b"), 2)

            def h1b(i, par):
                st2.tile(i)
                read_sum("h1b", i, par, F, dinv, V)
                st2.done(e.tensor_tensor(V[:, :], V[:, :], bc["h1"][:, :], ALU.add))
                prelu(st2, G[:, :], V[:, :], U[:, :]).then_inc(S("tile_active"), 1)

            def h1b_split(i, par):
                split_v("h1b", pD2[par], XSa, F, i)
            run("h1b", [(1, h1b), (2, h1b_split)])
            hyperedge("h2a")
            st3 = Steps(e, S("steps_h2b"), 6)

            def h2b(i, par):
                st3.tile(i)
                read_sum("h2b", i, par, F, dinv)
                st3.done(e.tensor_tensor(V[:, :], G[:, :], bc["h2"][:, :], ALU.add))
                st3.done(e.tensor_tensor(V[:, :], V[:, :], row(X, i), ALU.add))
                st3.done(prelu(st3, V[:, :], V[:, :], U[:, :]))
                st3.done(e.tensor_tensor(V[:, :], V[:, :], row(X, i), ALU.add))
                layernorm("h2b", st3, i, V[:, :], Xn[par])
                e.tensor_scalar(G2[:, :], Xn[par], tcol(nsrc, i), None, ALU.mult).then_inc(S("tile_scaled"), 1)
                e.wait_ge(S("tile_scaled"), past("h2b", "scaled") + i + 1)
                split_v("h2b", G2[:, :], XSa, F, i)
            run("h2b", [(1, h2b)])

            st.done(e.tensor_tensor(bc["gc"][:, :], bc["gc"][:, :], bc["res"][:, :], ALU.add))
            st4 = Steps(e, S("steps_l3"), 3)

            def l3_sum(i, par):
                read_sum("l3", i, par, F, ndst)

            def l3_x4(i, par):
                e.wait_ge(S("tile_pre"), past("l3", "pre") + i + 1)
                e.wait_ge(S("tile_x4_kept"), past("l3", "x4_kept") + i)
                e.tensor_tensor(V[:, :], pD[0], bc["gc"][:, :], ALU.add).then_inc(S("tile_x4_made"), 1)

            def l3_top(i, par):
                st4.tile(i)
                e.wait_ge(S("tile_logits"), past("l3", "logits") + i + 1)
                st4.done(e.tensor_tensor(U[:, 0:NE], pD2[par][:, 0:NE], bgb[:, :], ALU.add))
                carry_wait(e)
                st4.done(e.max(max8[:, :], U[:, 0:NE]))
                carry_wait(e)
                st4.done(e.max_index(idx8[:, :], max8[:, :], U[:, 0:NE]))
                e.tensor_copy(row(top_val, i), max8[:, 0:TOP])
                e.tensor_copy(row(top_idx, i), idx8[:, 0:TOP]).then_inc(S("tile_top"), 1)
                e.wait_ge(S("tile_top"), past("l3", "top") + i + 1)
            pipeline(e, [(1, l3_sum), (2, l3_x4), (3, l3_top)])
            dve_moe(e)

        @block.gpsimd
        def _(e):
            e.memset(identF[:, :], 0.0).then_inc(S("pool_cleared"), 1)
            e.memset(identB[:, :], 0.0).then_inc(S("pool_cleared"), 1)
            e.wait_ge(S("pool_cleared"), 2)
            for m in (identF, identB):
                e.affine_select(out=m[:, :], in_=m[:, :], compare_op=ALU.not_equal, fill=1.0, base=0,
                                pattern=[[-1, P]], channel_multiplier=1).then_inc(S("ident_set"), 1)
            e.iota(iota_s, [[1, NP]], base=-MID, channel_multiplier=0, allow_small_or_imprecise_dtypes=True)\
                .then_inc(S("iotas_set"), 1)
            e.iota(iota_p, [[1, P]], base=0, channel_multiplier=0, allow_small_or_imprecise_dtypes=True)\
                .then_inc(S("iotas_set"), 1)
            e.iota(chunk_id, [[1, EG * P]], base=0, channel_multiplier=0, allow_small_or_imprecise_dtypes=True)\
                .then_inc(S("iotas_set"), 1)
            e.iota(bandcol[:, 2:4], [[P - 1, 2]], base=0, channel_multiplier=P,
                   allow_small_or_imprecise_dtypes=True).then_inc(S("iotas_set"), 1)
            for m in (tri, vmask):
                e.memset(m[:, :], 1.0).then_inc(S("masks_set"), 1)
            e.memset(valid[:, :], 1.0).then_inc(S("masks_set"), 1)
            e.wait_ge(S("masks_set"), 3)
            e.affine_select(out=tri[:, :], in_=tri[:, :], compare_op=ALU.is_gt, fill=0.0, base=0,
                            pattern=[[1, P]], channel_multiplier=-1).then_inc(S("masks_set"), 1)
            e.affine_select(out=vmask[:, :], in_=vmask[:, :], compare_op=ALU.is_ge, fill=0.0, base=LAST - 1,
                            pattern=[[0, P]], channel_multiplier=-1).then_inc(S("masks_set"), 1)
            e.affine_select(out=valid[:, :], in_=valid[:, :], compare_op=ALU.is_ge, fill=0.0, base=N - 1,
                            pattern=[[-P, T]], channel_multiplier=-1).then_inc(S("masks_set"), 1)
            e.iota(iota_e[:, :], [[1, NE]], base=0, channel_multiplier=0, allow_small_or_imprecise_dtypes=True)\
                .then_inc(S("masks_set"), 1)
            e.iota(trash[:, :, :], [[NP, TOP], [P, T]], base=TRASH, channel_multiplier=1,
                   allow_small_or_imprecise_dtypes=True).then_inc(S("masks_set"), 1)
            e.iota(pcol[:, :], [[0, 1]], base=0, channel_multiplier=1, allow_small_or_imprecise_dtypes=True)\
                .then_inc(S("masks_set"), 1)
            e.wait_ge(S("iotas_set"), 4)
            e.wait_ge(S("masks_set"), 9)
            phase_end(e, "load")
            phase_end(e, "table")
            e.sem_inc(S("onehots_used"), 2)
            e.wait_ge(S("inverses_made"), 1)
            for n in (nsrc, ndst, dis):
                e.tensor_tensor(n[:, :], n[:, :], mhalf[:, :], ALU.pow).then_inc(S("norms_ready"), 1)
            e.wait_ge(S("norms_ready"), 3)
            phase_end(e, "counts")
            phase_end(e, "split")

            def norm_tile(ph, lag):
                def body(i, par):
                    e.wait_ge(S("tile_moments"), past(ph, "moments") + i + 1)
                    carry_wait(e)
                    e.tensor_scalar(ve[:, :], mv[:, 1:2], EPS, None, ALU.add).then_inc(S("tile_eps"), 1)
                    e.wait_ge(S("tile_eps"), past(ph, "eps") + i + 1)
                    e.tensor_tensor(rstd[:, :], ve[:, :], mhalf[:, 0:1], ALU.pow).then_inc(S("tile_rstd"), 1)
                    e.wait_ge(S("tile_normed"), past(ph, "normed") + i + 1)
                    e.tensor_copy(X[:, bass.ds(i, 1), :].rearrange("p a f -> p (a f)"), Xn[par])\
                        .then_inc(S("tile_x_kept"), 1)
                pipeline(e, [(lag, body)])
                e.wait_ge(S("tile_x_kept"), past(ph, "x_kept") + T)
                phase_end(e, ph)

            norm_tile("l0", 2)
            norm_tile("l1", 3)
            phase_end(e, "h1a")
            phase_end(e, "h1b")
            phase_end(e, "h2a")
            norm_tile("h2b", 1)

            def l3_own(i, par):
                e.wait_ge(S("tile_x_turned"), past("l3", "x_turned") + i)
                e.tensor_copy(Xn[par], X[:, bass.ds(i, 1), :].rearrange("p a f -> p (a f)"))\
                    .then_inc(S("tile_own_copied"), 1)

            def l3_keep(i, par):
                e.wait_ge(S("tile_x4_made"), past("l3", "x4_made") + i + 1)
                e.tensor_copy(X4[:, bass.ds(i, 1), :].rearrange("p a f -> p (a f)"), V[:, :])\
                    .then_inc(S("tile_x4_kept"), 1)
            pipeline(e, [(1, l3_own), (2, l3_keep)])
            e.wait_ge(S("tile_x4_kept"), past("l3", "x4_kept") + T)
            pool_moe(e)


_INS = ["x", "src", "dst", "L0_gnn_weight", "L0_gnn_bias", "L1_gnn_W_conv", "L1_gnn_b_conv", "L1_gnn_W_lin",
        "L1_gnn_b_lin", "L1_gnn_W_dec1", "L1_gnn_b_dec1", "L1_gnn_W_dec2", "L1_gnn_b_dec2", "L2_gnn_W1", "L2_gnn_b1",
        "L2_gnn_W2", "L2_gnn_b2", "L2_gnn_a", "L3_gnn_W_gc", "L3_gnn_b_gc", "L3_gnn_W_res", "L3_gnn_b_res",
        "L3_gnn_Wg", "L3_gnn_bg", "L3_gnn_w1", "L3_gnn_b1", "L3_gnn_w2", "L3_gnn_b2", "L3_gnn_gamma", "L3_gnn_beta"]


def kernel(**inputs):
    import numpy as _np
    import concourse.bacc as _bacc
    from concourse import mybir as _mybir
    from concourse.bass_utils import run_bass_kernel_spmd as _run

    nc = _bacc.Bacc("TRN2", target_bir_lowering=False, num_devices=1)
    arrays, args = {}, {}
    for name in _INS:
        a = _np.ascontiguousarray(inputs[name])
        arrays[f"in_{name}"] = a
        args[name] = nc.dram_tensor(f"in_{name}", a.shape, _mybir.dt.from_np(a.dtype), kind="ExternalInput").ap()
    out = nc.dram_tensor("out", arrays["in_x"].shape, F32, kind="ExternalOutput").ap()
    gnn_program(nc, args, out)
    return _run(nc, [arrays], core_ids=[0]).results[0]["out"]
```

```python
from contextlib import ExitStack

import concourse.bass as bass
from concourse import mybir

ALU = mybir.AluOpType
ACT = mybir.ActivationFunctionType
AX = mybir.AxisListType
F32 = mybir.dt.float32
BF16 = mybir.dt.bfloat16
F16 = mybir.dt.float16
I32 = mybir.dt.int32
U32 = mybir.dt.uint32
U8 = mybir.dt.uint8

P = 128
TOP = 2
CAP = 1024
EPS = 1e-05
FAR = 8191
RING = 4


class Steps:

    def __init__(self, eng, sem, per_tile=0):
        self.eng, self.sem, self.per_tile, self.base, self.n = eng, sem, per_tile, 0, 0

    def tile(self, i):
        assert self.n in (0, self.per_tile), (self.n, self.per_tile)
        self.base, self.n = i * self.per_tile, 0

    def done(self, ins):
        self.n += 1
        ins.then_inc(self.sem, 1)
        self.eng.wait_ge(self.sem, self.base + self.n)


def gnn_program(nc, A, out):
    x, src, dst = A["x"], A["src"], A["dst"]
    N, F = x.shape
    E = src.shape[0]
    T = (N + P - 1) // P
    NP = T * P
    LAST = N - (T - 1) * P
    EC = (E + P - 1) // P
    EG = (EC + P - 1) // P
    HC = A["L1_gnn_W_conv"].shape[1]
    HL = A["L1_gnn_W_lin"].shape[1]
    NE, _, H = A["L3_gnn_w1"].shape
    HT = H // P
    KF = F // P
    PARTS = 3
    BANK = 512
    NB = (NP + BANK - 1) // BANK
    TPB = BANK // P
    FIELDS = 3
    FT = -(-T // FIELDS)
    FW = FT * P
    UNROLL = 4
    SPLIT = 5
    ROUND = 7
    ROUNDS = -(-T // ROUND)
    MAXCH = TOP * N // P + NE
    MAXCH = -(-MAXCH // RING) * RING
    ZROWS = 20
    NCH = -(-(MAXCH + RING) // ZROWS) * ZROWS
    TRASH = NCH * P
    assert T % 2 == 1 and T % SPLIT == 0 and NCH <= P and F == 256 and HC == P

    a_fwd = nc.dram_tensor("counts_src_on_rows", (T, P, T * P), BF16, kind="Internal").ap()
    a_rev = nc.dram_tensor("counts_dst_on_rows", (T, P, T * P), BF16, kind="Internal").ap()
    a_fwd2 = nc.dram_tensor("rests_src_on_rows", (T, P, T * P), BF16, kind="Internal").ap()
    a_rev2 = nc.dram_tensor("rests_dst_on_rows", (T, P, T * P), BF16, kind="Internal").ap()
    xbuf = nc.dram_tensor("expert_rows_in", (TRASH + TOP * NP, F), F32, kind="Internal").ap()
    ybuf = nc.dram_tensor("expert_rows_out", (TRASH, F), F32, kind="Internal").ap()

    with ExitStack() as ctx:
        def sb(name, shape, dt=F32):
            return ctx.enter_context(nc.sbuf_tensor(name, shape, dt))

        sems = {}

        def S(name):
            if name not in sems:
                sems[name] = ctx.enter_context(nc.semaphore(name))
            return sems[name]

        X = sb("X", [P, T, F])
        X4 = sb("X4", [P, T, F])
        xsa = sb("xsa", [P, T * PARTS * F], BF16)
        xsb = sb("xsb", [P, T * PARTS * F], BF16)
        XSa = xsa[:, :].rearrange("p (t s f) -> p t s f", t=T, s=PARTS)
        XSb = xsb[:, :].rearrange("p (t s f) -> p t s f", t=T, s=PARTS)
        blk = [sb(f"blk{n}", [P, T * P], BF16) for n in range(2)]
        rblk = sb("rblk", [P, T * P], BF16)
        identF = sb("identF", [P, P])
        identB = sb("identB", [P, P], BF16)
        zrow = sb("zrow", [P, BANK], BF16)
        ones = sb("ones", [P, P])
        onesB = sb("onesB", [P, P], BF16)
        triB = sb("triB", [P, P], BF16)
        wl0 = sb("wl0", [P, KF, F])
        wcv = sb("wcv", [P, KF, HC])
        wln = sb("wln", [P, HL])
        wd1 = sb("wd1", [HL, HC])
        wd2 = sb("wd2", [P, F])
        wh1 = sb("wh1", [P, KF, F])
        wh2 = sb("wh2", [P, KF, F])
        wgc = sb("wgc", [P, KF, F])
        wrs = sb("wrs", [P, KF, F])
        wgt = sb("wgt", [P, KF, NE])
        bc = {k: sb("bc_" + k, [P, F]) for k in ("l0", "dec2", "h1", "h2", "gc", "res", "gam", "bet")}
        bgb = sb("bgb", [P, NE])
        col = {k: sb("col_" + k, [P, 1]) for k in ("conv", "lin", "dec1", "a")}
        b1T = sb("b1T", [P, HT, NE])
        outdeg = sb("outdeg", [P, T])
        indeg = sb("indeg", [P, T])
        nsrc = sb("nsrc", [P, T])
        ndst = sb("ndst", [P, T])
        dis = sb("dis", [P, T])
        dinv = sb("dinv", [P, T])
        binv = sb("binv", [P, T])
        mhalf = sb("mhalf", [P, T])
        tab = sb("tab", [1, 3, 32], I32)
        heavy = sb("heavy", [1, 1], I32)
        totals = sb("totals", [P, 2])
        outdeg_by = sb("outdeg_by", [P, T, T])
        G = sb("G", [P, F])
        G2 = sb("G2", [P, F])
        V = sb("V", [P, F])
        R1 = sb("R1", [P, F])
        U = sb("U", [P, F])
        Xn = [sb(f"Xn{n}", [P, F])[:, :] for n in range(2)]
        V2 = sb("V2", [P, F])
        R2 = sb("R2", [P, F])
        tT = sb("tT", [P, KF, P])
        tT2 = sb("tT2", [P, KF, P])
        tT3 = sb("tT3", [P, KF, P])
        st6 = sb("st6", [P, 6])
        mv = sb("mv", [P, 2])
        ve = sb("ve", [P, 1])
        rstd = sb("rstd", [P, 1])
        max8 = sb("max8", [P, 8])
        idx8 = sb("idx8", [P, 8], U32)

        def view(buf, at, n, dt):
            w = 2 if dt in (F32, I32, U32) else 1
            v = buf[:, at:at + n * w]
            return (v if dt == BF16 else v.bitcast(dt)), at + n * w

        at = 0
        iota_f, at = view(xsb, at, FW, F16)
        iota_p, at = view(xsb, at, P, F16)
        src_rows_i, at = view(xsb, at, EG * P, I32)
        dst_rows_i, at = view(xsb, at, EG * P, I32)
        src_rows, at = view(xsb, at, EG * P, F32)
        dst_rows, at = view(xsb, at, EG * P, F32)
        chunk_lo, at = view(xsb, at, EG * 32, F32)
        chunk_hi, at = view(xsb, at, EG * 32, F32)
        chunk_id, at = view(xsb, at, EG * P, F32)
        in_band, at = view(xsb, at, EG * P, F32)
        scr1, at = view(xsb, at, EG * P, F32)
        bandcol, at = view(xsb, at, 8, F32)
        bandrow, at = view(xsb, at, 4 * 32, F32)
        dcol, at = view(xsb, at, EG * P, F32)
        scol, at = view(xsb, at, EG * P, F32)
        fcol = [None] * FIELDS
        for n in range(FIELDS):
            fcol[n], at = view(xsb, at, EG * P, F32)
        words, at = view(xsb, at, FW + 2, I32)
        assert at <= T * PARTS * F
        wcol = src_rows
        one_w = FW + 2
        one_s, at = view(xsa, 0, UNROLL * one_w, BF16)
        wide_s = one_s[:, 0:FIELDS * FW]
        one_s = one_s.rearrange("p (b s) -> p b s", b=UNROLL)
        one_d, at = view(xsa, at, UNROLL * P, BF16)
        one_d = one_d.rearrange("p (b s) -> p b s", b=UNROLL)
        band_rows, band_cols = [None, None], [None, None]
        for n in range(2):
            band_rows[n], at = view(xsa, at, NP, BF16)
            band_cols[n], at = view(xsa, at, NP, BF16)
        assert at <= T * PARTS * F

        b1rows = sb("b1rows", [NE, H])
        vmask = sb("vmask", [P, P])
        iota_e = sb("iota_e", [P, NE])
        valid = sb("valid", [P, T])
        trash = sb("trash", [P, TOP, T])
        pcol = sb("pcol", [P, 1])
        etab = sb("etab", [1, P], I32)
        nturn = sb("nturn", [1, 1], I32)
        gate = sb("gate", [P, TOP, T])
        slot_to = sb("slot_to", [P, TOP, T], U32)
        slot_from = sb("slot_from", [P, TOP, T], U32)

        def cut(buf, at, shape, dt=F32):
            n = 1
            for s_ in shape:
                n *= s_
            v, at = view(buf, at, n, dt)
            if len(shape) == 2:
                v = v.rearrange("p (a b) -> p a b", a=shape[0])
            return v, at

        at = 0
        top_val, at = cut(xsb, at, (T, TOP))
        top_idx, at = cut(xsb, at, (T, TOP), U32)
        idxf, at = cut(xsb, at, (T, TOP))
        gap, at = cut(xsb, at, (T,))
        OH1, at = cut(xsb, at, (T, NE))
        OH2, at = cut(xsb, at, (T, NE))
        M, at = cut(xsb, at, (T, NE))
        chosen, at = cut(xsb, at, (T, NE), BF16)
        before_tile, at = cut(xsb, at, (T + 1, NE), BF16)
        rk, at = cut(xsb, at, (TOP, T))
        slot, at = cut(xsb, at, (TOP, T))
        keep, at = cut(xsb, at, (TOP, T))
        ecnt, at = cut(xsb, at, (NE,))
        eint, at = cut(xsb, at, (NE,), I32)
        eincl, at = cut(xsb, at, (NE,))
        ebase, at = cut(xsb, at, (NE,))
        ecol, at = cut(xsb, at, (2,))
        assert at <= T * PARTS * F
        SQ, at = cut(xsb, 0, (T, F))
        w1s, w2s, xin, xTs, hTs, yout, b2s, ring = ([] for _ in range(8))
        for base, lot in ((xsa, ((w1s, (KF, H), RING), (w2s, (HT, F), RING))),
                          (xsb, ((xin, (F,), RING), (yout, (F,), RING), (b2s, (F,), RING), (xTs, (F,), 2),
                                 (hTs, (HT, P), 2)))):
            at = 0
            for bufs, shape, n in lot:
                for _ in range(n):
                    v, at = cut(base, at, shape)
                    bufs.append(v)
            assert at <= T * PARTS * F
        for n in range(4):
            v, _ = cut(xsa, 2 * n * TOP * F, (TOP, F))
            ring.append(v)
        at = 8 * TOP * F
        out_stats, at = cut(xsa, at, (T, 6))
        out_mv, at = cut(xsa, at, (T, 2))
        out_r, at = cut(xsa, at, (T,))
        bn_r, at = cut(xsa, at, (KF,))

        psum = ctx.enter_context(nc.psum_tensor("psum", [P, 8, BANK], F32))
        agg = [psum[:, 0, 0:F], psum[:, 1, 0:F]]
        pT, pT2 = psum[:, 2, 0:F], psum[:, 3, 0:F]
        pD, pD2 = [psum[:, 4, 0:F], psum[:, 5, 0:F]], [psum[:, 6, 0:F], psum[:, 7, 0:F]]
        plin, pdec, px4 = psum[0:HL, 5, 0:P], psum[:, 5, P:2 * P], psum[:, 5, 0:F]

        block = ctx.enter_context(nc.Block())
        PHASES = ["load", "table", "counts", "checked", "rests", "split", "l0", "l1", "h1a", "h1b", "h2a", "h2b", "l3", "route", "experts",
                  "combine"]

        def field(n, w):
            return words[:, 0:w].bitcast(U8).rearrange("p (c b) -> p c b", b=4)[:, :, n]

        def phase_end(e, name):
            e.drain().then_inc(S("phases_ended"), 1)
            e.wait_ge(S("phases_ended"), 5 * (PHASES.index(name) + 1))

        SIGNALS = {
            "scaled": ["split", "l0", "h2b"], "part0": ["split", "l0", "l1", "h1a", "h1b", "h2a", "h2b"],
            "summed": ["l0", "l1", "h1a", "h1b", "h2a", "h2b", "l3"],
            "g_turned": ["l0", "l1", "h1b", "l3"], "pre": ["l0", "l1", "l3"], "x_turned": ["l0", "l1", "l3"],
            "proj": ["l0", "l1", "h1b"], "lin": ["l1"], "dec": ["l1"], "zT": ["l1"], "dT": ["l1"],
            "normed": ["l0", "l1", "h2b"], "negative": ["l0"], "exped": ["l0"], "active": ["h1b"],
            "own_copied": ["l3"], "x4_made": ["l3"], "x4_turned": ["l3"], "x4T": ["l3"], "logits": ["l3"],
            "x4_kept": ["l3"], "top": ["l3"]}
        SIGNALS["rest"] = SIGNALS["part1"] = SIGNALS["part2"] = SIGNALS["part0"]
        SIGNALS["sum_read"] = SIGNALS["summed"]
        SIGNALS["gT"], SIGNALS["xT"] = SIGNALS["g_turned"], SIGNALS["x_turned"]
        SIGNALS["moments"] = SIGNALS["eps"] = SIGNALS["rstd"] = SIGNALS["x_kept"] = SIGNALS["normed"]

        def past(ph, name):
            return T * SIGNALS[name].index(ph)

        def past_blocks(ph, par):
            return (T // 2 + (1 - par)) * SIGNALS["summed"].index(ph)

        def carry_wait(e):
            e.sem_inc(S("waits_carried"), 1)

        def tiles(e, body):
            pipeline(e, [(0, body)])

        def pipeline(e, stages, whole=None):
            depth = max(lag for lag, _ in stages)

            def turn(it, par, known):
                todo = [(lambda f=f, lag=lag: f(it(lag), (par + lag) % 2)) for lag, f in stages
                        if not known or 0 <= it(lag) < T]
                if whole is None:
                    for f in todo:
                        f()
                else:
                    whole(it, par, todo, known)

            pairs = (T - depth) // 2
            for n in range(depth):
                turn(lambda lag, n=n: n - lag, n % 2, True)
            with e.Fori(0, pairs) as j:
                for u in range(2):
                    turn(lambda lag, u=u: 2 * j + (depth + u - lag), (depth + u) % 2, False)
            for n in range(depth + 2 * pairs, T + depth):
                turn(lambda lag, n=n: n - lag, n % 2, True)

        def sync_moe(e):
            def expert_of(c):
                return e.value_load(etab[0:1, bass.ds(c, 1)], min_val=0, max_val=NE - 1)

            def load_rows(c, n):
                e.dma_start(xin[n], xbuf[bass.ds(c * P, P), :]).then_inc(S(f"rows_in{n}"), 16)

            def load_w1(ex, n):
                e.dma_start(w1s[n], A["L3_gnn_w1"][bass.ds(ex, 1), :, :].rearrange("a (k p) h -> p (a k) h", p=P))\
                    .then_inc(S(f"w1_in{n}"), 16)

            def load_w2(ex, n):
                e.dma_start(w2s[n], A["L3_gnn_w2"][bass.ds(ex, 1), :, :].rearrange("a (k p) f -> p (a k) f", p=P))\
                    .then_inc(S(f"w2_in{n}"), 16)

            def load_b2(ex, n):
                e.dma_start(b2s[n], A["L3_gnn_b2"][bass.ds(ex, 1), :].to_broadcast([P, F]))\
                    .then_inc(S(f"b2_in{n}"), 16)

            e.wait_ge(S("experts_known"), 1)
            for c in range(RING):
                ex = expert_of(c)
                load_w1(ex, c)
                load_w2(ex, c)
            phase_end(e, "route")
            for c in range(RING):
                load_rows(c, c)
                load_b2(expert_of(c), c)
            turns = e.value_load(nturn[0:1, 0:1], min_val=1, max_val=MAXCH // RING)
            with e.Fori(0, turns) as j:
                for n in range(RING):
                    c = RING * j + n
                    ex = expert_of(c + RING)
                    e.wait_ge(S("chunk_turned"), c + 1)
                    load_rows(c + RING, n)
                    e.wait_ge(S("hidden_summed"), c + 1)
                    load_w1(ex, n)
                    e.wait_ge(S("chunk_made"), c + 3)
                    load_w2(ex, n)
                    load_b2(ex, n)
            for n in range(RING):
                for name in ("rows_in", "w1_in", "w2_in", "b2_in"):
                    e.wait_ge(S(f"{name}{n}"), 16 * turns + 16)
            carry_wait(e)
            phase_end(e, "experts")
            phase_end(e, "combine")
            stores = 0
            for g in range(T // SPLIT):
                e.wait_ge(S("out_made"), (g + 1) * SPLIT)
                lo, hi = g * SPLIT, min((g + 1) * SPLIT, T - 1)
                e.dma_start(out[lo * P:hi * P, :].rearrange("(t p) f -> p t f", p=P), X4[:, lo:hi, :])\
                    .then_inc(S("out_stored"), 16)
                stores += 1
            e.dma_start(out[(T - 1) * P:N, :], X4[0:LAST, T - 1, :]).then_inc(S("out_stored"), 16)
            e.wait_ge(S("out_stored"), 16 * stores + 16)

        def pe_moe(e):
            for h in range(HT):
                mm = e.transpose(psum[:, 5, h * NE:(h + 1) * NE], b1rows[:, h * P:(h + 1) * P], identF[0:NE, 0:NE])
            mm.then_inc(S("b1_turned"), 1)
            e.wait_ge(S("running_counts"), 1)
            tpb = BANK // NE
            for q in range(-(-T // tpb)):
                lo, hi = q * tpb, min(T, (q + 1) * tpb)
                o = psum[:, q, 0:(hi - lo) * NE]
                e.matmul(o, triB[:, :], chosen[:, lo:hi, :].rearrange("p t x -> p (t x)"), start=True, stop=False)
                e.matmul(o, onesB[:, :], before_tile[:, lo:hi, :].rearrange("p t x -> p (t x)"),
                         start=False, stop=True)
            e.matmul(psum[:, 4, 0:NE], onesB[:, :], before_tile[:, T, :], start=True, stop=True)\
                .then_inc(S("ranked"), 1)
            e.wait_ge(S("chunk_experts"), 1)
            e.transpose(psum[0:1, 6, 0:P], ecol[:, 0:1], identF[:, :]).then_inc(S("chunk_experts_up"), 1)
            phase_end(e, "route")

            def turn(c, j, n, par):
                e.wait_ge(S(f"rows_in{n}"), 16 * j + 16)
                for k in range(KF):
                    mm = e.transpose(psum[:, par, k * P:(k + 1) * P], xin[n][:, k * P:(k + 1) * P], identF[:, :])
                mm.then_inc(S("chunk_turned"), 1)

            def hidden(c, j, n, par):
                e.wait_ge(S("chunk_copied"), c + 1)
                e.wait_ge(S(f"w1_in{n}"), 16 * j + 16)
                for h in range(HT):
                    for k in range(KF):
                        mm = e.matmul(psum[:, 2 + par, h * P:(h + 1) * P], w1s[n][:, k, h * P:(h + 1) * P],
                                      xTs[par][:, k * P:(k + 1) * P], start=(k == 0), stop=(k == KF - 1))
                mm.then_inc(S("hidden_summed"), 1)

            def rows_out(c, j, n, par):
                e.wait_ge(S("gelu_made"), c + 1)
                e.wait_ge(S(f"w2_in{n}"), 16 * j + 16)
                e.wait_ge(S("chunk_made"), c + 1)
                for h in range(HT):
                    mm = e.matmul(psum[:, 4 + par, 0:F], hTs[par][:, h, :], w2s[n][:, h, :],
                                  start=(h == 0), stop=(h == HT - 1))
                mm.then_inc(S("chunk_summed"), 1)

            turns = e.value_load(nturn[0:1, 0:1], min_val=1, max_val=MAXCH // RING)
            turn(0, 0, 0, 0)
            turn(1, 0, 1, 1)
            hidden(0, 0, 0, 0)
            with e.Fori(0, turns) as j:
                for n in range(RING):
                    c = RING * j + n
                    par = n % 2
                    e.wait_ge(S("chunk_copied"), c + 1)
                    turn(c + 2, j + (n + 2) // RING, (n + 2) % RING, par)
                    e.wait_ge(S("gelu_made"), c)
                    hidden(c + 1, j + (n + 1) // RING, (n + 1) % RING, 1 - par)
                    rows_out(c, j, n, par)
            phase_end(e, "experts")
            for n in range(2):
                e.matmul(psum[:, n, 0:F], zrow[:, 0:P], zrow[:, 0:F], start=True, stop=True)
            for n, (name, buf) in enumerate((("combined", X4), ("squared", SQ))):
                with e.Fori(0, T - 1) as t:
                    e.wait_ge(S(name), t + 1)
                    r = buf[:, bass.ds(t, 1), :].rearrange("p a f -> p (a f)")
                    e.matmul(psum[:, n, 0:F], ones[:, :], r, start=False, stop=True, skip_group_check=True)
                e.wait_ge(S(name), T)
                e.matmul(psum[:, n, 0:F], vmask[:, :], buf[:, T - 1, :], start=False, stop=True,
                         skip_group_check=True).then_inc(S("bn_summed"), 1)
            e.wait_ge(S("bn_diagonal"), 1)
            e.matmul(psum[:, 2, 0:F], ones[:, :], G2[:, :], start=True, stop=True).then_inc(S("bn_spread"), 1)
            phase_end(e, "combine")

        def act_moe(e):
            e.wait_ge(S("top_gap"), 1)
            e.activation(gate[:, 1, :], gap, ACT.Exp).then_inc(S("top_exp"), 1)
            e.wait_ge(S("b1_turned"), 1)
            e.activation(b1T[:, :, :].rearrange("p h x -> p (h x)"), psum[:, 5, 0:HT * NE], ACT.Copy)\
                .then_inc(S("b1_ready"), 1)
            e.wait_ge(S("b1_ready"), 1)
            phase_end(e, "route")

            def gelu(c, par):
                ex = e.value_load(etab[0:1, bass.ds(c, 1)], min_val=0, max_val=NE - 1)
                e.wait_ge(S("hidden_summed"), c + 1)
                for h in range(HT):
                    mm = e.activation(hTs[par][:, h, :], psum[:, 2 + par, h * P:(h + 1) * P], ACT.Gelu,
                                      bias=b1T[:, h, bass.ds(ex, 1)])
                mm.then_inc(S("gelu_made"), 1)

            turns = e.value_load(nturn[0:1, 0:1], min_val=1, max_val=MAXCH // RING)
            gelu(0, 0)
            with e.Fori(0, turns) as j:
                for n in range(RING):
                    c, par = RING * j + n, n % 2
                    e.wait_ge(S("chunk_summed"), c)
                    gelu(c + 1, 1 - par)
            phase_end(e, "experts")

            def square(t, par):
                e.wait_ge(S("centred"), t + 1)
                e.activation(SQ[:, bass.ds(t, 1), :].rearrange("p a f -> p (a f)"),
                             X4[:, bass.ds(t, 1), :].rearrange("p a f -> p (a f)"), ACT.Square)\
                    .then_inc(S("squared"), 1)
            tiles(e, square)
            phase_end(e, "combine")

        def dve_moe(e):
            phase_end(e, "l3")
            st = Steps(e, S("dve_route"))
            e.tensor_tensor(gap, top_val[:, :, 1], top_val[:, :, 0], ALU.subtract).then_inc(S("top_gap"), 1)
            st.done(e.tensor_copy(idxf, top_idx[:, :, 0:TOP]))
            one_hot = (OH1, OH2)
            ex_ids = iota_e[:, :].unsqueeze(1).to_broadcast([P, T, NE])
            alive = valid[:, T - 1:T].to_broadcast([P, NE])
            for k in range(TOP):
                st.done(e.tensor_tensor(one_hot[k], ex_ids, idxf[:, :, k:k + 1].to_broadcast([P, T, NE]),
                                        ALU.is_equal))
                st.done(e.tensor_tensor(one_hot[k][:, T - 1, :], one_hot[k][:, T - 1, :], alive, ALU.mult))
            st.done(e.tensor_tensor(chosen, OH1, OH2, ALU.add))
            st.done(e.memset(before_tile[:, 0, :], 0.0))
            for t in range(T):
                st.done(e.tensor_tensor(before_tile[:, t + 1, :], before_tile[:, t, :], chosen[:, t, :], ALU.add))
            e.sem_inc(S("running_counts"), 1)
            e.wait_ge(S("ranked"), 1)
            ranks = psum[:, 0:4, :].rearrange("p b c -> p (b c)")[:, 0:T * NE].rearrange("p (t x) -> p t x", t=T)
            st.done(e.tensor_scalar(ecnt, psum[:, 4, 0:NE], float(CAP), float(P - 1), ALU.min, ALU.add))
            st.done(e.tensor_copy(eint, ecnt))
            st.done(e.tensor_scalar(eint, eint, 7, None, ALU.arith_shift_right))
            st.done(e.tensor_copy(ecnt, eint))
            st.done(e.tensor_tensor_scan(eincl, ones[:, 0:NE], ecnt, 0.0, ALU.mult, ALU.add))
            st.done(e.tensor_tensor(ebase, eincl, ecnt, ALU.subtract))
            st.done(e.tensor_scalar(ecnt, eincl, pcol[:, 0:1], None, ALU.is_le))
            st.done(e.tensor_reduce(ecol[:, 1:2], ecnt, AX.X, ALU.add))
            e.tensor_scalar(ecol[:, 0:1], ecol[:, 1:2], float(NE - 1), None, ALU.min)\
                .then_inc(S("chunk_experts"), 1)
            st.done(e.tensor_scalar(eint[0:1, 0:1], eincl[0:1, NE - 1:NE], float(RING - 1), None, ALU.add))
            st.done(e.tensor_scalar(nturn[0:1, 0:1], eint[0:1, 0:1], RING.bit_length() - 1, None,
                                    ALU.arith_shift_right))
            st.done(e.tensor_scalar(ebase, ebase, float(P), None, ALU.mult))
            e.wait_ge(S("chunk_experts_up"), 1)
            st.done(e.tensor_copy(etab[0:1, :], psum[0:1, 6, 0:P]))
            e.sem_inc(S("experts_known"), 1)
            first_row = ebase.unsqueeze(1).to_broadcast([P, T, NE])
            for k in range(TOP):
                st.done(e.tensor_tensor(M, one_hot[k], ranks, ALU.mult))
                st.done(e.tensor_reduce(rk[:, k, :], M, AX.X, ALU.add))
                st.done(e.tensor_tensor(M, one_hot[k], first_row, ALU.mult))
                st.done(e.tensor_reduce(slot[:, k, :], M, AX.X, ALU.add))
                st.done(e.tensor_tensor(slot[:, k, :], slot[:, k, :], rk[:, k, :], ALU.add))
                st.done(e.scalar_tensor_tensor(keep[:, k, :], rk[:, k, :], float(CAP), valid[:, :],
                                               ALU.is_lt, ALU.mult))
                st.done(e.tensor_tensor(slot[:, k, :], slot[:, k, :], keep[:, k, :], ALU.mult))
                st.done(e.tensor_copy(slot_from[:, k, :], slot[:, k, :]))
                st.done(e.tensor_scalar(rk[:, k, :], keep[:, k, :], -1.0, 1.0, ALU.mult, ALU.add))
                st.done(e.tensor_tensor(rk[:, k, :], rk[:, k, :], trash[:, k, :], ALU.mult))
                st.done(e.tensor_tensor(slot[:, k, :], slot[:, k, :], rk[:, k, :], ALU.add))
                st.done(e.tensor_copy(slot_to[:, k, :], slot[:, k, :]))
                e.sem_inc(S("slots_ready"), 1)
            e.wait_ge(S("top_exp"), 1)
            st.done(e.tensor_scalar(gap, gate[:, 1, :], 1.0, None, ALU.add))
            st.done(e.reciprocal(gate[:, 0, :], gap))
            st.done(e.tensor_tensor(gate[:, 1, :], gate[:, 1, :], gate[:, 0, :], ALU.mult))
            for k in range(TOP):
                st.done(e.tensor_tensor(gate[:, k, :], gate[:, k, :], keep[:, k, :], ALU.mult))
            phase_end(e, "route")

            def copy_turned(c, par):
                e.wait_ge(S("chunk_turned"), c + 1)
                e.tensor_copy(xTs[par], psum[:, par, 0:F]).then_inc(S("chunk_copied"), 1)

            e.sem_inc(S("chunk_made"), 2)
            copy_turned(0, 0)
            copy_turned(1, 1)
            turns = e.value_load(nturn[0:1, 0:1], min_val=1, max_val=MAXCH // RING)
            with e.Fori(0, turns) as j:
                for n in range(RING):
                    c, par = RING * j + n, n % 2
                    e.wait_ge(S("hidden_summed"), c + 1)
                    copy_turned(c + 2, par)
                    e.wait_ge(S("chunk_summed"), c + 1)
                    e.wait_ge(S(f"b2_in{n}"), 16 * j + 16)
                    e.wait_ge(S(f"rows_stored{n}"), 16 * j)
                    e.tensor_tensor(yout[n], psum[:, 4 + par, 0:F], b2s[n], ALU.add)\
                        .then_inc(S("chunk_made"), 1)
            phase_end(e, "experts")
            st = Steps(e, S("dve_bn"))
            for t in range(T):
                r = ring[t % 4]
                e.wait_ge(S(f"gathered{t % 4}"), 32 * (t // 4) + 32)
                st.done(e.scalar_tensor_tensor(X4[:, t, :], r[:, 0, :], gate[:, 0, t:t + 1], X4[:, t, :],
                                               ALU.mult, ALU.add))
                e.scalar_tensor_tensor(X4[:, t, :], r[:, 1, :], gate[:, 1, t:t + 1], X4[:, t, :],
                                       ALU.mult, ALU.add).then_inc(S("combined"), 1)
                if t % SPLIT == SPLIT - 1:
                    b = slice(t + 1 - SPLIT, t + 1)
                    st.done(e.tensor_tensor(X[:, b, :], X[:, b, :],
                                            bc["bet"][:, :].unsqueeze(1).to_broadcast([P, SPLIT, F]), ALU.add))
            e.wait_ge(S("combined"), T)
            e.wait_ge(S("bn_summed"), 1)
            st.done(e.tensor_scalar(G[:, :], psum[:, 0, 0:F], 1.0 / N, None, ALU.mult))
            for t in range(T):
                e.tensor_tensor(X4[:, t, :], X4[:, t, :], G[:, :], ALU.subtract).then_inc(S("centred"), 1)
            e.wait_ge(S("centred"), T)
            e.wait_ge(S("bn_summed"), 2)
            halves = [P, KF, P]
            diagonal = identF[:, :].unsqueeze(1).to_broadcast(halves)
            V3, G3 = [m[:, :].rearrange("p (k c) -> p k c", k=KF) for m in (V, G2)]
            st.done(e.tensor_scalar(V[:, :], psum[:, 1, 0:F], 1.0 / N, EPS, ALU.mult, ALU.add))
            st.done(e.tensor_tensor(V3, V3, diagonal, ALU.mult))
            e.tensor_reduce(bn_r[:, 0:KF], V3, AX.X, ALU.add).then_inc(S("bn_var"), 1)
            e.wait_ge(S("bn_rstd"), 1)
            e.tensor_tensor(G3, diagonal, bn_r[:, 0:KF].unsqueeze(2).to_broadcast(halves), ALU.mult)\
                .then_inc(S("bn_diagonal"), 1)
            e.wait_ge(S("bn_spread"), 1)
            st.done(e.tensor_tensor(U[:, :], psum[:, 2, 0:F], bc["gam"][:, :], ALU.mult))
            phase_end(e, "combine")
            stf = Steps(e, S("dve_out"))
            for g in range(T // SPLIT + 1):
                if g < T // SPLIT:
                    b = slice(g * SPLIT, (g + 1) * SPLIT)
                    stf.done(e.tensor_tensor(X4[:, b, :], X4[:, b, :],
                                             U[:, :].unsqueeze(1).to_broadcast([P, SPLIT, F]), ALU.mult))
                    stf.done(e.tensor_tensor(X4[:, b, :], X4[:, b, :], X[:, b, :], ALU.add))
                    for t in range(g * SPLIT, (g + 1) * SPLIT):
                        e.bn_stats(out_stats[:, t, :], X4[:, t, :]).then_inc(S("out_statted"), 1)
                    for t in range(g * SPLIT, (g + 1) * SPLIT):
                        e.wait_ge(S("out_statted"), t + 1)
                        e.bn_aggr(out_mv[:, t, :], out_stats[:, t, :]).then_inc(S("out_moments"), 1)
                if g:
                    e.wait_ge(S("out_moments"), g * SPLIT)
                    e.wait_ge(S("out_rstd"), g)
                    for t in range((g - 1) * SPLIT, g * SPLIT):
                        e.tensor_scalar(X4[:, t, :], X4[:, t, :], out_mv[:, t, 0:1], out_r[:, t:t + 1],
                                        ALU.subtract, ALU.mult).then_inc(S("out_made"), 1)

        def pool_moe(e):
            phase_end(e, "l3")
            for k in range(TOP):
                e.wait_ge(S("slots_ready"), k + 1)
                for t in range(T):
                    e.indirect_dma_start(out=xbuf, out_offset=bass.IndirectOffsetOnAxis(ap=slot_to[:, k, t:t + 1], axis=0),
                                         in_=X4[:, t, :], in_offset=None).then_inc(S("rows_scattered"), 16)
            e.wait_ge(S("rows_scattered"), 16 * TOP * T)
            phase_end(e, "route")
            turns = e.value_load(nturn[0:1, 0:1], min_val=1, max_val=MAXCH // RING)
            with e.Fori(0, turns) as j:
                for n in range(RING):
                    c, par = RING * j + n, n % 2
                    e.wait_ge(S("chunk_made"), c + 3)
                    e.dma_start(ybuf[bass.ds(c * P, P), :], yout[n]).then_inc(S(f"rows_stored{n}"), 16)
            for n in range(RING):
                e.wait_ge(S(f"rows_stored{n}"), 16 * turns)
            carry_wait(e)
            phase_end(e, "experts")
            for t in range(T):
                if t >= 4:
                    e.wait_ge(S("combined"), t - 3)
                for k in range(TOP):
                    e.indirect_dma_start(out=ring[t % 4][:, k, :], out_offset=None, in_=ybuf,
                                         in_offset=bass.IndirectOffsetOnAxis(ap=slot_from[:, k, t:t + 1], axis=0))\
                        .then_inc(S(f"gathered{t % 4}"), 16)
            e.wait_ge(S("bn_var"), 1)
            e.tensor_tensor(bn_r[:, 0:KF], bn_r[:, 0:KF], mhalf[:, 0:KF], ALU.pow).then_inc(S("bn_rstd"), 1)
            phase_end(e, "combine")

            for g in range(T // SPLIT):
                b = slice(g * SPLIT, (g + 1) * SPLIT)
                e.wait_ge(S("out_moments"), (g + 1) * SPLIT)
                e.tensor_scalar(out_r[:, b], out_mv[:, b, 1], EPS, None, ALU.add).then_inc(S("out_eps"), 1)
                e.wait_ge(S("out_eps"), g + 1)
                e.tensor_tensor(out_r[:, b], out_r[:, b], mhalf[:, b], ALU.pow).then_inc(S("out_rstd"), 1)

        @block.sync
        def _(e):
            ld = S("inputs_loaded")
            n = [0]

            def load(o, i):
                e.dma_start(o, i).then_inc(ld, 16)
                n[0] += 16

            full = EC - 1
            e.wait_ge(S("pads_set"), 1)
            for rows, a in ((src_rows_i, src), (dst_rows_i, dst)):
                r = rows.rearrange("c (g e) -> c g e", g=EG)
                load(r[:, 0:EG - 1, :], a[0:(EG - 1) * P * P].rearrange("(g c e) -> c g e", g=EG - 1, c=P))
                k = full - (EG - 1) * P
                load(r[0:k, EG - 1, :], a[(EG - 1) * P * P:full * P].rearrange("(c e) -> c e", e=P))
                load(r[k:k + 1, EG - 1, 0:E - full * P], a[full * P:E].rearrange("(c e) -> c e", c=1))
            e.wait_ge(ld, n[0])
            e.sem_inc(S("edges_loaded"), 1)
            e.wait_ge(S("pads_set"), 2)
            load(X[:, 0:T - 1, :], x[0:(T - 1) * P, :].rearrange("(t p) f -> p t f", p=P))
            load(X[0:LAST, T - 1, :], x[(T - 1) * P:N, :])
            for w, k in ((wl0, "L0_gnn_weight"), (wcv, "L1_gnn_W_conv"), (wh1, "L2_gnn_W1"), (wh2, "L2_gnn_W2"),
                         (wgc, "L3_gnn_W_gc"), (wrs, "L3_gnn_W_res"), (wgt, "L3_gnn_Wg")):
                load(w[:, :, :], A[k].rearrange("(k p) f -> p k f", p=P))
            for w, k in ((wln, "L1_gnn_W_lin"), (wd1, "L1_gnn_W_dec1"), (wd2, "L1_gnn_W_dec2")):
                load(w[:, :], A[k])
            for w, k in (("l0", "L0_gnn_bias"), ("dec2", "L1_gnn_b_dec2"), ("h1", "L2_gnn_b1"), ("h2", "L2_gnn_b2"),
                         ("gc", "L3_gnn_b_gc"), ("res", "L3_gnn_b_res"), ("gam", "L3_gnn_gamma"),
                         ("bet", "L3_gnn_beta")):
                load(bc[w][:, :], A[k].rearrange("(a f) -> a f", a=1).to_broadcast([P, F]))
            load(b1rows[:, :], A["L3_gnn_b1"])
            load(bgb[:, :], A["L3_gnn_bg"].rearrange("(a f) -> a f", a=1).to_broadcast([P, NE]))
            load(col["conv"][:, :], A["L1_gnn_b_conv"].rearrange("(p a) -> p a", a=1))
            load(col["lin"][0:HL, :], A["L1_gnn_b_lin"].rearrange("(p a) -> p a", a=1))
            load(col["dec1"][:, :], A["L1_gnn_b_dec1"].rearrange("(p a) -> p a", a=1))
            load(col["a"][:, :], A["L2_gnn_a"].rearrange("(p a) -> p a", a=1).to_broadcast([P, 1]))
            phase_end(e, "load")
            phase_end(e, "table")
            e.wait_ge(ld, n[0])
            e.wait_ge(S("zeros_set"), 1)
            zeros = X4[:, :, :].rearrange("p t f -> p (t f)")[:, 0:ZROWS * F].rearrange("p (k f) -> p k f", f=F)
            for buf in (xbuf, ybuf):
                with e.Fori(0, NCH // ZROWS) as g:
                    e.dma_start(buf[bass.ds(g * ZROWS * P, ZROWS * P), :].rearrange("(p k) f -> p k f", p=P),
                                zeros).then_inc(S("rows_zeroed"), 16)
            e.wait_ge(S("rows_zeroed"), 2 * 16 * (NCH // ZROWS))

            def store_rows(i, par):
                e.wait_ge(S("field0_cast"), i + 1)
                e.wait_ge(S("fields_cast"), 3 * i + 3)
                e.dma_start(a_rev[:, :, bass.ds(i * P, P)].rearrange("s p c -> p s c"),
                            band_rows[par].rearrange("p (s c) -> p s c", c=P)).then_inc(S(f"rows_stored_{par}"), 16)

            def store_cols(i, par):
                e.wait_ge(S("band_turned"), ROUNDS * (i + 1) + 1)
                e.dma_start(a_fwd[bass.ds(i, 1), :, :].rearrange("a p c -> p (a c)"), band_cols[par])\
                    .then_inc(S(f"cols_stored_{par}"), 16)
            pipeline(e, [(1, store_rows), (2, store_cols)])
            for par in range(2):
                e.wait_ge(S(f"rows_stored_{par}"), 16 * (T // 2 + 1 - par))
                e.wait_ge(S(f"cols_stored_{par}"), 16 * (T // 2 + 1 - par))
            phase_end(e, "counts")
            phase_end(e, "checked")
            is_heavy = e.value_load(heavy[0:1, 0:1], min_val=0, max_val=1)
            with e.If(is_heavy > 0):
                with e.Fori(0, T) as b:
                    e.wait_ge(S("rest_turned"), 2 * ROUNDS * (b + 1))
                    for n, (rev, fwd) in enumerate(((a_rev, a_fwd), (a_rev2, a_fwd2))):
                        e.dma_start(rev[:, :, bass.ds(b * P, P)].rearrange("s p c -> p s c"),
                                    band_rows[n].rearrange("p (s c) -> p s c", c=P)).then_inc(S("rest_stored"), 16)
                        e.dma_start(fwd[bass.ds(b, 1), :, :].rearrange("a p c -> p (a c)"), band_cols[n])\
                            .then_inc(S("rest_stored"), 16)
                e.wait_ge(S("rest_stored"), 64 * T)
            phase_end(e, "rests")
            phase_end(e, "split")

            def blocks(ph, mat, mat2):
                def load_block(i, par):
                    e.dma_start(blk[par][:, :], mat[bass.ds(i, 1), :, :].rearrange("a p c -> p (a c)"))\
                        .then_inc(S(f"block_in{par}"), 16)
                    with e.If(is_heavy > 0):
                        e.wait_ge(S("rest_used"), past(ph, "summed") + i)
                        e.dma_start(rblk[:, :], mat2[bass.ds(i, 1), :, :].rearrange("a p c -> p (a c)"))\
                            .then_inc(S("rest_in"), 16)

                load_block(0, 0)
                load_block(1, 1)
                with e.Fori(1, T // 2) as j:
                    for par in range(2):
                        e.wait_ge(S("tile_summed"), past(ph, "summed") + 2 * j + par - 1)
                        load_block(2 * j + par, par)
                e.wait_ge(S("tile_summed"), past(ph, "summed") + T - 2)
                load_block(T - 1, 0)
                phase_end(e, ph)

            blocks("l0", a_fwd, a_fwd2)
            blocks("l1", a_fwd, a_fwd2)
            blocks("h1a", a_fwd, a_fwd2)
            blocks("h1b", a_rev, a_rev2)
            blocks("h2a", a_fwd, a_fwd2)
            blocks("h2b", a_rev, a_rev2)
            blocks("l3", a_fwd, a_fwd2)
            sync_moe(e)

        @block.tensor
        def _(e):
            phase_end(e, "load")
            e.wait_ge(S("rows_float"), 2)
            e.wait_ge(S("ident_set"), 2)
            for g in range(EG):
                e.transpose(psum[:, 0, g * P:(g + 1) * P], src_rows[:, g * P:(g + 1) * P], identF[:, :])
                mm = e.transpose(psum[:, 1, g * P:(g + 1) * P], dst_rows[:, g * P:(g + 1) * P], identF[:, :])
            mm.then_inc(S("edges_turned"), 1)
            e.wait_ge(S("chunk_ends"), 2)
            for g in range(EG):
                e.matmul(psum[0:32, 2, g * P:(g + 1) * P], chunk_lo[:, g * 32:(g + 1) * 32], identF[:, :],
                         start=True, stop=True)
                mm = e.matmul(psum[0:32, 3, g * P:(g + 1) * P], chunk_hi[:, g * 32:(g + 1) * 32], identF[:, :],
                              start=True, stop=True)
            mm.then_inc(S("chunk_rows"), 1)
            e.wait_ge(S("band_cols_ready"), 2)
            for k in range(2):
                mm = e.transpose(psum[0:1, 4, k * 32:(k + 1) * 32], bandcol[0:32, k:k + 1], identF[0:32, 0:32])
            mm.then_inc(S("band_rows_up"), 1)
            phase_end(e, "table")

            psb = psum[:, :, :].rearrange("p b c -> p (b c)").bitcast(BF16).rearrange("p (b c) -> p b c", b=8)
            cuts = [(o, min(BANK, FW + 1 - o)) for o in range(0, FW + 1, BANK)]

            def chunks(b, par):
                before = e.value_load(tab[0:1, 1, bass.ds(b, 1)], min_val=0, max_val=T * EC)
                upto = e.value_load(tab[0:1, 2, bass.ds(b, 1)], min_val=1, max_val=T * EC)
                if not (isinstance(b, int) and b < 2):
                    e.wait_ge(S("words_read"), b - 1)
                for q, (o, w) in enumerate(cuts):
                    e.matmul(psum[:, 3 * par + q, 0:w], zrow[:, 0:P], zrow[:, 0:w], start=True, stop=True)
                with e.Fori(before, upto) as g:
                    for u in range(UNROLL):
                        e.wait_ge(S("onehots_ready"), 2 * (UNROLL * g + u) + 2)
                        for q, (o, w) in enumerate(cuts):
                            mm = e.matmul(psum[:, 3 * par + q, 0:w], one_d[:, u, :], one_s[:, u, o:o + w],
                                          start=False, stop=True, skip_group_check=True)
                        mm.then_inc(S("onehots_used"), 1)
                e.matmul(psum[:, 3 * par + 2, BANK - 1:BANK], zrow[:, 0:P], zrow[:, 0:1], start=True, stop=True)\
                    .then_inc(S("band_summed"), 1)

            def turn_rounds(lo, hi):
                def do(b, par):
                    if lo == 0:
                        e.wait_ge(S("field0_cast"), b + 1)
                        e.wait_ge(S("fields_cast"), 3 * b + 3)
                    for r in range(lo, hi):
                        e.wait_ge(S("band_turned"), ROUNDS * b + r)
                        for t in range(r * ROUND, min(T, (r + 1) * ROUND)):
                            o = (t - r * ROUND) * P
                            v = band_rows[par][:, t * P:(t + 1) * P]
                            e.matmul(psum[:, 6 + r % 2, 448 + t:449 + t], v, onesB[:, 0:1], start=True, stop=True)
                            mm = e.transpose(psb[:, 6 + r % 2, o:o + P], v, identB[:, :])
                        mm.then_inc(S("band_transposed"), 1)
                return do

            def band(it, par, side, known):
                if side:
                    side[0]()
                if not (known and it(0) >= T):
                    chunks(it(0), par)
                if side:
                    side[1]()
            pipeline(e, [(2, turn_rounds(0, 2)), (2, turn_rounds(2, ROUNDS))], band)
            phase_end(e, "counts")
            e.wait_ge(S("degrees_summed"), 1)
            e.matmul(psum[:, 0, 0:2], ones[:, :], totals[:, :], start=True, stop=True).then_inc(S("edges_summed"), 1)
            phase_end(e, "checked")
            is_heavy = e.value_load(heavy[0:1, 0:1], min_val=0, max_val=1)
            with e.If(is_heavy > 0):
                with e.Fori(0, T) as b:
                    before = e.value_load(tab[0:1, 1, bass.ds(b, 1)], min_val=0, max_val=T * EC)
                    upto = e.value_load(tab[0:1, 2, bass.ds(b, 1)], min_val=1, max_val=T * EC)
                    e.wait_ge(S("rest_turned"), 2 * ROUNDS * b)
                    e.wait_ge(S("rest_degrees"), b)
                    for q in range(NB):
                        w = min(BANK, NP - q * BANK)
                        e.matmul(psum[:, q, 0:w], zrow[:, 0:P], zrow[:, 0:w], start=True, stop=True)
                    with e.Fori(UNROLL * before, UNROLL * upto) as k:
                        e.wait_ge(S("wide_ready"), 4 * k + 4)
                        for q in range(NB):
                            w = min(BANK, NP - q * BANK)
                            mm = e.matmul(psum[:, q, 0:w], one_d[:, 0, :], wide_s[:, q * BANK:q * BANK + w],
                                          start=False, stop=True, skip_group_check=True)
                        mm.then_inc(S("wide_used"), 1)
                    e.matmul(psum[:, 7, 0:T], zrow[:, 0:P], zrow[:, 0:T], start=True, stop=True)\
                        .then_inc(S("wide_summed"), 1)
                    e.wait_ge(S("plane1_made"), b + 1)
                    for n in range(2):
                        for r in range(ROUNDS):
                            e.wait_ge(S("rest_turned"), 2 * ROUNDS * b + ROUNDS * n + r)
                            for t in range(r * ROUND, min(T, (r + 1) * ROUND)):
                                v = band_rows[n][:, t * P:(t + 1) * P]
                                e.matmul(psum[:, 7, t:t + 1], v, onesB[:, 0:1], start=False, stop=True,
                                         skip_group_check=True)
                                mm = e.transpose(psb[:, 0, (t - r * ROUND) * P:(t - r * ROUND + 1) * P], v,
                                                 identB[:, :])
                            mm.then_inc(S("rest_transposed"), 1)
            phase_end(e, "rests")
            phase_end(e, "split")

            def aggregate(ph, XS, Fw, own, steps):
                def add(i, par, side):
                    e.wait_ge(S(f"block_in{par}"), 16 * past_blocks(ph, par) + 8 * (i - par) + 16)
                    if isinstance(i, int) and i < 2:
                        pass
                    else:
                        e.wait_ge(S("tile_sum_read"), past(ph, "sum_read") + i - 1)
                    o = agg[par][:, 0:Fw]
                    gap = min(8, (T - 1) // max(len(side), 1))
                    for k in range(T):
                        for s in range(PARTS):
                            mm = e.matmul(o, blk[par][:, k * P:(k + 1) * P], XS[:, k, s, 0:Fw],
                                          start=(k == 0 and s == 0), stop=False)
                        if k % gap == gap - 1 and k // gap < len(side) and k < T - 1:
                            side[k // gap]()
                    with e.If(is_heavy > 0):
                        e.wait_ge(S("rest_in"), 16 * past(ph, "summed") + 16 * i + 16)
                        carry_wait(e)
                        with e.Fori(0, T) as k:
                            for s in range(PARTS):
                                e.matmul(o, rblk[:, bass.ds(k * P, P)],
                                         XS[:, bass.ds(k, 1), s, 0:Fw].rearrange("p a f -> p (a f)"),
                                         start=False, stop=False, skip_group_check=True)
                        e.matmul(o, zrow[:, 0:P], zrow[:, 0:Fw], start=False, stop=False,
                                 skip_group_check=True).then_inc(S("rest_used"), 1)
                    if not own:
                        mm = e.matmul(o, zrow[:, 0:P], zrow[:, 0:Fw], start=False, stop=True)
                    if own:
                        for s in range(PARTS):
                            mm = e.matmul(o, identB[:, :],
                                          XS[:, bass.ds(i, 1), s, 0:Fw].rearrange("p a f -> p (a f)"),
                                          start=False, stop=(s == PARTS - 1))
                    mm.then_inc(S("tile_summed"), 1)

                def whole(it, par, side, known):
                    if known and it(0) >= T:
                        for f in side:
                            f()
                    else:
                        add(it(0), par, side)

                pipeline(e, [(lag, f) for lag, f in steps] or [(0, lambda i, par: None)], whole)
                phase_end(e, ph)

            def turn(ph, need, sig, o, a, nt):
                def step(i, par):
                    e.wait_ge(S("tile_" + need), past(ph, need) + i + 1)
                    v = a[par] if isinstance(a, list) else a
                    for k in range(nt):
                        mm = e.transpose(o[:, k * P:(k + 1) * P], v[:, k * P:(k + 1) * P], identF[:, :])
                    mm.then_inc(S("tile_" + sig), 1)
                return step

            def dense(ph, need, sig, o, pairs):
                def step(i, par):
                    for nd in need:
                        e.wait_ge(S("tile_" + nd), past(ph, nd) + i + 1)
                    v = o[par] if isinstance(o, list) else o
                    if ph == "l1" and sig == "pre":
                        e.wait_ge(S("tile_moments"), past(ph, "moments") + i)
                    for n_, (l, r) in enumerate(pairs):
                        mm = e.matmul(v, l, r, start=(n_ == 0), stop=(n_ == len(pairs) - 1))
                    mm.then_inc(S("tile_" + sig), 1)
                return step

            def two(t, w):
                return [(t[:, k, :], w[:, k, :]) for k in range(KF)]

            aggregate("l0", XSa, F, False, [
                (1, turn("l0", "sum_read", "g_turned", pT, G, KF)),
                (3, turn("l0", "normed", "x_turned", pT2, Xn, KF)),
                (1, dense("l0", ["gT"], "pre", pD, two(tT, wl0))),
                (3, dense("l0", ["xT"], "proj", [o[:, 0:HC] for o in pD2], two(tT2, wcv)))])
            aggregate("l1", XSb, HC, True, [
                (2, dense("l1", ["zT"], "dec", pdec, [(wd1[:, :], G2[0:HL, 0:P])])),
                (1, turn("l1", "sum_read", "g_turned", pT, G, 1)),
                (4, turn("l1", "normed", "x_turned", pT2, Xn, KF)),
                (2, dense("l1", ["dT"], "pre", pD[0], [(tT[:, 1, :], wd2[:, :])])),
                (1, dense("l1", ["gT"], "lin", plin, [(wln[:, :], tT[:, 0, :])])),
                (4, dense("l1", ["xT"], "proj", pD2, two(tT2, wh1)))])
            aggregate("h1a", XSa, F, False, [])
            aggregate("h1b", XSb, F, False, [
                (1, turn("h1b", "active", "g_turned", pT, G, KF)),
                (1, dense("h1b", ["gT"], "proj", pD2, two(tT, wh2)))])
            aggregate("h2a", XSa, F, False, [])
            aggregate("h2b", XSb, F, False, [])
            aggregate("l3", XSa, F, False, [
                (1, turn("l3", "own_copied", "x_turned", pT2, Xn, KF)),
                (1, turn("l3", "sum_read", "g_turned", pT, G, KF)),
                (2, turn("l3", "x4_made", "x4_turned", px4, V, KF)),
                (1, dense("l3", ["xT", "gT"], "pre", pD[0], two(tT, wgc) + two(tT2, wrs))),
                (2, dense("l3", ["x4T"], "logits", [o[:, 0:NE] for o in pD2], two(tT3, wgt)))])
            pe_moe(e)

        @block.scalar
        def _(e):
            phase_end(e, "load")
            phase_end(e, "table")
            psb = psum[:, :, :].rearrange("p b c -> p (b c)").bitcast(BF16).rearrange("p (b c) -> p b c", b=8)
            psf = psum[:, :, :].rearrange("p b c -> p (b c)")

            def unpack(b, par):
                e.wait_ge(S("band_summed"), b + 1)
                e.wait_ge(S("fields_cast"), 3 * b)
                e.activation(words[:, 0:FW + 1], psf[:, 3 * par * BANK:3 * par * BANK + FW + 1], ACT.Copy)\
                    .then_inc(S("words_read"), 1)
                e.wait_ge(S("words_read"), b + 1)
                if not (isinstance(b, int) and b < 1):
                    e.wait_ge(S("band_transposed"), ROUNDS * (b - 1))
                e.wait_ge(S(f"rows_stored_{par}"), 8 * (b - par))
                e.activation(band_rows[par][:, 0:FW], field(0, FW), ACT.Copy).then_inc(S("field0_cast"), 1)

            def out_rounds(lo, hi):
                def do(b, par):
                    if lo == 0:
                        e.wait_ge(S(f"cols_stored_{par}"), 8 * (b - par))
                    for r in range(lo, hi):
                        n = min(T, (r + 1) * ROUND) - r * ROUND
                        e.wait_ge(S("band_transposed"), ROUNDS * b + r + 1)
                        e.activation(outdeg_by[:, bass.ds(b, 1), r * ROUND:r * ROUND + n]
                                     .rearrange("p a t -> p (a t)"),
                                     psum[:, 6 + r % 2, 448 + r * ROUND:448 + r * ROUND + n], ACT.Copy)
                        e.activation(band_cols[par][:, r * ROUND * P:(r * ROUND + n) * P],
                                     psb[:, 6 + r % 2, 0:n * P], ACT.Copy).then_inc(S("band_turned"), 1)
                return do
            pipeline(e, [(2, out_rounds(0, 2)), (1, unpack), (2, out_rounds(2, ROUNDS))])
            phase_end(e, "counts")
            phase_end(e, "checked")
            is_heavy = e.value_load(heavy[0:1, 0:1], min_val=0, max_val=1)
            with e.If(is_heavy > 0):
                with e.Fori(0, T) as b:
                    e.wait_ge(S("rest_stored"), 64 * b)
                    e.wait_ge(S("wide_summed"), b + 1)
                    e.activation(band_rows[0], psf[:, 0:NP], ACT.Copy).then_inc(S("plane0_made"), 1)
                    for n in range(2):
                        for r in range(ROUNDS):
                            w = (min(T, (r + 1) * ROUND) - r * ROUND) * P
                            e.wait_ge(S("rest_transposed"), 2 * ROUNDS * b + ROUNDS * n + r + 1)
                            e.activation(band_cols[n][:, r * ROUND * P:r * ROUND * P + w], psb[:, 0, 0:w], ACT.Copy)\
                                .then_inc(S("rest_turned"), 1)
                    e.activation(outdeg_by[:, bass.ds(b, 1), :].rearrange("p a t -> p (a t)"), psum[:, 7, 0:T],
                                 ACT.Copy).then_inc(S("rest_degrees"), 1)
            phase_end(e, "rests")

            def pick(v, par):
                return v[par] if isinstance(v, list) else v

            def split_a(ph, need, a, XS, w):
                def do(i, par):
                    e.wait_ge(S("tile_" + need), past(ph, need) + i + 1)
                    e.activation(XS[:, bass.ds(i, 1), 0, 0:w].rearrange("p a f -> p (a f)"), pick(a, par), ACT.Copy)\
                        .then_inc(S("tile_part0"), 1)
                    e.wait_ge(S("tile_rest"), past(ph, "rest") + i + 1)
                    e.activation(XS[:, bass.ds(i, 1), 1, 0:w].rearrange("p a f -> p (a f)"), R1[:, 0:w], ACT.Copy)\
                        .then_inc(S("tile_part1"), 1)
                return do

            def copy(ph, need, sig, o, a, func=ACT.Copy, **kw):
                def do(i, par):
                    e.wait_ge(S("tile_" + need), past(ph, need) + i + 1)
                    e.activation(o, pick(a, par), func, **kw).then_inc(S("tile_" + sig), 1)
                return do

            def run(ph, stages):
                pipeline(e, stages)
                phase_end(e, ph)

            def flat(t):
                return t[:, :, :].rearrange("p k c -> p (k c)")

            for g in range(T // SPLIT + 1):
                if g < T // SPLIT:
                    b = slice(g * SPLIT, (g + 1) * SPLIT)
                    e.wait_ge(S("tile_scaled"), (g + 1) * SPLIT)
                    e.activation(XSa[:, b, 0, :], X4[:, b, :], ACT.Copy).then_inc(S("tile_part0"), SPLIT)
                if g >= 1:
                    b = slice((g - 1) * SPLIT, g * SPLIT)
                    e.wait_ge(S("tile_rest"), g * SPLIT)
                    e.activation(XSa[:, b, 1, :], X4[:, b, :], ACT.Copy).then_inc(S("tile_part1"), SPLIT)
            phase_end(e, "split")
            run("l0", [(1, copy("l0", "g_turned", "gT", flat(tT), pT)),
                       (3, copy("l0", "x_turned", "xT", flat(tT2), pT2)),
                       (2, copy("l0", "negative", "exped", G2[:, :], U[:, :], ACT.Exp)),
                       (4, split_a("l0", "scaled", V2[:, 0:HC], XSb, HC))])
            run("l1", [(2, copy("l1", "lin", "zT", G2[0:HL, 0:P], plin, ACT.Identity, bias=col["lin"][0:HL, :])),
                       (1, copy("l1", "g_turned", "gT", tT[:, 0, :], pT[:, 0:P], ACT.Relu, bias=col["conv"][:, :])),
                       (2, copy("l1", "dec", "dT", tT[:, 1, :], pdec, ACT.Relu, bias=col["dec1"][:, :])),
                       (4, copy("l1", "x_turned", "xT", flat(tT2), pT2)),
                       (5, split_a("l1", "proj", pD2, XSa, F))])
            run("h1a", [(1, split_a("h1a", "sum_read", G[:, :], XSb, F))])
            run("h1b", [(2, split_a("h1b", "proj", pD2, XSa, F)),
                        (1, copy("h1b", "g_turned", "gT", flat(tT), pT))])
            run("h2a", [(1, split_a("h2a", "sum_read", G[:, :], XSb, F))])
            run("h2b", [(1, split_a("h2b", "scaled", G2[:, :], XSa, F))])
            run("l3", [(1, copy("l3", "x_turned", "xT", flat(tT2), pT2)),
                       (1, copy("l3", "g_turned", "gT", flat(tT), pT)),
                       (2, copy("l3", "x4_turned", "x4T", flat(tT3), px4))])
            act_moe(e)

        @block.vector
        def _(e):
            st = Steps(e, S("dve_setup"))
            st.done(e.memset(src_rows_i, FAR))
            st.done(e.memset(dst_rows_i, FAR))
            e.sem_inc(S("pads_set"), 1)
            st.done(e.memset(X[:, T - 1, :], 0.0))
            e.sem_inc(S("pads_set"), 1)
            e.memset(zrow[:, :], 0.0)
            e.memset(mhalf[:, :], -0.5)
            e.memset(ones[:, :], 1.0)
            e.memset(onesB[:, :], 1.0)
            e.wait_ge(S("edges_loaded"), 1)
            e.tensor_copy(src_rows, src_rows_i).then_inc(S("rows_float"), 1)
            e.tensor_copy(dst_rows, dst_rows_i).then_inc(S("rows_float"), 1)
            e.wait_ge(S("rows_float"), 2)
            phase_end(e, "load")
            ends = scr1[:, 0:2 * EG]
            d3 = dst_rows.rearrange("c (g e) -> c g e", g=EG)
            st.done(e.tensor_reduce(ends[:, 0:EG], d3, AX.X, ALU.min))
            st.done(e.tensor_reduce(ends[:, EG:2 * EG], d3, AX.X, ALU.max))
            e.tensor_copy(chunk_lo.rearrange("p (g b) -> p g b", g=EG),
                          ends[:, 0:EG].unsqueeze(2).to_broadcast([P, EG, 32])).then_inc(S("chunk_ends"), 1)
            e.tensor_copy(chunk_hi.rearrange("p (g b) -> p g b", g=EG),
                          ends[:, EG:2 * EG].unsqueeze(2).to_broadcast([P, EG, 32])).then_inc(S("chunk_ends"), 1)
            e.wait_ge(S("edges_turned"), 1)
            for n in range(1, FIELDS):
                st.done(e.tensor_scalar(fcol[n], psum[:, 0, 0:EG * P], float(n * FW), None, ALU.is_ge))
            st.done(e.tensor_tensor(fcol[0], fcol[1], fcol[2], ALU.add))
            st.done(e.scalar_tensor_tensor(scol, fcol[0], float(-FW), psum[:, 0, 0:EG * P], ALU.mult, ALU.add))
            st.done(e.tensor_scalar(wcol, fcol[1], 255.0, 1.0, ALU.mult, ALU.add))
            st.done(e.scalar_tensor_tensor(wcol, fcol[2], 65280.0, wcol, ALU.mult, ALU.add))
            st.done(e.tensor_scalar(fcol[0], fcol[1], -1.0, 1.0, ALU.mult, ALU.add))
            st.done(e.tensor_tensor(fcol[1], fcol[1], fcol[2], ALU.subtract))
            st.done(e.tensor_scalar(dcol, psum[:, 1, 0:EG * P], float(P), None, ALU.add))
            e.wait_ge(S("chunk_rows"), 1)
            e.wait_ge(S("iotas_set"), 4)
            e.wait_ge(S("chunk_ends"), 2)
            B = slice(0, 32)
            st.done(e.tensor_scalar(in_band[B, :], psum[B, 2, :], bandcol[B, 3:4], None, ALU.is_le))
            st.done(e.scalar_tensor_tensor(in_band[B, :], psum[B, 3, :], bandcol[B, 2:3], in_band[B, :],
                                           ALU.is_ge, ALU.mult))
            BIG = float(EG * P)
            st.done(e.scalar_tensor_tensor(scr1[B, :], chunk_id[B, :], 1.0, in_band[B, :], ALU.add, ALU.mult))
            st.done(e.tensor_reduce(bandcol[B, 5:6], scr1[B, :], AX.X, ALU.max))
            st.done(e.scalar_tensor_tensor(scr1[B, :], chunk_id[B, :], -BIG, in_band[B, :], ALU.add, ALU.mult))
            st.done(e.tensor_reduce(bandcol[B, 4:5], scr1[B, :], AX.X, ALU.min))
            e.tensor_scalar(bandcol[B, 0:1], bandcol[B, 4:5], BIG, float(EC - 1), ALU.add, ALU.min)\
                .then_inc(S("band_cols_ready"), 1)
            e.wait_ge(S("band_cols_ready"), 1)
            st.done(e.tensor_scalar(bandcol[B, 6:7], bandcol[B, 0:1], 1.0, None, ALU.add))
            e.tensor_tensor(bandcol[B, 1:2], bandcol[B, 5:6], bandcol[B, 6:7], ALU.max)\
                .then_inc(S("band_cols_ready"), 1)
            e.wait_ge(S("band_rows_up"), 1)
            br = bandrow[0:1, :]
            st.done(e.tensor_copy(br[:, 0:64], psum[0:1, 4, 0:64]))
            st.done(e.tensor_tensor(scr1[0:1, 0:32], br[:, 32:64], br[:, 0:32], ALU.subtract))
            groups = words[0:1, 0:32]
            st.done(e.tensor_scalar(groups, scr1[0:1, 0:32], float(UNROLL - 1), None, ALU.add))
            st.done(e.tensor_scalar(groups, groups, UNROLL.bit_length() - 1, None, ALU.arith_shift_right))
            st.done(e.tensor_copy(scr1[0:1, 0:32], groups))
            st.done(e.memset(br[:, 96:128], 1.0))
            st.done(e.tensor_tensor_scan(br[:, 64:96], br[:, 96:128], scr1[0:1, 0:32], 0.0, ALU.mult, ALU.add))
            st.done(e.tensor_tensor(br[:, 32:64], br[:, 64:96], scr1[0:1, 0:32], ALU.subtract))
            st.done(e.memset(one_s[:, :, FW:FW + 1], 1.0))
            st.done(e.tensor_copy(tab[:, :, :].rearrange("a k b -> a (k b)"), br[:, 0:96]))
            phase_end(e, "table")

            def chunk_loop(b, one):
                first = e.value_load(tab[0:1, 0, bass.ds(b, 1)], min_val=0, max_val=EC - 1)
                before = e.value_load(tab[0:1, 1, bass.ds(b, 1)], min_val=0, max_val=T * EC)
                upto = e.value_load(tab[0:1, 2, bass.ds(b, 1)], min_val=1, max_val=T * EC)
                with e.Fori(before, upto) as g:
                    for u in range(UNROLL):
                        c = nc.s_assert_within(first + UNROLL * (g - before) + u, 0, EC + UNROLL - 2,
                                               skip_runtime_bounds_check_because="g runs from before to upto")
                        one(UNROLL * g + u, u, c)
                return upto

            def packed(k, u, c):
                e.wait_ge(S("onehots_used"), k + 1)
                e.tensor_scalar(one_d[:, u, :], iota_p,
                                dcol[:, bass.ds(c, 1)], None, ALU.is_equal).then_inc(S("onehots_ready"), 1)
                e.tensor_scalar(one_s[:, u, 0:FW], iota_f,
                                scol[:, bass.ds(c, 1)], wcol[:, bass.ds(c, 1)], ALU.is_equal, ALU.mult)\
                    .then_inc(S("onehots_ready"), 1)

            def wide(k, u, c):
                e.wait_ge(S("wide_used"), k)
                e.tensor_scalar(one_d[:, 0, :], iota_p, dcol[:, bass.ds(c, 1)], None, ALU.is_equal)\
                    .then_inc(S("wide_ready"), 1)
                for n in range(FIELDS):
                    e.tensor_scalar(wide_s[:, n * FW:(n + 1) * FW], iota_f, scol[:, bass.ds(c, 1)],
                                    fcol[n][:, bass.ds(c, 1)], ALU.is_equal, ALU.mult).then_inc(S("wide_ready"), 1)

            with e.Fori(0, T) as b:
                e.tensor_scalar(dcol, dcol, float(-P), None, ALU.add).then_inc(S("band_shifted"), 1)
                e.wait_ge(S("band_shifted"), b + 1)
                carry_wait(e)
                done = chunk_loop(b, packed)
                e.wait_ge(S("onehots_ready"), 2 * UNROLL * done)
                carry_wait(e)
            phase_end(e, "counts")

            def sum_outdeg():
                st.done(e.tensor_reduce(outdeg[:, :], outdeg_by[:, :, :].rearrange("p b t -> p t b"), AX.X, ALU.add))

            sum_outdeg()
            st.done(e.tensor_reduce(totals[:, 0:1], outdeg[:, :], AX.X, ALU.add))
            st.done(e.tensor_reduce(totals[:, 1:2], indeg[:, :], AX.X, ALU.add))
            e.sem_inc(S("degrees_summed"), 1)
            e.wait_ge(S("edges_summed"), 1)
            st.done(e.tensor_copy(totals[:, :], psum[:, 0, 0:2]))
            st.done(e.tensor_tensor(heavy[0:1, 0:1], totals[0:1, 0:1], totals[0:1, 1:2], ALU.is_lt))
            phase_end(e, "checked")
            is_heavy = e.value_load(heavy[0:1, 0:1], min_val=0, max_val=1)
            with e.If(is_heavy > 0):
                e.tensor_scalar(dcol, dcol, float(T * P), None, ALU.add).then_inc(S("rest_shifted"), 1)
                e.wait_ge(S("rest_shifted"), 1)
                with e.Fori(0, T) as b:
                    e.tensor_scalar(dcol, dcol, float(-P), None, ALU.add).then_inc(S("rest_shifted"), 1)
                    e.wait_ge(S("rest_shifted"), b + 2)
                    carry_wait(e)
                    chunk_loop(b, wide)
                    e.wait_ge(S("plane0_made"), b + 1)
                    e.tensor_tensor(band_rows[1], psum[:, :, :].rearrange("p b c -> p (b c)")[:, 0:NP], band_rows[0],
                                    ALU.subtract).then_inc(S("plane1_made"), 1)
                    e.wait_ge(S("plane1_made"), b + 1)
            phase_end(e, "rests")
            sum_outdeg()
            st.done(e.tensor_scalar(nsrc[:, :], outdeg[:, :], 1.0, None, ALU.max))
            st.done(e.tensor_scalar(ndst[:, :], indeg[:, :], 1.0, None, ALU.max))
            st.done(e.tensor_scalar(dis[:, :], indeg[:, :], 1.0, None, ALU.add))
            st.done(e.reciprocal(dinv[:, :], nsrc[:, :]))
            st.done(e.reciprocal(binv[:, :], ndst[:, :]))
            e.sem_inc(S("degrees_read"), 1)
            st.done(e.scalar_tensor_tensor(dinv[:, :], outdeg[:, :], 0.5, dinv[:, :], ALU.is_ge, ALU.mult))
            st.done(e.scalar_tensor_tensor(binv[:, :], indeg[:, :], 0.5, binv[:, :], ALU.is_ge, ALU.mult))

            def row(buf, i):
                return buf[:, bass.ds(i, 1), :].rearrange("p a f -> p (a f)")

            def tcol(buf, i):
                return buf[:, bass.ds(i, 1)]

            def split_v(ph, a, XS, w, i):
                e.wait_ge(S("tile_part2"), past(ph, "part2") + i)
                e.wait_ge(S("tile_part0"), past(ph, "part0") + i + 1)
                e.tensor_tensor(R1[:, 0:w], a, XS[:, bass.ds(i, 1), 0, 0:w].rearrange("p a f -> p (a f)"),
                                ALU.subtract).then_inc(S("tile_rest"), 1)
                e.wait_ge(S("tile_part1"), past(ph, "part1") + i + 1)
                e.tensor_tensor(XS[:, bass.ds(i, 1), 2, 0:w].rearrange("p a f -> p (a f)"), R1[:, 0:w],
                                XS[:, bass.ds(i, 1), 1, 0:w].rearrange("p a f -> p (a f)"), ALU.subtract)\
                    .then_inc(S("tile_part2"), 1)

            def read_sum(ph, i, par, w, scale, o=None):
                e.wait_ge(S("tile_summed"), past(ph, "summed") + i + 1)
                e.tensor_scalar((G if o is None else o)[:, 0:w], agg[par][:, 0:w], tcol(scale, i), None, ALU.mult)\
                    .then_inc(S("tile_sum_read"), 1)
                e.wait_ge(S("tile_sum_read"), past(ph, "sum_read") + i + 1)

            def layernorm(ph, st, i, a, o):
                st.done(e.bn_stats(st6[:, :], a))
                carry_wait(e)
                e.bn_aggr(mv[:, :], st6[:, :]).then_inc(S("tile_moments"), 1)
                e.wait_ge(S("tile_moments"), past(ph, "moments") + i + 1)
                e.wait_ge(S("tile_rstd"), past(ph, "rstd") + i + 1)
                e.wait_ge(S("tile_x_kept"), past(ph, "x_kept") + i)
                e.tensor_scalar(o, a, mv[:, 0:1], rstd[:, 0:1], ALU.subtract, ALU.mult)\
                    .then_inc(S("tile_normed"), 1)
                e.wait_ge(S("tile_normed"), past(ph, "normed") + i + 1)

            def prelu(st, o, a, tmp):
                st.done(e.tensor_scalar(tmp, a, 0.0, col["a"][:, 0:1], ALU.min, ALU.mult))
                return e.scalar_tensor_tensor(o, a, 0.0, tmp, ALU.max, ALU.add)

            e.wait_ge(S("norms_ready"), 1)
            for g in range(T // SPLIT + 2):
                if g < T // SPLIT:
                    b = slice(g * SPLIT, (g + 1) * SPLIT)
                    e.tensor_tensor(X4[:, b, :], X[:, b, :], nsrc[:, b].unsqueeze(2).to_broadcast([P, SPLIT, F]),
                                    ALU.mult).then_inc(S("tile_scaled"), SPLIT)
                if 1 <= g <= T // SPLIT:
                    b = slice((g - 1) * SPLIT, g * SPLIT)
                    e.wait_ge(S("tile_scaled"), g * SPLIT)
                    e.wait_ge(S("tile_part0"), g * SPLIT)
                    e.tensor_tensor(X4[:, b, :], X4[:, b, :], XSa[:, b, 0, :], ALU.subtract)\
                        .then_inc(S("tile_rest"), SPLIT)
                if g >= 2:
                    b = slice((g - 2) * SPLIT, (g - 1) * SPLIT)
                    e.wait_ge(S("tile_rest"), (g - 1) * SPLIT)
                    e.wait_ge(S("tile_part1"), (g - 1) * SPLIT)
                    e.tensor_tensor(XSa[:, b, 2, :], X4[:, b, :], XSa[:, b, 1, :], ALU.subtract)\
                        .then_inc(S("tile_part2"), SPLIT)
            phase_end(e, "split")

            def run(ph, stages):
                pipeline(e, stages)
                phase_end(e, ph)

            st0 = Steps(e, S("steps_l0"), 4)

            def l0_sum(i, par):
                read_sum("l0", i, par, F, ndst)

            def l0_norm(i, par):
                st0.tile(i)
                e.wait_ge(S("tile_pre"), past("l0", "pre") + i + 1)
                st0.done(e.tensor_tensor(V[:, :], pD[par], bc["l0"][:, :], ALU.add))
                e.tensor_scalar(U[:, :], V[:, :], 0.0, None, ALU.min).then_inc(S("tile_negative"), 1)
                st0.done(e.scalar_tensor_tensor(R2[:, :], V[:, :], 0.0, row(X, i), ALU.max, ALU.add))
                e.wait_ge(S("tile_exped"), past("l0", "exped") + i + 1)
                st0.done(e.scalar_tensor_tensor(V[:, :], G2[:, :], -1.0, R2[:, :], ALU.add, ALU.add))
                layernorm("l0", st0, i, V[:, :], Xn[par])

            def l0_split(i, par):
                e.wait_ge(S("tile_proj"), past("l0", "proj") + i + 1)
                e.tensor_scalar(V2[:, 0:HC], pD2[par][:, 0:HC], tcol(dis, i), None, ALU.mult)\
                    .then_inc(S("tile_scaled"), 1)
                e.wait_ge(S("tile_scaled"), past("l0", "scaled") + i + 1)
                split_v("l0", V2[:, 0:HC], XSb, HC, i)
            run("l0", [(1, l0_sum), (2, l0_norm), (4, l0_split)])

            st1 = Steps(e, S("steps_l1"), 3)

            def l1_sum(i, par):
                read_sum("l1", i, par, HC, dis)

            def l1_norm(i, par):
                st1.tile(i)
                e.wait_ge(S("tile_pre"), past("l1", "pre") + i + 1)
                st1.done(e.tensor_tensor(V[:, :], pD[0], bc["dec2"][:, :], ALU.add))
                st1.done(e.tensor_tensor(V[:, :], V[:, :], row(X, i), ALU.add))
                layernorm("l1", st1, i, V[:, :], Xn[par])

            def l1_split(i, par):
                split_v("l1", pD2[par], XSa, F, i)
            run("l1", [(1, l1_sum), (3, l1_norm), (5, l1_split)])

            def hyperedge(ph):
                def body(i, par):
                    read_sum(ph, i, par, F, binv)
                    split_v(ph, G[:, :], XSb, F, i)
                run(ph, [(1, body)])

            hyperedge("h1a")
            st2 = Steps(e, S("steps_h1b"), 2)

            def h1b(i, par):
                st2.tile(i)
                read_sum("h1b", i, par, F, dinv, V)
                st2.done(e.tensor_tensor(V[:, :], V[:, :], bc["h1"][:, :], ALU.add))
                prelu(st2, G[:, :], V[:, :], U[:, :]).then_inc(S("tile_active"), 1)

            def h1b_split(i, par):
                split_v("h1b", pD2[par], XSa, F, i)
            run("h1b", [(1, h1b), (2, h1b_split)])
            hyperedge("h2a")
            st3 = Steps(e, S("steps_h2b"), 6)

            def h2b(i, par):
                st3.tile(i)
                read_sum("h2b", i, par, F, dinv)
                st3.done(e.tensor_tensor(V[:, :], G[:, :], bc["h2"][:, :], ALU.add))
                st3.done(e.tensor_tensor(V[:, :], V[:, :], row(X, i), ALU.add))
                st3.done(prelu(st3, V[:, :], V[:, :], U[:, :]))
                st3.done(e.tensor_tensor(V[:, :], V[:, :], row(X, i), ALU.add))
                layernorm("h2b", st3, i, V[:, :], Xn[par])
                e.tensor_scalar(G2[:, :], Xn[par], tcol(nsrc, i), None, ALU.mult).then_inc(S("tile_scaled"), 1)
                e.wait_ge(S("tile_scaled"), past("h2b", "scaled") + i + 1)
                split_v("h2b", G2[:, :], XSa, F, i)
            run("h2b", [(1, h2b)])

            st.done(e.tensor_tensor(bc["gc"][:, :], bc["gc"][:, :], bc["res"][:, :], ALU.add))
            st4 = Steps(e, S("steps_l3"), 3)

            def l3_sum(i, par):
                read_sum("l3", i, par, F, ndst)

            def l3_x4(i, par):
                e.wait_ge(S("tile_pre"), past("l3", "pre") + i + 1)
                e.wait_ge(S("tile_x4_kept"), past("l3", "x4_kept") + i)
                e.tensor_tensor(V[:, :], pD[0], bc["gc"][:, :], ALU.add).then_inc(S("tile_x4_made"), 1)

            def l3_top(i, par):
                st4.tile(i)
                e.wait_ge(S("tile_logits"), past("l3", "logits") + i + 1)
                st4.done(e.tensor_tensor(U[:, 0:NE], pD2[par][:, 0:NE], bgb[:, :], ALU.add))
                carry_wait(e)
                st4.done(e.max(max8[:, :], U[:, 0:NE]))
                carry_wait(e)
                st4.done(e.max_index(idx8[:, :], max8[:, :], U[:, 0:NE]))
                e.tensor_copy(row(top_val, i), max8[:, 0:TOP])
                e.tensor_copy(row(top_idx, i), idx8[:, 0:TOP]).then_inc(S("tile_top"), 1)
                e.wait_ge(S("tile_top"), past("l3", "top") + i + 1)
            pipeline(e, [(1, l3_sum), (2, l3_x4), (3, l3_top)])
            dve_moe(e)

        @block.gpsimd
        def _(e):
            e.memset(identF[:, :], 0.0).then_inc(S("pool_cleared"), 1)
            e.memset(identB[:, :], 0.0).then_inc(S("pool_cleared"), 1)
            e.wait_ge(S("pool_cleared"), 2)
            for m in (identF, identB):
                e.affine_select(out=m[:, :], in_=m[:, :], compare_op=ALU.not_equal, fill=1.0, base=0,
                                pattern=[[-1, P]], channel_multiplier=1).then_inc(S("ident_set"), 1)
            e.iota(iota_f, [[1, FW]], base=0, channel_multiplier=0, allow_small_or_imprecise_dtypes=True)\
                .then_inc(S("iotas_set"), 1)
            e.iota(iota_p, [[1, P]], base=0, channel_multiplier=0, allow_small_or_imprecise_dtypes=True)\
                .then_inc(S("iotas_set"), 1)
            e.iota(chunk_id, [[1, EG * P]], base=0, channel_multiplier=0, allow_small_or_imprecise_dtypes=True)\
                .then_inc(S("iotas_set"), 1)
            e.iota(bandcol[:, 2:4], [[P - 1, 2]], base=0, channel_multiplier=P,
                   allow_small_or_imprecise_dtypes=True).then_inc(S("iotas_set"), 1)
            for m in (triB, vmask):
                e.memset(m[:, :], 1.0).then_inc(S("masks_set"), 1)
            e.memset(valid[:, :], 1.0).then_inc(S("masks_set"), 1)
            e.wait_ge(S("masks_set"), 3)
            e.affine_select(out=triB[:, :], in_=triB[:, :], compare_op=ALU.is_gt, fill=0.0, base=0,
                            pattern=[[1, P]], channel_multiplier=-1).then_inc(S("masks_set"), 1)
            e.affine_select(out=vmask[:, :], in_=vmask[:, :], compare_op=ALU.is_ge, fill=0.0, base=LAST - 1,
                            pattern=[[0, P]], channel_multiplier=-1).then_inc(S("masks_set"), 1)
            e.affine_select(out=valid[:, :], in_=valid[:, :], compare_op=ALU.is_ge, fill=0.0, base=N - 1,
                            pattern=[[-P, T]], channel_multiplier=-1).then_inc(S("masks_set"), 1)
            e.iota(iota_e[:, :], [[1, NE]], base=0, channel_multiplier=0, allow_small_or_imprecise_dtypes=True)\
                .then_inc(S("masks_set"), 1)
            e.iota(trash[:, :, :], [[NP, TOP], [P, T]], base=TRASH, channel_multiplier=1,
                   allow_small_or_imprecise_dtypes=True).then_inc(S("masks_set"), 1)
            e.iota(pcol[:, :], [[0, 1]], base=0, channel_multiplier=1, allow_small_or_imprecise_dtypes=True)\
                .then_inc(S("masks_set"), 1)
            e.wait_ge(S("iotas_set"), 4)
            e.wait_ge(S("masks_set"), 9)
            phase_end(e, "load")
            e.memset(X4[:, :, :], 0.0).then_inc(S("zeros_set"), 1)
            phase_end(e, "table")
            e.sem_inc(S("onehots_used"), UNROLL)
            e.sem_inc(S("band_turned"), 1)

            def unpack(b, par):
                e.wait_ge(S("words_read"), b + 1)
                if not (isinstance(b, int) and b < 1):
                    e.wait_ge(S("band_transposed"), ROUNDS * (b - 1))
                e.wait_ge(S(f"rows_stored_{par}"), 8 * (b - par))
                carry_wait(e)
                e.tensor_copy(band_rows[par][:, FW:2 * FW], field(1, FW)).then_inc(S("fields_cast"), 1)
                e.tensor_copy(band_rows[par][:, 2 * FW:NP], field(2, NP - 2 * FW)).then_inc(S("fields_cast"), 1)
                e.tensor_copy(indeg[:, bass.ds(b, 1)], words[:, FW:FW + 1]).then_inc(S("fields_cast"), 1)
            pipeline(e, [(1, unpack), (2, lambda i, par: None)])
            phase_end(e, "counts")
            phase_end(e, "checked")
            phase_end(e, "rests")
            for n in (nsrc, ndst, dis):
                e.wait_ge(S("degrees_read"), 1)
                e.tensor_tensor(n[:, :], n[:, :], mhalf[:, :], ALU.pow).then_inc(S("norms_ready"), 1)
            e.wait_ge(S("norms_ready"), 3)
            phase_end(e, "split")

            def norm_tile(ph, lag):
                def body(i, par):
                    e.wait_ge(S("tile_moments"), past(ph, "moments") + i + 1)
                    carry_wait(e)
                    e.tensor_scalar(ve[:, :], mv[:, 1:2], EPS, None, ALU.add).then_inc(S("tile_eps"), 1)
                    e.wait_ge(S("tile_eps"), past(ph, "eps") + i + 1)
                    e.tensor_tensor(rstd[:, :], ve[:, :], mhalf[:, 0:1], ALU.pow).then_inc(S("tile_rstd"), 1)
                    e.wait_ge(S("tile_normed"), past(ph, "normed") + i + 1)
                    e.tensor_copy(X[:, bass.ds(i, 1), :].rearrange("p a f -> p (a f)"), Xn[par])\
                        .then_inc(S("tile_x_kept"), 1)
                pipeline(e, [(lag, body)])
                e.wait_ge(S("tile_x_kept"), past(ph, "x_kept") + T)
                phase_end(e, ph)

            norm_tile("l0", 2)
            norm_tile("l1", 3)
            phase_end(e, "h1a")
            phase_end(e, "h1b")
            phase_end(e, "h2a")
            norm_tile("h2b", 1)

            def l3_own(i, par):
                e.wait_ge(S("tile_x_turned"), past("l3", "x_turned") + i)
                e.tensor_copy(Xn[par], X[:, bass.ds(i, 1), :].rearrange("p a f -> p (a f)"))\
                    .then_inc(S("tile_own_copied"), 1)

            def l3_keep(i, par):
                e.wait_ge(S("tile_x4_made"), past("l3", "x4_made") + i + 1)
                e.tensor_copy(X4[:, bass.ds(i, 1), :].rearrange("p a f -> p (a f)"), V[:, :])\
                    .then_inc(S("tile_x4_kept"), 1)
            pipeline(e, [(1, l3_own), (2, l3_keep)])
            e.wait_ge(S("tile_x4_kept"), past("l3", "x4_kept") + T)
            pool_moe(e)


_INS = ["x", "src", "dst", "L0_gnn_weight", "L0_gnn_bias", "L1_gnn_W_conv", "L1_gnn_b_conv", "L1_gnn_W_lin",
        "L1_gnn_b_lin", "L1_gnn_W_dec1", "L1_gnn_b_dec1", "L1_gnn_W_dec2", "L1_gnn_b_dec2", "L2_gnn_W1", "L2_gnn_b1",
        "L2_gnn_W2", "L2_gnn_b2", "L2_gnn_a", "L3_gnn_W_gc", "L3_gnn_b_gc", "L3_gnn_W_res", "L3_gnn_b_res",
        "L3_gnn_Wg", "L3_gnn_bg", "L3_gnn_w1", "L3_gnn_b1", "L3_gnn_w2", "L3_gnn_b2", "L3_gnn_gamma", "L3_gnn_beta"]


def kernel(**inputs):
    import numpy as _np
    import concourse.bacc as _bacc
    from concourse import mybir as _mybir
    from concourse.bass_utils import run_bass_kernel_spmd as _run

    nc = _bacc.Bacc("TRN2", target_bir_lowering=False, num_devices=1)
    arrays, args = {}, {}
    for name in _INS:
        a = _np.ascontiguousarray(inputs[name])
        arrays[f"in_{name}"] = a
        args[name] = nc.dram_tensor(f"in_{name}", a.shape, _mybir.dt.from_np(a.dtype), kind="ExternalInput").ap()
    out = nc.dram_tensor("out", arrays["in_x"].shape, F32, kind="ExternalOutput").ap()
    gnn_program(nc, args, out)
    return _run(nc, [arrays], core_ids=[0]).results[0]["out"]
```
